# Optimizing a Trainium2 kernel written in Bass

```python
import numpy as np
import jax
import jax.numpy as jnp

def _softmax(x, axis=-1):
    return jax.nn.softmax(x, axis=axis)

def _gelu(x):
    return jax.nn.gelu(x, approximate=True)

def _silu(x):
    return jax.nn.silu(x)

def _sigmoid(x):
    return jax.nn.sigmoid(x)

def _layernorm(x, axis=-1, eps=1e-05):
    m = jnp.mean(x, axis=axis, keepdims=True)
    v = jnp.var(x, axis=axis, keepdims=True)
    return (x - m) / jnp.sqrt(v + eps)

def _scatter_add(tgt, idx, src, axis=0):
    return tgt.at[idx].add(src)

def _segment_sum(src, seg, n):
    return jax.ops.segment_sum(src, seg, n)
kernel_name = 'mk_sandwich_d2_jaxref_r8_dc358f'

def setup_inputs(seed: int=0):
    np.random.seed(seed)
    _w = jnp.asarray

    def _L0_attn_setup():
        import jax, jax.numpy as jnp
        import numpy as np
        NUM_HEADS = 16
        LN_EPS = 1e-05

        def _rope(x):
            S, D = (x.shape[-2], x.shape[-1])
            rot = D // 2
            inv_freq = 1.0 / 10000.0 ** (jnp.arange(0, rot, 2, dtype=jnp.float32) / rot)
            ang = jnp.arange(S, dtype=jnp.float32)[:, None] * inv_freq[None, :]
            ang = jnp.repeat(ang, 2, axis=-1)
            cos, sin = (jnp.cos(ang), jnp.sin(ang))
            xr, xp = (x[..., :rot], x[..., rot:])
            x1, x2 = (xr[..., 0::2], xr[..., 1::2])
            rot_half = jnp.stack((-x2, x1), axis=-1).reshape(xr.shape)
            xr = xr * cos + rot_half * sin
            return jnp.concatenate([xr, xp], axis=-1)
        key = jax.random.key(seed)
        k1, k2, k3 = jax.random.split(key, 3)
        B, S, D = (4, 256, 256)
        X = jax.random.normal(k1, (B, S, D), dtype=jnp.float32)
        ln_w = jnp.ones((D,), dtype=jnp.float32)
        ln_b = jnp.zeros((D,), dtype=jnp.float32)
        W_in = jax.random.normal(k2, (D, 3 * D), dtype=jnp.float32) * 0.02
        W_out = jax.random.normal(k3, (D, D), dtype=jnp.float32) * 0.02
        return {'X': X, 'ln_w': ln_w, 'ln_b': ln_b, 'W_in': W_in, 'W_out': W_out}
    _L0_attn_in = _L0_attn_setup()

    def _L0_ffn_setup():
        import jax, jax.numpy as jnp
        import numpy as np
        import math
        GOLDEN_CENTER = 1.0 / math.e
        GOLDEN_LOWER = 0.5 - math.log(4.0 / 3.0)
        GOLDEN_UPPER = 0.5
        B, T, D = (4, 128, 256)
        E = 8
        F = 1024 // (E // 2)
        R = 64
        NL = 2

        def _router_weights(x, Wr, temperature):
            logits = jnp.einsum('btd,de->bte', x, Wr)
            inhibition = jax.nn.sigmoid(logits / temperature)
            in_zone = (inhibition >= GOLDEN_LOWER) & (inhibition <= GOLDEN_UPPER)
            distance = jnp.abs(inhibition - GOLDEN_CENTER)
            w = jnp.exp(-distance / 0.1) * in_zone.astype(x.dtype)
            wsum = w.sum(axis=-1, keepdims=True)
            no_expert = wsum < 1e-08
            fb = jnp.exp(-distance / 0.3)
            _, top2 = jax.lax.top_k(fb, 2)
            fb_mask = jax.nn.one_hot(top2, E, dtype=x.dtype).sum(axis=-2)
            fb_w = fb * fb_mask
            fb_w = fb_w / jnp.clip(fb_w.sum(axis=-1, keepdims=True), 1e-08)
            w = jnp.where(no_expert, fb_w, w)
            return w / jnp.clip(w.sum(axis=-1, keepdims=True), 1e-08)
        key = jax.random.key(seed)
        ks = jax.random.split(key, 13)
        s = 0.02
        x = jax.random.normal(ks[0], (B, T, D), dtype=jnp.float32)
        Wg = jax.random.normal(ks[1], (E, D, F), dtype=jnp.float32) * s
        Wu = jax.random.normal(ks[2], (E, D, F), dtype=jnp.float32) * s
        Wd = jax.random.normal(ks[3], (E, F, D), dtype=jnp.float32) * s
        Ga = jax.random.normal(ks[4], (NL, D, R), dtype=jnp.float32) * s
        Gb = jax.random.normal(ks[5], (NL, R, F), dtype=jnp.float32) * s
        Ua = jax.random.normal(ks[6], (NL, D, R), dtype=jnp.float32) * s
        Ub = jax.random.normal(ks[7], (NL, R, F), dtype=jnp.float32) * s
        Da = jax.random.normal(ks[8], (NL, F, R), dtype=jnp.float32) * s
        Db = jax.random.normal(ks[9], (NL, R, D), dtype=jnp.float32) * s
        Wr = jax.random.normal(ks[10], (D, E), dtype=jnp.float32) * s
        temperature = jnp.ones((1,), dtype=jnp.float32)
        return {'x': x, 'Wg': Wg, 'Wu': Wu, 'Wd': Wd, 'Ga': Ga, 'Gb': Gb, 'Ua': Ua, 'Ub': Ub, 'Da': Da, 'Db': Db, 'Wr': Wr, 'temperature': temperature}
    _L0_ffn_in = _L0_ffn_setup()

    def _L1_attn_setup():
        import jax, jax.numpy as jnp
        import numpy as np
        from jax import lax
        B, L, D = (2, 256, 256)
        H, DK, DV, K = (16, 128, 128, 4)
        Q_DIM = H * DK
        V_DIM = H * DV

        def silu(x):
            return x * jax.nn.sigmoid(x)

        def causal_dwconv(x, w, b):
            Kk = w.shape[1]
            xp = jnp.pad(x, ((0, 0), (Kk - 1, 0), (0, 0)))
            kern = w.T[:, None, :]
            y = lax.conv_general_dilated(xp, kern, window_strides=(1,), padding='VALID', dimension_numbers=('NWC', 'WIO', 'NWC'), feature_group_count=w.shape[0])
            return y + b

        def layernorm(x, w, b, eps=1e-05):
            m = jnp.mean(x, axis=-1, keepdims=True)
            var = jnp.mean((x - m) ** 2, axis=-1, keepdims=True)
            return (x - m) * lax.rsqrt(var + eps) * w + b
        key = jax.random.key(seed)
        ks = jax.random.split(key, 16)
        s = 0.02
        f32 = jnp.float32
        return {'hidden_states': jax.random.normal(ks[0], (B, L, D), f32), 'Wq': jax.random.normal(ks[1], (D, Q_DIM), f32) * s, 'Wk': jax.random.normal(ks[2], (D, Q_DIM), f32) * s, 'Wv': jax.random.normal(ks[3], (D, V_DIM), f32) * s, 'Wb': jax.random.normal(ks[4], (D, H), f32) * s, 'bb': jnp.full((H,), -2.0, f32), 'Wg': jax.random.normal(ks[5], (D, V_DIM), f32) * s, 'Wo': jax.random.normal(ks[6], (V_DIM, D), f32) * s, 'qconv_w': jax.random.normal(ks[7], (Q_DIM, K), f32) * 0.5, 'qconv_b': jnp.zeros((Q_DIM,), f32), 'kconv_w': jax.random.normal(ks[8], (Q_DIM, K), f32) * 0.5, 'kconv_b': jnp.zeros((Q_DIM,), f32), 'qn_w': jnp.ones((DK,), f32), 'qn_b': jnp.zeros((DK,), f32), 'kn_w': jnp.ones((DK,), f32), 'kn_b': jnp.zeros((DK,), f32)}
    _L1_attn_in = _L1_attn_setup()

    def _L1_ffn_setup():
        import jax, jax.numpy as jnp
        import numpy as np
        HIDDEN = 256
        FFN = 176
        N_EXPERTS = 16
        TOP_K = 4
        SHARED_FFN = 2 * FFN

        def _glu_ffn(x, gate_up, down):
            gu = x @ gate_up.T
            g, u = jnp.split(gu, 2, axis=-1)
            return jax.nn.silu(g) * u @ down.T
        key = jax.random.key(seed)
        ks = jax.random.split(key, 6)
        s = 0.02
        return {'hidden_states': jax.random.normal(ks[0], (1, 256, HIDDEN), jnp.float32), 'gate_weight': jax.random.normal(ks[1], (N_EXPERTS, HIDDEN), jnp.float32) * s, 'gate_up_weights': jax.random.normal(ks[2], (N_EXPERTS, 2 * FFN, HIDDEN), jnp.float32) * s, 'down_weights': jax.random.normal(ks[3], (N_EXPERTS, HIDDEN, FFN), jnp.float32) * s, 'shared_gate_up': jax.random.normal(ks[4], (2 * SHARED_FFN, HIDDEN), jnp.float32) * s, 'shared_down': jax.random.normal(ks[5], (HIDDEN, SHARED_FFN), jnp.float32) * s}
    _L1_ffn_in = _L1_ffn_setup()
    _d = {'L0_attn_X': _L0_attn_in['X'], 'L0_attn_ln_w': _L0_attn_in['ln_w'], 'L0_attn_ln_b': _L0_attn_in['ln_b'], 'L0_attn_W_in': _L0_attn_in['W_in'], 'L0_attn_W_out': _L0_attn_in['W_out'], 'L0_ffn_Wg': _L0_ffn_in['Wg'], 'L0_ffn_Wu': _L0_ffn_in['Wu'], 'L0_ffn_Wd': _L0_ffn_in['Wd'], 'L0_ffn_Ga': _L0_ffn_in['Ga'], 'L0_ffn_Gb': _L0_ffn_in['Gb'], 'L0_ffn_Ua': _L0_ffn_in['Ua'], 'L0_ffn_Ub': _L0_ffn_in['Ub'], 'L0_ffn_Da': _L0_ffn_in['Da'], 'L0_ffn_Db': _L0_ffn_in['Db'], 'L0_ffn_Wr': _L0_ffn_in['Wr'], 'L0_ffn_temperature': _L0_ffn_in['temperature'], 'L1_attn_Wq': _L1_attn_in['Wq'], 'L1_attn_Wk': _L1_attn_in['Wk'], 'L1_attn_Wv': _L1_attn_in['Wv'], 'L1_attn_Wb': _L1_attn_in['Wb'], 'L1_attn_bb': _L1_attn_in['bb'], 'L1_attn_Wg': _L1_attn_in['Wg'], 'L1_attn_Wo': _L1_attn_in['Wo'], 'L1_attn_qconv_w': _L1_attn_in['qconv_w'], 'L1_attn_qconv_b': _L1_attn_in['qconv_b'], 'L1_attn_kconv_w': _L1_attn_in['kconv_w'], 'L1_attn_kconv_b': _L1_attn_in['kconv_b'], 'L1_attn_qn_w': _L1_attn_in['qn_w'], 'L1_attn_qn_b': _L1_attn_in['qn_b'], 'L1_attn_kn_w': _L1_attn_in['kn_w'], 'L1_attn_kn_b': _L1_attn_in['kn_b'], 'L1_ffn_gate_weight': _L1_ffn_in['gate_weight'], 'L1_ffn_gate_up_weights': _L1_ffn_in['gate_up_weights'], 'L1_ffn_down_weights': _L1_ffn_in['down_weights'], 'L1_ffn_shared_gate_up': _L1_ffn_in['shared_gate_up'], 'L1_ffn_shared_down': _L1_ffn_in['shared_down']}
    _x0 = _d['L0_attn_X']
    _d['L0_attn_X'] = jax.random.normal(jax.random.fold_in(jax.random.key(seed), 1), (1, 1024, 256), dtype=_x0.dtype)
    del _x0
    return _d

def reference(L0_attn_X, L0_attn_ln_w, L0_attn_ln_b, L0_attn_W_in, L0_attn_W_out, L0_ffn_Wg, L0_ffn_Wu, L0_ffn_Wd, L0_ffn_Ga, L0_ffn_Gb, L0_ffn_Ua, L0_ffn_Ub, L0_ffn_Da, L0_ffn_Db, L0_ffn_Wr, L0_ffn_temperature, L1_attn_Wq, L1_attn_Wk, L1_attn_Wv, L1_attn_Wb, L1_attn_bb, L1_attn_Wg, L1_attn_Wo, L1_attn_qconv_w, L1_attn_qconv_b, L1_attn_kconv_w, L1_attn_kconv_b, L1_attn_qn_w, L1_attn_qn_b, L1_attn_kn_w, L1_attn_kn_b, L1_ffn_gate_weight, L1_ffn_gate_up_weights, L1_ffn_down_weights, L1_ffn_shared_gate_up, L1_ffn_shared_down):

    def _L0_attn_ref(X, ln_w, ln_b, W_in, W_out):
        import jax, jax.numpy as jnp
        import numpy as np
        NUM_HEADS = 16
        LN_EPS = 1e-05

        def _rope(x):
            S, D = (x.shape[-2], x.shape[-1])
            rot = D // 2
            inv_freq = 1.0 / 10000.0 ** (jnp.arange(0, rot, 2, dtype=jnp.float32) / rot)
            ang = jnp.arange(S, dtype=jnp.float32)[:, None] * inv_freq[None, :]
            ang = jnp.repeat(ang, 2, axis=-1)
            cos, sin = (jnp.cos(ang), jnp.sin(ang))
            xr, xp = (x[..., :rot], x[..., rot:])
            x1, x2 = (xr[..., 0::2], xr[..., 1::2])
            rot_half = jnp.stack((-x2, x1), axis=-1).reshape(xr.shape)
            xr = xr * cos + rot_half * sin
            return jnp.concatenate([xr, xp], axis=-1)
        B, S, D = X.shape
        H = NUM_HEADS
        Dh = D // H
        mu = jnp.mean(X, axis=-1, keepdims=True)
        var = jnp.mean(jnp.square(X - mu), axis=-1, keepdims=True)
        Xn = (X - mu) * jax.lax.rsqrt(var + LN_EPS) * ln_w + ln_b
        qkv = jnp.einsum('bsd,df->bsf', Xn, W_in)
        Q, K, V = jnp.split(qkv, 3, axis=-1)
        Q = Q.reshape(B, S, H, Dh).transpose(0, 2, 1, 3)
        K = K.reshape(B, S, H, Dh).transpose(0, 2, 1, 3)
        V = V.reshape(B, S, H, Dh).transpose(0, 2, 1, 3)
        Q, K = (_rope(Q), _rope(K))
        scores = jnp.einsum('bhqd,bhkd->bhqk', Q, K) / jnp.sqrt(jnp.float32(Dh))
        probs = jax.nn.softmax(scores, axis=-1)
        ctx = jnp.einsum('bhqk,bhkd->bhqd', probs, V)
        ctx = ctx.transpose(0, 2, 1, 3).reshape(B, S, D)
        out = jnp.einsum('bsd,df->bsf', ctx, W_out)
        return out + X

    def _L0_ffn_ref(x, Wg, Wu, Wd, Ga, Gb, Ua, Ub, Da, Db, Wr, temperature):
        import jax, jax.numpy as jnp
        import numpy as np
        import math
        GOLDEN_CENTER = 1.0 / math.e
        GOLDEN_LOWER = 0.5 - math.log(4.0 / 3.0)
        GOLDEN_UPPER = 0.5
        B, T, D = (4, 128, 256)
        E = 8
        F = 1024 // (E // 2)
        R = 64
        NL = 2

        def _router_weights(x, Wr, temperature):
            logits = jnp.einsum('btd,de->bte', x, Wr)
            inhibition = jax.nn.sigmoid(logits / temperature)
            in_zone = (inhibition >= GOLDEN_LOWER) & (inhibition <= GOLDEN_UPPER)
            distance = jnp.abs(inhibition - GOLDEN_CENTER)
            w = jnp.exp(-distance / 0.1) * in_zone.astype(x.dtype)
            wsum = w.sum(axis=-1, keepdims=True)
            no_expert = wsum < 1e-08
            fb = jnp.exp(-distance / 0.3)
            _, top2 = jax.lax.top_k(fb, 2)
            fb_mask = jax.nn.one_hot(top2, E, dtype=x.dtype).sum(axis=-2)
            fb_w = fb * fb_mask
            fb_w = fb_w / jnp.clip(fb_w.sum(axis=-1, keepdims=True), 1e-08)
            w = jnp.where(no_expert, fb_w, w)
            return w / jnp.clip(w.sum(axis=-1, keepdims=True), 1e-08)
        weights = _router_weights(x, Wr, temperature)
        gate = jnp.einsum('btd,edf->ebtf', x, Wg)
        up = jnp.einsum('btd,edf->ebtf', x, Wu)
        gate = gate.at[:NL].add(jnp.einsum('btd,edr,erf->ebtf', x, Ga, Gb))
        up = up.at[:NL].add(jnp.einsum('btd,edr,erf->ebtf', x, Ua, Ub))
        mid = jax.nn.silu(gate) * up
        out = jnp.einsum('ebtf,efd->ebtd', mid, Wd)
        out = out.at[:NL].add(jnp.einsum('ebtf,efr,erd->ebtd', mid[:NL], Da, Db))
        return jnp.einsum('bte,ebtd->btd', weights, out)

    def _L1_attn_ref(hidden_states, Wq, Wk, Wv, Wb, bb, Wg, Wo, qconv_w, qconv_b, kconv_w, kconv_b, qn_w, qn_b, kn_w, kn_b):
        import jax, jax.numpy as jnp
        import numpy as np
        from jax import lax
        B, L, D = (2, 256, 256)
        H, DK, DV, K = (16, 128, 128, 4)
        Q_DIM = H * DK
        V_DIM = H * DV

        def silu(x):
            return x * jax.nn.sigmoid(x)

        def causal_dwconv(x, w, b):
            Kk = w.shape[1]
            xp = jnp.pad(x, ((0, 0), (Kk - 1, 0), (0, 0)))
            kern = w.T[:, None, :]
            y = lax.conv_general_dilated(xp, kern, window_strides=(1,), padding='VALID', dimension_numbers=('NWC', 'WIO', 'NWC'), feature_group_count=w.shape[0])
            return y + b

        def layernorm(x, w, b, eps=1e-05):
            m = jnp.mean(x, axis=-1, keepdims=True)
            var = jnp.mean((x - m) ** 2, axis=-1, keepdims=True)
            return (x - m) * lax.rsqrt(var + eps) * w + b
        Bs, Ls, Ds = hidden_states.shape
        q = hidden_states @ Wq
        k = hidden_states @ Wk
        v = hidden_states @ Wv
        beta = jax.nn.sigmoid(hidden_states @ Wb + bb)
        gate = silu(hidden_states @ Wg)
        q = silu(causal_dwconv(q, qconv_w, qconv_b))
        k = silu(causal_dwconv(k, kconv_w, kconv_b))
        q = layernorm(q.reshape(Bs, Ls, H, DK), qn_w, qn_b)
        k = layernorm(k.reshape(Bs, Ls, H, DK), kn_w, kn_b)
        v = v.reshape(Bs, Ls, H, DV)
        qs = q.transpose(1, 0, 2, 3)
        ks_ = k.transpose(1, 0, 2, 3)
        vs = v.transpose(1, 0, 2, 3)
        bs = beta.transpose(1, 0, 2)
        S0 = jnp.zeros((Bs, H, DV, DK), hidden_states.dtype)

        def step(S, inp):
            q_t, k_t, v_t, b_t = inp
            b = b_t[..., None, None]
            S = (1.0 - b) * S + b * (v_t[..., :, None] * k_t[..., None, :])
            o_t = jnp.einsum('bhvk,bhk->bhv', S, q_t)
            return (S, o_t)
        _, os = lax.scan(step, S0, (qs, ks_, vs, bs))
        o = os.transpose(1, 0, 2, 3).reshape(Bs, Ls, H * DV)
        o = o * gate
        return o @ Wo

    def _L1_ffn_ref(hidden_states, gate_weight, gate_up_weights, down_weights, shared_gate_up, shared_down):
        import jax, jax.numpy as jnp
        import numpy as np
        HIDDEN = 256
        FFN = 176
        N_EXPERTS = 16
        TOP_K = 4
        SHARED_FFN = 2 * FFN

        def _glu_ffn(x, gate_up, down):
            gu = x @ gate_up.T
            g, u = jnp.split(gu, 2, axis=-1)
            return jax.nn.silu(g) * u @ down.T
        orig_shape = hidden_states.shape
        x = hidden_states.reshape(-1, orig_shape[-1])
        scores = jax.nn.softmax(x @ gate_weight.T, axis=-1)
        topk_weight, topk_idx = jax.lax.top_k(scores, TOP_K)
        y = jnp.zeros_like(x)
        for e in range(N_EXPERTS):
            w_e = jnp.sum(jnp.where(topk_idx == e, topk_weight, 0.0), axis=-1)
            y = y + w_e[:, None] * _glu_ffn(x, gate_up_weights[e], down_weights[e])
        y = y + _glu_ffn(x, shared_gate_up, shared_down)
        return y.reshape(orig_shape)
    x = L0_attn_X
    x = x + _layernorm(_L0_attn_ref(_layernorm(x, axis=-1), L0_attn_ln_w, L0_attn_ln_b, L0_attn_W_in, L0_attn_W_out), axis=-1)
    x = x + _layernorm(_L0_ffn_ref(_layernorm(x, axis=-1), L0_ffn_Wg, L0_ffn_Wu, L0_ffn_Wd, L0_ffn_Ga, L0_ffn_Gb, L0_ffn_Ua, L0_ffn_Ub, L0_ffn_Da, L0_ffn_Db, L0_ffn_Wr, L0_ffn_temperature), axis=-1)
    x = x + _layernorm(_L1_attn_ref(_layernorm(x, axis=-1), L1_attn_Wq, L1_attn_Wk, L1_attn_Wv, L1_attn_Wb, L1_attn_bb, L1_attn_Wg, L1_attn_Wo, L1_attn_qconv_w, L1_attn_qconv_b, L1_attn_kconv_w, L1_attn_kconv_b, L1_attn_qn_w, L1_attn_qn_b, L1_attn_kn_w, L1_attn_kn_b), axis=-1)
    x = x + _layernorm(_L1_ffn_ref(_layernorm(x, axis=-1), L1_ffn_gate_weight, L1_ffn_gate_up_weights, L1_ffn_down_weights, L1_ffn_shared_gate_up, L1_ffn_shared_down), axis=-1)
    return x

_drawn_inputs = setup_inputs


def setup_inputs(seed=0):
    import zlib

    import numpy as np

    out = dict(_drawn_inputs(seed))
    spreads = {'L0_attn_ln_w': (1.0, 0.6),
     'L0_attn_ln_b': (0.0, 0.28),
     'L1_attn_bb': (-2.0, 0.2),
     'L1_attn_qconv_b': (0.0, 0.1),
     'L1_attn_kconv_b': (0.0, 0.1),
     'L1_attn_qn_w': (1.0, 0.2),
     'L1_attn_qn_b': (0.0, 0.1),
     'L1_attn_kn_w': (1.0, 0.2),
     'L1_attn_kn_b': (0.0, 0.1)}
    factors = {'L0_attn_W_out': 3.045}
    for name, (base, spread) in spreads.items():
        noise = np.random.default_rng([zlib.crc32(name.encode()), seed]).standard_normal(out[name].shape)
        drawn = base * np.exp(spread * noise) if base else spread * noise
        out[name] = jnp.asarray(drawn.astype(out[name].dtype))
    for name, factor in factors.items():
        out[name] = (out[name] * factor).astype(out[name].dtype)
    return out
```

```python
import math
from contextlib import ExitStack

import numpy as np
import concourse.bass as bass
import concourse.mybir as mybir

F32 = mybir.dt.float32
BF16 = mybir.dt.bfloat16
ALU = mybir.AluOpType
ACT = mybir.ActivationFunctionType
AX = mybir.AxisListType.X

P = 128
T = 1024
NT = T // P
D = 256
DK = D // P
HALF = 512
EPS = 1e-5


class Scope:

    used = []

    def __init__(self, nc, tag):
        self.nc, self.tag, self.ctx = nc, tag, ExitStack()

    def __enter__(self):
        self.ctx.__enter__()
        return self

    def __exit__(self, *a):
        return self.ctx.__exit__(*a)

    def sb(self, name, shape, dt=F32):
        return self.ctx.enter_context(self.nc.sbuf_tensor(f"{self.tag}_{name}", shape, dt))

    def ps(self, name, shape, dt=F32):
        return self.ctx.enter_context(self.nc.psum_tensor(f"{self.tag}_{name}", shape, dt))

    def sem(self, name):
        handle = self.ctx.enter_context(self.nc.semaphore(f"{self.tag}_{name}"))
        Scope.used.append(handle.num)
        return handle


def clear_semaphores(nc):
    with nc.Block() as block:

        @block.gpsimd
        def _(pool):
            pool.sem_clear(range(min(Scope.used), max(Scope.used) + 1))

    Scope.used.clear()


def col(ap, n):
    p, a = ap.shape
    return ap.rearrange("p (a o) -> p a o", o=1).to_broadcast((p, a, n))


def load_constants(nc, consts, ident, identb, neg_half):
    with Scope(nc, "const") as s:
        zeroed, loaded = s.sem("zeroed"), s.sem("loaded")
        with nc.Block() as block:

            @block.gpsimd
            def _(pool):
                pool.memset(ident[:, :], 0.0)
                pool.memset(identb[:, :], 0.0)
                pool.memset(neg_half[:, :], -0.5).then_inc(zeroed, 1)
                pool.wait_ge(zeroed, 1)
                pool.drain()
                for m in (ident, identb):
                    pool.affine_select(out=m[:, :], in_=m[:, :], compare_op=ALU.not_equal, fill=1.0,
                                       base=0, pattern=[[-1, P]], channel_multiplier=1)

            @block.sync
            def _(sp):
                for n, (dst, src) in enumerate(consts):
                    sp.dma_start(dst, src, allow_slow_non_contiguous=True).then_inc(loaded, 16)
                sp.wait_ge(loaded, 16 * len(consts))


def norm_block(nc, tag, ident, neg_half, x, y=None, normed=None, normed_T=None, inner=None, inner_wb=None,
               store=None):
    with Scope(nc, tag) as s:
        stats = s.sb("stats", [P, NT, 6])
        mean_var = s.sb("mean_var", [P, NT, 2])
        var_eps = s.sb("var_eps", [P, NT])
        rstd = s.sb("rstd", [P, NT])
        turned = [s.ps(f"turned{k}", [P, T]) for k in range(DK)]
        var_ready, rstd_ready, tile_ready = s.sem("var_ready"), s.sem("rstd_ready"), s.sem("tile_ready")
        x_ready, stored = s.sem("x_ready"), s.sem("stored")
        turn_done, evacuated = s.sem("turn_done"), s.sem("evacuated")
        chain = []
        if y is not None:
            chain.append((y, y))
        if normed is not None:
            chain.append((x, normed))
        if inner is not None:
            chain.append((normed, inner))
        last = chain[-1][1]
        with nc.Block() as block:

            @block.vector
            def _(dve):
                for k, (src, dst) in enumerate(chain):
                    for c in range(NT):
                        dve.bn_stats(stats[:, c, :], src[:, c, :])
                    dve.drain()
                    for c in range(NT):
                        dve.bn_aggr(mean_var[:, c, :], stats[:, c, :])
                    dve.drain()
                    dve.tensor_scalar(var_eps[:, :], mean_var[:, :, 1], EPS, None, ALU.add).then_inc(var_ready, 1)
                    dve.wait_ge(rstd_ready, k + 1)
                    for c in range(NT):
                        i = dve.tensor_scalar(dst[:, c, :], src[:, c, :], mean_var[:, c, 0:1], rstd[:, c:c + 1],
                                              ALU.subtract, ALU.mult)
                        if k == len(chain) - 1 and normed_T is not None:
                            i.then_inc(tile_ready, 1)
                    dve.drain()
                    if y is not None and k == 0:
                        for c in range(NT):
                            dve.tensor_tensor(x[:, c, :], x[:, c, :], y[:, c, :], ALU.add).then_inc(x_ready, 1)
                        dve.drain()

            @block.gpsimd
            def _(pool):
                for k in range(len(chain)):
                    pool.wait_ge(var_ready, k + 1)
                    pool.tensor_tensor(rstd[:, :], var_eps[:, :], neg_half[:, 0:NT], ALU.pow).then_inc(rstd_ready, 1)

            @block.tensor
            def _(pe):
                if normed_T is None:
                    return
                for c in range(NT):
                    pe.wait_ge(tile_ready, c + 1)
                    for k in range(DK):
                        i = pe.transpose(turned[k][:, c * P:(c + 1) * P], last[:, c, k * P:(k + 1) * P], ident[:, :])
                    if c % 4 == 3:
                        i.then_inc(turn_done, 1)

            @block.scalar
            def _(act):
                if normed_T is None:
                    return
                for h in range(2):
                    act.wait_ge(turn_done, h + 1)
                    for k in range(DK):
                        cols = slice(h * HALF, (h + 1) * HALF)
                        if inner_wb is None:
                            act.activation(normed_T[:, k, cols], turned[k][:, cols], ACT.Identity)
                        else:
                            act.activation(normed_T[:, k, cols], turned[k][:, cols], ACT.Identity,
                                           scale=inner_wb[:, 0, k:k + 1], bias=inner_wb[:, 1, k:k + 1])

            @block.sync
            def _(sp):
                if store is None:
                    return
                for c in range(NT):
                    sp.wait_ge(x_ready, c + 1)
                    sp.dma_start(store[c * P:(c + 1) * P, :], x[:, c, :]).then_inc(stored, 16)
                sp.wait_ge(stored, 16 * NT)


def down_block(nc, tag, parts, y, add=None):
    with Scope(nc, tag) as s:
        acc = [s.ps(f"acc{b}", [P, HALF]) for b in range(4)]
        summed, taken = s.sem("summed"), s.sem("taken")
        with nc.Block() as block:

            @block.tensor
            def _(pe):
                for c in range(NT):
                    if c >= 4:
                        pe.wait_ge(taken, c - 3)
                    for n, (lhs, w) in enumerate(parts):
                        i = pe.matmul(acc[c % 4][:, 0:D], lhs[:, c * P:(c + 1) * P], w, start=(n == 0),
                                      stop=(n == len(parts) - 1))
                    i.then_inc(summed, 1)

            @block.vector
            def _(dve):
                for c in range(NT):
                    dve.wait_ge(summed, c + 1)
                    if add is None:
                        dve.tensor_copy(y[:, c, :], acc[c % 4][:, 0:D]).then_inc(taken, 1)
                    else:
                        dve.tensor_tensor(y[:, c, :], acc[c % 4][:, 0:D], add[:, c, :], ALU.add).then_inc(taken, 1)


NH, DH = 16, 16
ROT = DH // 2
TERMS = 6
QROWS = TERMS * DH
MROWS = 3
GH = 4
VW = 32


def qkv_block(nc, W_in, xT, w_in, rope, qk, v, k_stack):
    with Scope(nc, "qkv") as s:
        pq = [s.ps(f"qk{b}", [P, HALF]) for b in range(2)]
        pv = [s.ps(f"v{b}", [P, HALF]) for b in range(2)]
        prod = [s.sb(f"prod{b}", [P, 2 * NH, 4]) for b in range(4)]
        projected, taken, v_ones, w_loaded = s.sem("projected"), s.sem("taken"), s.sem("v_ones"), s.sem("w_loaded")
        copied = s.sem("copied")
        with nc.Block() as block:

            @block.sync
            def _(sp):
                sp.dma_start(w_in[:, :, :], W_in.rearrange("(k p) n -> p k n", p=P)).then_inc(w_loaded, 16)

            @block.tensor
            def _(pe):
                pe.wait_ge(w_loaded, 16)
                for c in range(NT):
                    if c >= 2:
                        pe.wait_ge(taken, c - 1)
                    for out, cols in ((pq[c % 2][:, :], slice(0, 2 * D)), (pv[c % 2][:, 0:D], slice(2 * D, 3 * D))):
                        for k in range(DK):
                            i = pe.matmul(out, xT[:, k, c * P:(c + 1) * P], w_in[:, k, cols], start=(k == 0),
                                          stop=(k == DK - 1))
                    i.then_inc(projected, 1)

            @block.scalar
            def _(act):
                act.wait_ge(v_ones, 1)
                for c in range(NT):
                    act.wait_ge(projected, c + 1)
                    act.activation(qk[:, c, 0:D], pq[c % 2][:, 0:D], ACT.Copy, scale=DH ** -0.5)
                    act.activation(qk[:, c, D:2 * D], pq[c % 2][:, D:2 * D], ACT.Copy).then_inc(copied, 1)
                    act.activation(v[:, c, :, 0:DH], pv[c % 2][:, 0:D].rearrange("p (h d) -> p h d", h=NH),
                                   ACT.Copy).then_inc(taken, 1)

            @block.gpsimd
            def _(pool):
                two_ones = float(np.uint32(0x3F803F80).view(np.float32))
                pool.memset(k_stack[QROWS:P, :, :].rearrange("p a b -> p (a b)").bitcast(F32), two_ones)

            @block.vector
            def _(dve):
                dve.memset(v[:, :, :, :].rearrange("p a b c -> p (a b c)"), 0.0)
                dve.drain()
                dve.memset(v[:, :, :, DH:DH + 1].rearrange("p a b c -> p (a b) c"), 1.0).then_inc(v_ones, 1)
                for c in range(NT):
                    dve.wait_ge(copied, c + 1)
                    dve.drain()
                    pairs = qk[:, c, :].rearrange("p (h j e) -> p h j e", h=2 * NH, e=2)
                    x1, x2 = pairs[:, :, 0:ROT // 2, 0], pairs[:, :, 0:ROT // 2, 1]

                    def table(n):
                        return rope[:, c, n, :].rearrange("p (o j) -> p o j", o=1).to_broadcast((P, 2 * NH, ROT // 2))

                    cos, sin = table(0), table(1)
                    dve.tensor_tensor(prod[0][:, :, :], x1, cos, ALU.mult)
                    dve.tensor_tensor(prod[1][:, :, :], x2, sin, ALU.mult)
                    dve.tensor_tensor(prod[2][:, :, :], x2, cos, ALU.mult)
                    dve.tensor_tensor(prod[3][:, :, :], x1, sin, ALU.mult)
                    dve.drain()
                    dve.tensor_tensor(x1, prod[0][:, :, :], prod[1][:, :, :], ALU.subtract)
                    dve.tensor_tensor(x2, prod[2][:, :, :], prod[3][:, :, :], ALU.add)


def attention_block(nc, ident, identb, qk, v, k_stack, ctx_out):
    with Scope(nc, "attn") as s:
        q_tok = [s.sb(f"q_tok{b}", [P, NT, TERMS, DH], BF16) for b in range(2)]
        k_tok = [s.sb(f"k_tok{b}", [P, NT, TERMS, DH], BF16) for b in range(2)]
        rest = s.sb("rest", [P, NT, DH])
        q_stack = s.sb("q_stack", [P, NH, T], BF16)
        v_group = [s.sb(f"v_group{b}", [P, NT, GH, VW]) for b in range(1)]
        row_max = s.sb("row_max", [P, NT, 2])
        neg_max = s.sb("neg_max", [P, NT])
        max_rest = s.sb("max_rest", [P, NT])
        max_tok = s.sb("max_tok", [P, NT, MROWS], BF16)
        probs = s.sb("probs", [P, 2 * GH, T])
        ctx_T = s.sb("ctx_T", [P, T])
        inv = s.sb("inv", [P, 4, GH])
        ps_q = [s.ps(f"rows_q{b}", [P, HALF]) for b in range(2)]
        ps_k = [s.ps(f"rows_k{b}", [P, HALF]) for b in range(3)]
        ps_ctx = [s.ps(f"ctx{b}", [P, HALF]) for b in range(2)]
        ps_turn = s.ps("turn", [P, HALF])
        turn_b = ps_turn[:, :].bitcast(BF16)
        split_q, split_k = s.sem("split_q"), s.sem("split_k")
        q_turned, k_turned = s.sem("q_turned"), s.sem("k_turned")
        q_stacked, k_stacked = s.sem("q_stacked"), s.sem("k_stacked")
        scored_q, maxed = s.sem("scored_q"), s.sem("maxed")
        max_split, max_turned, max_stacked = s.sem("max_split"), s.sem("max_turned"), s.sem("max_stacked")
        scored_k, exped = s.sem("scored_k"), s.sem("exped")
        v_ready, summed, ctx_copied = s.sem("v_ready"), s.sem("summed"), s.sem("ctx_copied")
        ctx_turned, ctx_done = s.sem("ctx_turned"), s.sem("ctx_done")
        NG = NH // GH

        with nc.Block() as block:

            @block.gpsimd
            def _(pool):
                one = dict(scalar1=1.0, scalar2=0.0, op0=ALU.mult, op1=ALU.add)

                def split(src, tok, places, done):
                    high, middle, low = places

                    def put(part, x):
                        for a, n, step in part:
                            dst = tok[:, :, a:a + (n - 1) * step + 1:step, :]
                            pool.tensor_scalar(dst, x.rearrange("p t (o d) -> p t o d", o=1).to_broadcast((P, NT, n, DH)),
                                               **one)
                        pool.drain()

                    put(high, src)
                    pool.tensor_tensor(rest[:, :, :], src, tok[:, :, high[0][0], :], ALU.subtract)
                    pool.drain()
                    put(middle, rest[:, :, :])
                    pool.tensor_tensor(rest[:, :, :], rest[:, :, :], tok[:, :, middle[0][0], :], ALU.subtract)
                    pool.drain()
                    (a, n, step), = low
                    pool.tensor_scalar(tok[:, :, a, :], rest[:, :, :], **one).then_inc(done, 1)
                    pool.drain()

                for h in range(NH):
                    b = h % 2
                    if h >= 2:
                        pool.wait_ge(q_turned, h - 1)
                        pool.wait_ge(k_turned, h - 1)
                    split(qk[:, :, h * DH:(h + 1) * DH], q_tok[b], ([(0, 2, 1), (5, 1, 1)], [(2, 2, 1)], [(4, 1, 1)]),
                          split_q)
                    split(qk[:, :, D + h * DH:D + (h + 1) * DH], k_tok[b], ([(0, 3, 2)], [(1, 2, 2)], [(5, 1, 1)]),
                          split_k)

            def slots():
                for n in range(NH + GH):
                    yield n, (n if n < NH else None), (n // GH - 1 if n >= GH else None), 2 * (n % GH)

            @block.tensor
            def _(pe):
                def turn_q(h):
                    pe.wait_ge(split_q, h + 1)
                    if h == 1:
                        pe.wait_ge(k_stacked, 1)
                    elif h > 1:
                        pe.wait_ge(max_stacked, h - 1)
                    for c in range(NT):
                        i = pe.transpose(turn_b[0:QROWS, c * P:(c + 1) * P],
                                         q_tok[h % 2][:, c, :, :].rearrange("p a b -> p (a b)"), identb[:, :])
                    i.then_inc(q_turned, 1)

                def turn_k(h):
                    pe.wait_ge(split_k, h + 1)
                    pe.wait_ge(q_stacked, h + 1)
                    for c in range(NT):
                        i = pe.transpose(turn_b[0:QROWS, c * P:(c + 1) * P],
                                         k_tok[h % 2][:, c, :, :].rearrange("p a b -> p (a b)"), identb[:, :])
                    i.then_inc(k_turned, 1)

                def turn_max(h):
                    pe.wait_ge(max_split, h + 1)
                    pe.wait_ge(k_stacked, min(h + 2, NH))
                    if h % GH == 0 and h >= 2 * GH:
                        pe.wait_ge(ctx_done, 2 * (h // GH - 1))
                    for c in range(NT):
                        i = pe.transpose(turn_b[0:MROWS, c * P:(c + 1) * P], max_tok[:, c, :], identb[:, :])
                    i.then_inc(max_turned, 1)

                def score_rows_q(h, r):
                    if r == 0:
                        pe.wait_ge(q_stacked, h + 1)
                        pe.wait_ge(k_stacked, h + 1)
                    for b in range(2):
                        n = 2 * (NT * h + r) + b
                        if n >= 2:
                            pe.wait_ge(maxed, n - 1)
                        pe.matmul(ps_q[b][:, :], q_stack[0:QROWS, h, r * P:(r + 1) * P],
                                  k_stack[0:QROWS, h, b * HALF:(b + 1) * HALF], start=True, stop=True)\
                            .then_inc(scored_q, 1)

                def score_rows_k(g, t, j):
                    h = g * GH + j
                    if t == 0:
                        pe.wait_ge(max_stacked, h + 1)
                    for b in range(2):
                        n = 2 * (g * NT * GH + t * GH + j) + b
                        if n >= 3:
                            pe.wait_ge(exped, n - 2)
                        pe.matmul(ps_k[n % 3][:, :], k_stack[0:QROWS + MROWS, h, t * P:(t + 1) * P],
                                  q_stack[0:QROWS + MROWS, h, b * HALF:(b + 1) * HALF], start=True, stop=True)\
                            .then_inc(scored_k, 1)

                def weigh(g, t):
                    pe.wait_ge(exped, 2 * GH * (g * NT + t + 1))
                    if t == 0:
                        pe.wait_ge(v_ready, g + 1)
                        if g >= 1:
                            pe.wait_ge(ctx_copied, g)
                    for b in range(2):
                        for j in range(GH):
                            i = pe.matmul(ps_ctx[b][j * VW:(j + 1) * VW, :], v_group[0][:, t, j, :],
                                          probs[:, (t % 2) * GH + j, b * HALF:(b + 1) * HALF],
                                          start=(t == 0), stop=(t == NT - 1))
                    i.then_inc(summed, 1)

                def turn_ctx(g):
                    pe.wait_ge(ctx_copied, g + 1)
                    for half in range(2):
                        if half == 1:
                            pe.wait_ge(ctx_done, 2 * g + 1)
                        elif g < NG - 2:
                            pe.wait_ge(k_stacked, GH * (g + 2) + 2)
                        else:
                            pe.wait_ge(max_stacked, NH)
                            if g == NG - 1:
                                pe.wait_ge(ctx_done, 2 * g)
                        for c in range(4):
                            cc = 4 * half + c
                            i = pe.transpose(ps_turn[:, c * P:(c + 1) * P], ctx_T[:, cc * P:(cc + 1) * P], ident[:, :])
                        i.then_inc(ctx_turned, 1)

                turn_q(0)
                turn_k(0)
                for n, head, g, t0 in slots():
                    for u in range(NT):
                        if u == 1 and 1 <= n <= NH:
                            turn_max(n - 1)
                        if head is not None:
                            if u == 3 and head + 1 < NH:
                                turn_q(head + 1)
                            if u == 5 and head + 1 < NH:
                                turn_k(head + 1)
                            score_rows_q(head, u)
                        if g is not None:
                            if u == 4:
                                if t0 > 0:
                                    weigh(g, t0 - 1)
                                elif g > 0:
                                    weigh(g - 1, NT - 1)
                            score_rows_k(g, t0 + u // GH, u % GH)
                            if u == 7:
                                weigh(g, t0)
                    if g is not None and g > 0 and n % GH == 0:
                        turn_ctx(g - 1)
                weigh(NG - 1, NT - 1)
                turn_ctx(NG - 1)

            @block.scalar
            def _(act):
                def stack_q(h):
                    act.wait_ge(q_turned, h + 1)
                    act.activation(q_stack[0:QROWS, h, :], turn_b[0:QROWS, :], ACT.Copy).then_inc(q_stacked, 1)

                def exp(g, t, j):
                    for b in range(2):
                        n = 2 * (g * NT * GH + t * GH + j) + b
                        if j == 0 and b == 0 and g * NT + t >= 2:
                            act.wait_ge(summed, g * NT + t - 1)
                        act.wait_ge(scored_k, n + 1)
                        act.activation(probs[:, (t % 2) * GH + j, b * HALF:(b + 1) * HALF], ps_k[n % 3][:, :],
                                       ACT.Exp).then_inc(exped, 1)

                stack_q(0)
                for n, head, g, t0 in slots():
                    for u in range(NT):
                        if head is not None and u == 3 and head + 1 < NH:
                            stack_q(head + 1)
                        if g is not None:
                            exp(g, t0 + u // GH, u % GH)

            @block.vector
            def _(dve):
                def stack_k(h):
                    dve.wait_ge(k_turned, h + 1)
                    dve.tensor_copy(k_stack[0:QROWS, h, :], turn_b[0:QROWS, :]).then_inc(k_stacked, 1)

                def stack_max(h):
                    dve.wait_ge(max_turned, h + 1)
                    dve.tensor_copy(q_stack[QROWS:QROWS + MROWS, h, :], turn_b[0:MROWS, :]).then_inc(max_stacked, 1)

                def row_maxima(h, r):
                    for b in range(2):
                        n = 2 * (NT * h + r) + b
                        dve.wait_ge(scored_q, n + 1)
                        dve.tensor_reduce(row_max[:, r, b:b + 1], ps_q[b][:, :], axis=AX, op=ALU.max)\
                            .then_inc(maxed, 1)

                def split_maxima(h):
                    dve.drain()
                    if h >= 1:
                        dve.wait_ge(max_turned, h)
                    dve.tensor_tensor(neg_max[:, :], row_max[:, :, 0], row_max[:, :, 1], ALU.max)
                    dve.drain()
                    dve.tensor_scalar(neg_max[:, :], neg_max[:, :], -1.0, None, ALU.mult)
                    dve.drain()
                    dve.tensor_copy(max_tok[:, :, 0], neg_max[:, :])
                    dve.drain()
                    dve.tensor_tensor(max_rest[:, :], neg_max[:, :], max_tok[:, :, 0], ALU.subtract)
                    dve.drain()
                    dve.tensor_copy(max_tok[:, :, 1], max_rest[:, :])
                    dve.drain()
                    dve.tensor_tensor(max_tok[:, :, 2], max_rest[:, :], max_tok[:, :, 1], ALU.subtract)\
                        .then_inc(max_split, 1)

                def values(g):
                    if g >= 1:
                        dve.wait_ge(summed, NT * g)
                    dve.tensor_copy(v_group[0][:, :, :, :], v[:, :, g * GH:(g + 1) * GH, :]).then_inc(v_ready, 1)

                def copy_ctx(g):
                    dve.wait_ge(summed, NT * (g + 1))
                    if g >= 1:
                        dve.wait_ge(ctx_turned, 2 * g)
                    for b in range(2):
                        i = dve.tensor_copy(ctx_T[:, b * HALF:(b + 1) * HALF], ps_ctx[b][:, :])
                    i.then_inc(ctx_copied, 1)

                def norm_ctx(g):
                    for half in range(2):
                        dve.wait_ge(ctx_turned, 2 * g + half + 1)
                        view = ps_turn[:, :].rearrange("p (c j w) -> p c j w", c=4, j=GH)
                        dve.reciprocal(inv[:, :, :], view[:, :, :, DH])
                        dve.drain()
                        for c in range(4):
                            out = ctx_out[:, 4 * half + c, g * GH * DH:(g + 1) * GH * DH].rearrange(
                                "p (j d) -> p j d", j=GH)
                            i = dve.tensor_tensor(out, view[:, c, :, 0:DH], col(inv[:, c, :], DH), ALU.mult)
                        i.then_inc(ctx_done, 1)

                stack_k(0)
                values(0)
                for n, head, g, t0 in slots():
                    for u in range(NT):
                        if u == 1 and 1 <= n <= NH:
                            stack_max(n - 1)
                        if u == 5 and head is not None and head + 1 < NH:
                            stack_k(head + 1)
                        if head is not None:
                            row_maxima(head, u)
                        if g is not None and u == 5 and n % GH == 0 and g > 0:
                            copy_ctx(g - 1)
                            values(g)
                    if head is not None:
                        split_maxima(head)
                    if g is not None and g > 0 and n % GH == 0:
                        norm_ctx(g - 1)
                copy_ctx(NG - 1)
                norm_ctx(NG - 1)


def turn_block(nc, tag, ident, src, dst):
    with Scope(nc, tag) as s:
        turned = [s.ps(f"turned{k}", [P, T]) for k in range(DK)]
        turn_done = s.sem("turn_done")
        with nc.Block() as block:

            @block.tensor
            def _(pe):
                for h in range(2):
                    for c in range(4 * h, 4 * h + 4):
                        for k in range(DK):
                            i = pe.transpose(turned[k][:, c * P:(c + 1) * P], src[:, c, k * P:(k + 1) * P], ident[:, :])
                    i.then_inc(turn_done, 1)

            @block.scalar
            def _(act):
                for h in range(2):
                    act.wait_ge(turn_done, h + 1)
                    for k in range(DK):
                        act.activation(dst[:, k, h * HALF:(h + 1) * HALF], turned[k][:, h * HALF:(h + 1) * HALF],
                                       ACT.Copy)


NE = 8
FE = 256
FK = FE // P
NL, RANK = 2, 64
CENTER = 1.0 / math.e
LOWER = 0.5 - math.log(4.0 / 3.0)
Z_LOWER = math.log(LOWER / (1.0 - LOWER))
Z_UPPER = 2.0 ** -23


def rank_mask(dve, scores, mask, greater, same, earlier, n, top):
    a = scores.shape[1]
    other = scores.rearrange("p a (o j) -> p a o j", o=1).to_broadcast((P, a, n, n))
    own = scores.rearrange("p a (i o) -> p a i o", o=1).to_broadcast((P, a, n, n))
    dve.tensor_tensor(greater, other, own, ALU.is_gt)
    dve.tensor_tensor(same, other, own, ALU.is_equal)
    dve.drain()
    dve.tensor_tensor(same, same, earlier.rearrange("p (o i) j -> p o i j", o=1).to_broadcast((P, a, n, n)), ALU.mult)
    dve.drain()
    dve.tensor_tensor(greater, greater, same, ALU.add)
    dve.drain()
    dve.tensor_reduce(mask, greater, axis=AX, op=ALU.add)
    dve.drain()
    dve.tensor_scalar(mask, mask, float(top), None, ALU.is_lt)
    dve.drain()


def golden_router_block(nc, ident, Wr, temperature, earlier, xT, w_dram):
    with Scope(nc, "gold") as s:
        wr = s.sb("wr", [P, DK, NE])
        temp = s.sb("temp", [P, 1])
        inv_temp = s.sb("inv_temp", [P, 1])
        z = s.sb("z", [P, NT, NE])
        ez = s.sb("ez", [P, NT, NE])
        dist = s.sb("dist", [P, NT, NE])
        w = s.sb("w", [P, NT, NE])
        fb = s.sb("fb", [P, NT, NE])
        zone = s.sb("zone", [P, NT, NE])
        mask = s.sb("mask", [P, NT, NE])
        total = s.sb("total", [P, NT])
        none = s.sb("none", [P, NT])
        greater = s.sb("greater", [P, NT, NE, NE])
        same = s.sb("same", [P, NT, NE, NE])
        w_rows = s.sb("w_rows", [NE, T])
        logits = s.ps("logits", [P, NT, NE])
        w_turned = s.ps("w_turned", [NE, T])
        loaded, scored, z_ready, e_ready = s.sem("loaded"), s.sem("scored"), s.sem("z_ready"), s.sem("e_ready")
        d_ready, f_ready, w_ready = s.sem("d_ready"), s.sem("f_ready"), s.sem("w_ready")
        turned, rows_ready, stored = s.sem("turned"), s.sem("rows_ready"), s.sem("stored")
        flat = "p a b -> p (a b)"
        with nc.Block() as block:

            @block.sync
            def _(sp):
                sp.dma_start(wr[:, :, :], Wr.rearrange("(k p) n -> p k n", p=P)).then_inc(loaded, 16)
                sp.dma_start(temp[:, :], temperature.rearrange("(o n) -> o n", o=1).to_broadcast((P, 1)))\
                    .then_inc(loaded, 16)
                sp.wait_ge(rows_ready, 1)
                sp.dma_start(w_dram, w_rows[:, :]).then_inc(stored, 16)
                sp.wait_ge(stored, 16)

            @block.tensor
            def _(pe):
                pe.wait_ge(loaded, 32)
                for c in range(NT):
                    for k in range(DK):
                        i = pe.matmul(logits[:, c, :], xT[:, k, c * P:(c + 1) * P], wr[:, k, :], start=(k == 0),
                                      stop=(k == DK - 1))
                i.then_inc(scored, 1)
                pe.wait_ge(w_ready, 1)
                for c in range(NT):
                    i = pe.transpose(w_turned[:, c * P:(c + 1) * P], w[:, c, :], ident[:, :])
                i.then_inc(turned, 1)

            @block.scalar
            def _(act):
                act.wait_ge(z_ready, 1)
                act.activation(ez[:, :, :], z[:, :, :], ACT.Exp, scale=-1.0).then_inc(e_ready, 1)
                act.wait_ge(d_ready, 1)
                act.activation(w[:, :, :], dist[:, :, :], ACT.Exp, scale=-1.0 / 0.1)
                act.activation(fb[:, :, :], dist[:, :, :], ACT.Exp, scale=-1.0 / 0.3).then_inc(f_ready, 1)
                act.wait_ge(turned, 1)
                act.activation(w_rows[:, :], w_turned[:, :], ACT.Copy).then_inc(rows_ready, 1)

            @block.vector
            def _(dve):
                dve.wait_ge(loaded, 32)
                dve.reciprocal(inv_temp[:, :], temp[:, :])
                dve.wait_ge(scored, 1)
                dve.drain()
                dve.tensor_scalar(z[:, :, :], logits[:, :, :], inv_temp[:, 0:1], -80.0, ALU.mult, ALU.max).then_inc(z_ready, 1)
                dve.drain()
                dve.tensor_scalar(zone[:, :, :], z[:, :, :], Z_LOWER, None, ALU.is_ge)
                dve.tensor_scalar(mask[:, :, :], z[:, :, :], Z_UPPER, None, ALU.is_le)
                dve.drain()
                dve.tensor_tensor(zone[:, :, :], zone[:, :, :], mask[:, :, :], ALU.mult)
                dve.wait_ge(e_ready, 1)
                dve.tensor_scalar(ez[:, :, :], ez[:, :, :], 1.0, None, ALU.add)
                dve.drain()
                dve.reciprocal(ez[:, :, :].rearrange(flat), ez[:, :, :].rearrange(flat))
                dve.drain()
                dve.tensor_scalar(ez[:, :, :], ez[:, :, :], CENTER, None, ALU.subtract)
                dve.drain()
                dve.tensor_scalar(dist[:, :, :], ez[:, :, :], -1.0, None, ALU.mult)
                dve.drain()
                dve.tensor_tensor(dist[:, :, :], dist[:, :, :], ez[:, :, :], ALU.max).then_inc(d_ready, 1)
                dve.wait_ge(f_ready, 1)
                dve.tensor_tensor(w[:, :, :], w[:, :, :], zone[:, :, :], ALU.mult)
                dve.drain()
                dve.tensor_reduce(total[:, :], w[:, :, :], axis=AX, op=ALU.add)
                dve.drain()
                dve.tensor_scalar(none[:, :], total[:, :], 1e-8, None, ALU.is_lt)
                rank_mask(dve, fb[:, :, :], mask[:, :, :], greater[:, :, :, :], same[:, :, :, :], earlier, NE, 2)

                def normalise(a):
                    dve.tensor_reduce(total[:, :], a, axis=AX, op=ALU.add)
                    dve.drain()
                    dve.tensor_scalar(total[:, :], total[:, :], 1e-8, None, ALU.max)
                    dve.drain()
                    dve.reciprocal(total[:, :], total[:, :])
                    dve.drain()
                    return dve.tensor_tensor(a, a, col(total[:, :], NE), ALU.mult)

                dve.tensor_tensor(fb[:, :, :], fb[:, :, :], mask[:, :, :], ALU.mult)
                dve.drain()
                normalise(fb[:, :, :])
                dve.drain()
                dve.tensor_tensor(fb[:, :, :], fb[:, :, :], w[:, :, :], ALU.subtract)
                dve.drain()
                dve.tensor_tensor(fb[:, :, :], fb[:, :, :], col(none[:, :], NE), ALU.mult)
                dve.drain()
                dve.tensor_tensor(w[:, :, :], w[:, :, :], fb[:, :, :], ALU.add)
                dve.drain()
                normalise(w[:, :, :]).then_inc(w_ready, 1)


def low_rank_block(nc, ident, lora, rings, w_down, Wg, Wu, Wd):
    with Scope(nc, "lora") as s:
        a_sb = s.sb("a", [P, 3, NL, FK, RANK])
        b_sb = s.sb("b", [RANK, 3, NL, FE])
        a_T = s.sb("a_T", [RANK, 3, NL, FK, P])
        ps_t = [s.ps(f"turned{b}", [RANK, FK, P]) for b in range(2)]
        ps_w = [s.ps(f"product{b}", [P, FK, FE]) for b in range(2)]
        loaded, turned, copied = s.sem("loaded"), s.sem("turned"), s.sem("copied")
        producted, added = s.sem("producted"), s.sem("added")
        jobs = [(m, e) for e in range(NL) for m in range(3)]
        with nc.Block() as block:

            @block.sync
            def _(sp):
                n = 0
                for m, (A, B) in enumerate(lora):
                    for e in range(NL):
                        sp.dma_start(a_sb[:, m, e, :, :], A[e].rearrange("(k p) r -> p k r", p=P)).then_inc(loaded, 16)
                        sp.dma_start(b_sb[:, m, e, :], B[e]).then_inc(loaded, 16)
                        n += 2
                for e in range(NL):
                    for r, W in zip(rings, (Wg, Wu)):
                        sp.dma_start(r[e][:, :, :], W[e].rearrange("(k p) f -> p k f", p=P)).then_inc(loaded, 16)
                        n += 1
                sp.dma_start(w_down[:, :, :, :], Wd.rearrange("e (k p) d -> p e k d", p=P)).then_inc(loaded, 16)
                assert n + 1 == 17

            @block.tensor
            def _(pe):
                pe.wait_ge(loaded, 16 * 17)
                for n, (m, e) in enumerate(jobs):
                    if n >= 2:
                        pe.wait_ge(copied, n - 1)
                    for k in range(FK):
                        i = pe.transpose(ps_t[n % 2][:, k, :], a_sb[:, m, e, k, :], ident[:, :])
                    i.then_inc(turned, 1)
                    pe.wait_ge(copied, n + 1)
                    if n >= 2:
                        pe.wait_ge(added, n - 1)
                    for k in range(FK):
                        i = pe.matmul(ps_w[n % 2][:, k, :], a_T[:, m, e, k, :], b_sb[:, m, e, :], start=True, stop=True)
                    i.then_inc(producted, 1)

            @block.scalar
            def _(act):
                for n, (m, e) in enumerate(jobs):
                    act.wait_ge(turned, n + 1)
                    act.activation(a_T[:, m, e, :, :], ps_t[n % 2][:, :, :], ACT.Copy).then_inc(copied, 1)

            @block.vector
            def _(dve):
                for n, (m, e) in enumerate(jobs):
                    dve.wait_ge(producted, n + 1)
                    dst = rings[m][e][:, :, :] if m < 2 else w_down[:, e, :, :]
                    dve.tensor_tensor(dst, dst, ps_w[n % 2][:, :, :], ALU.add).then_inc(added, 1)


def experts_block(nc, rings, xT, w_dram, Wg, Wu, mids):
    with Scope(nc, "moe0") as s:
        weight = [s.sb(f"weight{b}", [P, T]) for b in range(2)]
        gated = [s.sb(f"gated{b}", [P, HALF]) for b in range(2)]
        hidden = [s.sb(f"hidden{b}", [P, HALF]) for b in range(2)]
        ps_g = [s.ps(f"gate{b}", [P, HALF]) for b in range(2)]
        ps_u = [s.ps(f"up{b}", [P, HALF]) for b in range(2)]
        w_loaded = [s.sem(f"w_loaded{b}") for b in range(2)]
        r_loaded = [s.sem(f"r_loaded{b}") for b in range(2)]
        gate_done, up_done = s.sem("gate_done"), s.sem("up_done")
        gate_free, up_free = s.sem("gate_free"), s.sem("up_free")
        hidden_free = s.sem("hidden_free")
        U = 2 * FK

        with nc.Block() as block:

            @block.sync
            def _(sp):
                for b in range(2):
                    sp.dma_start(weight[b][:, :], w_dram[b:b + 1, :].to_broadcast((P, T))).then_inc(r_loaded[b], 16)
                with sp.Fori(0, NE // 2 - 1) as i:
                    for b in range(2):
                        sp.wait_ge(up_done, U * (2 * i + b + 1))
                        for r, W in zip(rings, (Wg, Wu)):
                            src = W[bass.ds(2 * i + b + 2, 1), :, :].rearrange("o (k p) f -> p (o k) f", p=P)
                            sp.dma_start(r[b][:, :, :], src).then_inc(w_loaded[b], 16)
                        sp.wait_ge(hidden_free, U * (2 * i + b + 1))
                        sp.dma_start(weight[b][:, :], w_dram[bass.ds(2 * i + b + 2, 1), :].to_broadcast((P, T)))\
                            .then_inc(r_loaded[b], 16)

            @block.tensor
            def _(pe):
                def expert(i, b, first):
                    if not first:
                        pe.wait_ge(w_loaded[b], 32 * i)
                    for u in range(U):
                        f, half = divmod(u, 2)
                        n = U * (2 * i + b) + u
                        for ring, ps, free, done in ((rings[0], ps_g, gate_free, gate_done),
                                                     (rings[1], ps_u, up_free, up_done)):
                            if not (first and b == 0 and u < 2):
                                pe.wait_ge(free, n - 1)
                            for k in range(DK):
                                m = pe.matmul(ps[u % 2][:, :], ring[b][:, k, f * P:(f + 1) * P],
                                              xT[:, k, half * HALF:(half + 1) * HALF], start=(k == 0), stop=(k == DK - 1))
                            m.then_inc(done, 1)
                for b in range(2):
                    expert(0, b, True)
                with pe.Fori(1, NE // 2) as i:
                    for b in range(2):
                        expert(i, b, False)

            @block.scalar
            def _(act):
                def expert(i, b, first):
                    for u in range(U):
                        n = U * (2 * i + b) + u
                        if not (first and b == 0 and u < 2):
                            act.wait_ge(up_free, n - 1)
                        act.wait_ge(gate_done, n + 1)
                        act.activation(gated[u % 2][:, :], ps_g[u % 2][:, :], ACT.Silu).then_inc(gate_free, 1)
                for b in range(2):
                    expert(0, b, True)
                with act.Fori(1, NE // 2) as i:
                    for b in range(2):
                        expert(i, b, False)

            @block.vector
            def _(dve):
                def expert(i, b, first):
                    for u in range(U):
                        n = U * (2 * i + b) + u
                        if not (first and b == 0 and u < 2):
                            dve.wait_ge(hidden_free, n - 1)
                        dve.wait_ge(gate_free, n + 1)
                        dve.wait_ge(up_done, n + 1)
                        dve.tensor_tensor(hidden[u % 2][:, :], gated[u % 2][:, :], ps_u[u % 2][:, :], ALU.mult)\
                            .then_inc(up_free, 1)
                for b in range(2):
                    expert(0, b, True)
                with dve.Fori(1, NE // 2) as i:
                    for b in range(2):
                        expert(i, b, False)

            @block.gpsimd
            def _(pool):
                def expert(i, b, first):
                    pool.wait_ge(r_loaded[b], 16 * i + 16)
                    for u in range(U):
                        f, half = divmod(u, 2)
                        n = U * (2 * i + b) + u
                        pool.wait_ge(up_free, n + 1)
                        cols = slice(half * HALF, (half + 1) * HALF)
                        out = (mids[:, FK * b + f:FK * b + f + 1, cols] if first else
                               mids[:, bass.ds(2 * FK * i + FK * b + f, 1), cols])
                        pool.tensor_tensor(out.rearrange("p o t -> p (o t)"), hidden[u % 2][:, :],
                                           weight[b][:, cols], ALU.mult).then_inc(hidden_free, 1)
                for b in range(2):
                    expert(0, b, True)
                with pool.Fori(1, NE // 2) as i:
                    for b in range(2):
                        expert(i, b, False)


LH = 16
HD = 128
TAPS = 4


def decay_block(nc, ident, Wb, bb, xT, decay_dram, cols):
    with Scope(nc, "decay") as s:
        wb = s.sb("wb", [P, DK, LH])
        bias = s.sb("bias", [LH, 1])
        z = s.sb("z", [LH, T])
        soft = s.sb("soft", [LH, T])
        log_b = s.sb("log_b", [LH, T])
        total = s.sb("total", [LH, T])
        one = s.sb("one", [LH, T])
        ps_z = s.ps("z_sum", [LH, T])
        ps_c = s.ps("turned", [P, 2, NT, LH])
        loaded, z_done, z_ready = s.sem("loaded"), s.sem("z_done"), s.sem("z_ready")
        soft_ready, sums_ready = s.sem("soft_ready"), s.sem("sums_ready")
        turned, stored, acts, one_ready = s.sem("turned"), s.sem("stored"), s.sem("acts"), s.sem("one_ready")
        with nc.Block() as block:

            @block.sync
            def _(sp):
                sp.dma_start(wb[:, :, :], Wb.rearrange("(k p) h -> p k h", p=P)).then_inc(loaded, 16)
                sp.dma_start(bias[:, :], bb.rearrange("(h o) -> h o", o=1)).then_inc(loaded, 16)
                sp.wait_ge(sums_ready, 1)
                sp.dma_start(decay_dram, total[:, :]).then_inc(stored, 16)
                sp.wait_ge(stored, 16)

            @block.tensor
            def _(pe):
                pe.wait_ge(loaded, 32)
                for half in range(2):
                    for k in range(DK):
                        i = pe.matmul(ps_z[:, half * HALF:(half + 1) * HALF], wb[:, k, :],
                                      xT[:, k, half * HALF:(half + 1) * HALF], start=(k == 0), stop=(k == DK - 1))
                i.then_inc(z_done, 1)
                pe.wait_ge(sums_ready, 1)
                for n, src in enumerate((total, log_b)):
                    for c in range(NT):
                        i = pe.transpose(ps_c[:, n, c, :], src[:, c * P:(c + 1) * P], ident[0:LH, 0:LH])
                i.then_inc(turned, 1)

            @block.scalar
            def _(act):
                act.wait_ge(z_done, 1)
                act.activation(z[:, :], ps_z[:, :], ACT.Identity, bias=bias[:, 0:1]).then_inc(z_ready, 1)
                act.wait_ge(z_ready, 1)
                act.activation(soft[:, :], z[:, :], ACT.Abs).then_inc(acts, 1)
                act.wait_ge(acts, 1)
                act.activation(soft[:, :], soft[:, :], ACT.Exp, scale=-1.0).then_inc(acts, 1)
                act.wait_ge(acts, 2)
                act.wait_ge(one_ready, 1)
                act.activation(soft[:, :], soft[:, :], ACT.Ln, bias=one[:, 0:1]).then_inc(soft_ready, 1)

            @block.vector
            def _(dve):
                dve.memset(one[:, :], 1.0).then_inc(one_ready, 1)
                dve.wait_ge(z_ready, 1)
                dve.tensor_scalar(log_b[:, :], z[:, :], 0.0, None, ALU.min)
                dve.wait_ge(soft_ready, 1)
                dve.drain()
                dve.tensor_tensor(log_b[:, :], log_b[:, :], soft[:, :], ALU.subtract)
                dve.drain()
                dve.tensor_tensor(z[:, :], log_b[:, :], z[:, :], ALU.subtract)
                dve.drain()
                for c in range(NT):
                    i = dve.tensor_tensor_scan(total[:, c * P:(c + 1) * P], one[:, 0:P], z[:, c * P:(c + 1) * P], 0.0,
                                               ALU.mult, ALU.add)
                i.then_inc(sums_ready, 1)
                dve.wait_ge(turned, 1)
                dve.tensor_copy(cols[:, :, :, :], ps_c[:, :, :, :])


def linear_attention_block(nc, ident, neg_half, w, xT, decay_dram, cols, norm_row, norm_col, gated_out):
    with Scope(nc, "lin") as s:
        Wq, Wk, Wv, Wg = w["q"], w["k"], w["v"], w["gate"]
        wq, wk, wv, wg = ([s.sb(f"w_{m}{b}", [P, DK, HD]) for b in range(2)] for m in ("q", "k", "v", "gate"))
        taps = [s.sb(f"taps{b}", [P, 2, TAPS + 1]) for b in range(2)]
        decay = [s.sb(f"decay{b}", [P, T]) for b in range(2)]
        hcol = [s.sb(f"hcol{b}", [P, 2, NT]) for b in range(2)]
        conv = [s.sb(f"conv_{m}", [P, T]) for m in "qk"]
        stats = s.sb("stats", [P, 2, NT, 6])
        mean_var = s.sb("mean_var", [P, 2, NT, 2])
        var_eps = s.sb("var_eps", [P, 2, NT])
        rstd = s.sb("rstd", [P, 2, NT])
        k_shift = s.sb("k_shift", [P, NT])
        normed = [s.sb(f"normed_{m}", [P, NT, HD]) for m in "qk"]
        k_rows = s.sb("k_rows", [P, NT, HD])
        q_T = s.sb("q_T", [P, T])
        k_T = s.sb("k_T", [P, T])
        q_dec = s.sb("q_dec", [P, T])
        v_rows = [s.sb(f"v_rows{b}", [P, NT, HD]) for b in range(2)]
        v_dec = s.sb("v_dec", [P, NT, HD])
        gate = s.sb("gate", [P, T])
        arg = s.sb("arg", [P, NT, P])
        mix = s.sb("mix", [P, NT, P])
        e_dec = s.sb("e_dec", [P, T])
        probs = s.sb("probs", [P, NT, P])
        state = s.sb("state", [P, NT, HD])
        ps = [s.ps(f"pair{n}", [P, T]) for n in range(4)]
        tiled = [p[:, :].rearrange("p (c d) -> p c d", c=NT) for p in ps]
        sem = s.sem
        qk_loaded, v_loaded, g_loaded, d_loaded = ([sem(f"{m}_loaded{b}") for b in range(2)] for m in ("qk", "v", "g", "d"))
        q_projected, k_projected, v_projected, g_projected = (sem(f"{m}_projected") for m in "qkvg")
        q_tapped, k_tapped, q_conved, k_conved, q_acted, k_acted = (
            sem(f"{m}_{x}") for x in ("tapped", "conved", "acted") for m in "qk")
        q_rowed, k_rowed = sem("q_rowed"), sem("k_rowed")
        var_ready, rstd_ready, shift_ready = sem("var_ready"), sem("rstd_ready"), sem("shift_ready")
        q_normed, k_normed, k_rows_done = sem("q_normed"), sem("k_normed"), sem("k_rows_done")
        q_turned, k_turned, q_T_done, k_T_done = sem("q_turned"), sem("k_turned"), sem("q_T_done"), sem("k_T_done")
        v_copied, v_dec_done, g_acted = sem("v_copied"), sem("v_dec_done"), sem("g_acted")
        arg_ready, mix_exped, masked, e_dec_done, q_dec_done = (
            sem(x) for x in ("arg_ready", "mix_exped", "masked", "e_dec_done", "q_dec_done"))
        scored, kv_done, probs_done, states_done = (sem(x) for x in ("scored", "kv_done", "probs_done", "states_done"))
        o_done, gated = sem("o_done"), sem("gated")

        def pipeline(eng, step):
            step(0, 0, True, False, False)
            step(0, 1, True, True, False)
            for b in range(2):
                step(1, b, True, True, True)
            with eng.Fori(2, LH // 2) as i:
                for b in range(2):
                    step(i, b, True, True, True)
            step(LH // 2, 0, False, True, True)
            step(LH // 2, 1, False, False, True)

        def wait_for(eng, semaphore, count):
            if not (isinstance(count, int) and count < 1):
                eng.wait_ge(semaphore, count)

        def loads(i, b, lag):
            return i + (b - lag - (b - lag) % 2) // 2 + 1

        with nc.Block() as block:

            @block.sync
            def _(sp):
                def head(m, b, reuse):
                    def cols_of(W):
                        view = W.rearrange("(k p) (h c) -> p k h c", p=P, c=HD)
                        return view[:, :, bass.ds(m, 1), :].rearrange("p k o c -> p k (o c)")

                    if reuse:
                        sp.wait_ge(k_projected, m - 1)
                        sp.wait_ge(k_conved, m - 1)
                    sp.dma_start(wq[b][:, :, :], cols_of(Wq)).then_inc(qk_loaded[b], 16)
                    sp.dma_start(wk[b][:, :, :], cols_of(Wk)).then_inc(qk_loaded[b], 16)
                    for j, (cw, cb) in enumerate((w["q_taps"], w["k_taps"])):
                        rows = cw.rearrange("(h p) t -> p h t", p=P)[:, bass.ds(m, 1), :].rearrange("p o t -> p (o t)")
                        sp.dma_start(taps[b][:, j, 0:TAPS], rows).then_inc(qk_loaded[b], 16)
                        bias = cb.rearrange("(h p o) -> p h o", p=P, o=1)[:, bass.ds(m, 1), :]
                        sp.dma_start(taps[b][:, j, TAPS:TAPS + 1], bias.rearrange("p a o -> p (a o)"))\
                            .then_inc(qk_loaded[b], 16)
                    if reuse:
                        sp.wait_ge(v_projected, m - 1)
                    sp.dma_start(wv[b][:, :, :], cols_of(Wv)).then_inc(v_loaded[b], 16)
                    if reuse:
                        sp.wait_ge(e_dec_done, m - 1)
                    sp.dma_start(decay[b][:, :], decay_dram[bass.ds(m, 1), :].to_broadcast((P, T))).then_inc(d_loaded[b], 16)
                    if reuse:
                        sp.wait_ge(g_projected, m - 1)
                    sp.dma_start(wg[b][:, :, :], cols_of(Wg)).then_inc(g_loaded[b], 16)

                for b in range(2):
                    head(b, b, False)
                with sp.Fori(1, LH // 2) as i:
                    for b in range(2):
                        head(2 * i + b, b, True)

            @block.tensor
            def _(pe):
                def project(weights, out, done):
                    for half in range(2):
                        cols = slice(half * HALF, (half + 1) * HALF)
                        for k in range(DK):
                            i = pe.matmul(out[:, cols], weights[:, k, :], xT[:, k, cols], start=(k == 0), stop=(k == DK - 1))
                    i.then_inc(done, 1)

                def turn(out, src, done):
                    for c in range(NT):
                        i = pe.transpose(out[:, c * P:(c + 1) * P], src(c), ident[:, :])
                    i.then_inc(done, 1)

                def step(i_, b, a0, a1, a2):
                    n = 2 * i_ + b
                    if a1:
                        pe.wait_ge(v_loaded[1 - b], 16 * loads(i_, b, 1))
                        pe.wait_ge(q_conved, n)
                        for c in range(NT):
                            for k in range(DK):
                                i = pe.matmul(tiled[0][:, c, :], xT[:, k, c * P:(c + 1) * P], wv[1 - b][:, k, :],
                                              start=(k == 0), stop=(k == DK - 1))
                        i.then_inc(v_projected, 1)
                        pe.wait_ge(q_acted, n)
                        if a2:
                            pe.wait_ge(k_T_done, n - 1)
                        turn(ps[1], lambda c: conv[0][:, c * P:(c + 1) * P], q_rowed)
                        pe.wait_ge(k_acted, n)
                        turn(ps[2], lambda c: conv[1][:, c * P:(c + 1) * P], k_rowed)
                    if a2:
                        pe.wait_ge(g_loaded[b], 16 * loads(i_, b, 2))
                        wait_for(pe, gated, n - 2)
                        project(wg[b], ps[3], g_projected)
                        if a1:
                            pe.wait_ge(v_copied, n)
                        else:
                            wait_for(pe, probs_done, n - 2)
                        pe.wait_ge(q_T_done, n - 1)
                        pe.wait_ge(k_T_done, n - 1)
                        for c in range(NT):
                            cols = slice(c * P, (c + 1) * P)
                            i = pe.matmul(ps[0][:, cols], k_T[:, cols], q_T[:, cols], start=True, stop=True)
                        i.then_inc(scored, 1)
                        pe.wait_ge(g_acted, n - 1)
                        pe.wait_ge(k_rows_done, n - 1)
                        pe.wait_ge(v_dec_done, n - 1)
                        for c in range(NT - 1):
                            i = pe.matmul(tiled[3][:, c, :], k_rows[:, c, :], v_dec[:, c, :], start=True, stop=True)
                        i.then_inc(kv_done, 1)
                    if a0:
                        pe.wait_ge(qk_loaded[b], 96 * loads(i_, b, 0))
                        if a2:
                            pe.wait_ge(probs_done, n - 1)
                        elif a1:
                            pe.wait_ge(v_copied, n)
                        project(wq[b], ps[0], q_projected)
                    if a1:
                        pe.wait_ge(q_normed, n)
                        if a2:
                            pe.wait_ge(states_done, n - 1)
                        turn(ps[3], lambda c: normed[0][:, c, :], q_turned)
                        pe.wait_ge(k_normed, n)
                        turn(ps[1], lambda c: normed[1][:, c, :], k_turned)
                    if a0:
                        project(wk[b], ps[2], k_projected)
                    if a2:
                        pe.wait_ge(probs_done, n - 1)
                        pe.wait_ge(states_done, n - 1)
                        pe.wait_ge(q_dec_done, n - 1)
                        if a1:
                            pe.wait_ge(q_T_done, n)
                        for c in range(NT):
                            cols = slice(c * P, (c + 1) * P)
                            i = pe.matmul(ps[3][:, cols], v_rows[b][:, c, :], probs[:, c, :], start=True, stop=(c == 0))
                            if c:
                                i = pe.matmul(ps[3][:, cols], state[:, c, :], q_dec[:, cols], start=False, stop=True)
                        i.then_inc(o_done, 1)

                pipeline(pe, step)

            @block.scalar
            def _(act):
                def step(i_, b, a0, a1, a2):
                    n = 2 * i_ + b
                    if a1:
                        act.wait_ge(v_projected, n)
                        if a2:
                            wait_for(act, o_done, n - 2)
                            wait_for(act, v_dec_done, n - 2)
                        act.activation(v_rows[1 - b][:, :, :], tiled[0], ACT.Copy).then_inc(v_copied, 1)
                    if a2:
                        act.wait_ge(g_projected, n - 1)
                        wait_for(act, gated, n - 2)
                        act.activation(gate[:, :], ps[3][:, :], ACT.Silu).then_inc(g_acted, 1)
                    if a1:
                        act.wait_ge(shift_ready, n)
                        if a2:
                            act.wait_ge(k_turned, n - 1)
                            act.wait_ge(k_rows_done, n - 1)
                        for c in range(NT):
                            i = act.activation(normed[1][:, c, :], tiled[2][:, c, :], ACT.Identity,
                                               scale=rstd[:, 1, c:c + 1], bias=k_shift[:, c:c + 1])
                        i.then_inc(k_normed, 1)
                        act.wait_ge(arg_ready, n)
                        if a2:
                            act.wait_ge(probs_done, n - 1)
                            act.wait_ge(v_dec_done, n - 1)
                        for c in range(NT):
                            i = act.activation(mix[:, c, :], arg[:, c, :], ACT.Exp, bias=hcol[1 - b][:, 1, c:c + 1])
                        i.then_inc(mix_exped, 1)
                        if a2:
                            act.wait_ge(states_done, n - 1)
                            act.wait_ge(q_dec_done, n - 1)
                        act.activation(e_dec[:, :], decay[1 - b][:, :], ACT.Exp).then_inc(e_dec_done, 1)
                    if a0:
                        act.wait_ge(q_projected, n + 1)
                        act.activation(conv[0][:, :], ps[0][:, :], ACT.Identity, scale=taps[b][:, 0, TAPS - 1:TAPS],
                                       bias=taps[b][:, 0, TAPS:TAPS + 1]).then_inc(q_tapped, 1)
                    if a1:
                        act.wait_ge(q_turned, n)
                        if a2:
                            act.wait_ge(q_dec_done, n - 1)
                            act.wait_ge(scored, n - 1)
                        act.activation(q_T[:, :], ps[3][:, :], ACT.Identity, scale=norm_col[:, 0:1],
                                       bias=norm_col[:, 1:2]).then_inc(q_T_done, 1)
                        act.wait_ge(k_turned, n)
                        act.activation(k_T[:, :], ps[1][:, :], ACT.Identity, scale=norm_col[:, 2:3],
                                       bias=norm_col[:, 3:4]).then_inc(k_T_done, 1)
                    if a0:
                        act.wait_ge(k_projected, n + 1)
                        act.activation(conv[1][:, :], ps[2][:, :], ACT.Identity, scale=taps[b][:, 1, TAPS - 1:TAPS],
                                       bias=taps[b][:, 1, TAPS:TAPS + 1]).then_inc(k_tapped, 1)
                        act.wait_ge(q_conved, n + 1)
                        act.activation(conv[0][:, :], conv[0][:, :], ACT.Silu).then_inc(q_acted, 1)
                        act.wait_ge(k_conved, n + 1)
                        act.activation(conv[1][:, :], conv[1][:, :], ACT.Silu).then_inc(k_acted, 1)

                pipeline(act, step)

            @block.vector
            def _(dve):
                def convolve(n, b, m, pair, tapped, done):
                    dve.wait_ge(tapped, n + 1)
                    for j in range(TAPS - 1):
                        back = TAPS - 1 - j
                        i = dve.scalar_tensor_tensor(conv[m][:, back:T], ps[pair][:, 0:T - back], taps[b][:, m, j:j + 1],
                                                     conv[m][:, back:T], ALU.mult, ALU.add)
                        if j < TAPS - 2:
                            dve.drain()
                    i.then_inc(done, 1)

                def step(i_, b, a0, a1, a2):
                    n = 2 * i_ + b
                    if a1:
                        m = n - 1
                        if a2:
                            dve.wait_ge(mix_exped, n - 1)
                        src = cols[:, :, :, bass.ds(m, 1)].rearrange("p a c o -> p a (c o)")
                        dve.tensor_copy(hcol[1 - b][:, :, :], src)
                        dve.drain()
                        dve.wait_ge(d_loaded[1 - b], 16 * loads(i_, b, 1))
                        for c in range(NT):
                            i = dve.tensor_scalar(arg[:, c, :], decay[1 - b][:, c * P:(c + 1) * P],
                                                  hcol[1 - b][:, 0, c:c + 1], 0.0, ALU.subtract, ALU.min)
                        i.then_inc(arg_ready, 1)
                        for m, (pair, rowed) in enumerate(((1, q_rowed), (2, k_rowed))):
                            dve.wait_ge(rowed, n)
                            for c in range(NT):
                                dve.bn_stats(stats[:, m, c, :], tiled[pair][:, c, :])
                        dve.drain()
                        for m in range(2):
                            for c in range(NT):
                                dve.bn_aggr(mean_var[:, m, c, :], stats[:, m, c, :])
                        dve.drain()
                        dve.tensor_scalar(var_eps[:, :, :], mean_var[:, :, :, 1], EPS, None, ALU.add).then_inc(var_ready, 1)
                    if a2:
                        dve.wait_ge(scored, n - 1)
                        dve.wait_ge(masked, n - 1)
                        wait_for(dve, o_done, n - 2)
                        dve.tensor_tensor(probs[:, :, :], tiled[0], mix[:, :, :], ALU.mult).then_inc(probs_done, 1)
                        dve.wait_ge(kv_done, n - 1)
                        dve.wait_ge(e_dec_done, n - 1)
                        dve.tensor_copy(state[:, 1, :], tiled[3][:, 0, :])
                        for c in range(1, NT - 1):
                            dve.drain()
                            i = dve.scalar_tensor_tensor(state[:, c + 1, :], state[:, c, :],
                                                         e_dec[:, (c + 1) * P - 1:(c + 1) * P], tiled[3][:, c, :],
                                                         ALU.mult, ALU.add)
                        i.then_inc(states_done, 1)
                    if a1:
                        dve.wait_ge(rstd_ready, n)
                        dve.scalar_tensor_tensor(k_shift[:, :], mean_var[:, 1, :, 0], -1.0, rstd[:, 1, :], ALU.mult,
                                                 ALU.mult).then_inc(shift_ready, 1)
                        if a2:
                            dve.wait_ge(q_turned, n - 1)
                        for c in range(NT):
                            i = dve.tensor_scalar(normed[0][:, c, :], tiled[1][:, c, :], mean_var[:, 0, c, 0:1],
                                                  rstd[:, 0, c:c + 1], ALU.subtract, ALU.mult)
                        i.then_inc(q_normed, 1)
                    if a0:
                        convolve(n, b, 0, 0, q_tapped, q_conved)
                        convolve(n, b, 1, 2, k_tapped, k_conved)
                    if a2:
                        dve.wait_ge(o_done, n - 1)
                        dve.wait_ge(g_acted, n - 1)
                        out = gated_out[:, bass.ds(n - 2, 1), :].rearrange("p o t -> p (o t)")
                        dve.tensor_tensor(out, gate[:, :], ps[3][:, :], ALU.mult).then_inc(gated, 1)

                pipeline(dve, step)

            @block.gpsimd
            def _(pool):
                def step(i_, b, a0, a1, a2):
                    n = 2 * i_ + b
                    if a1:
                        pool.wait_ge(var_ready, n)
                        if a2:
                            pool.wait_ge(k_normed, n - 1)
                        pool.tensor_tensor(rstd[:, :, :].rearrange("p a b -> p (a b)"),
                                           var_eps[:, :, :].rearrange("p a b -> p (a b)"), neg_half[:, 0:2 * NT],
                                           ALU.pow).then_inc(rstd_ready, 1)
                        pool.wait_ge(k_normed, n)
                        if a2:
                            pool.wait_ge(kv_done, n - 1)
                        rows = [norm_row[:, j, :].rearrange("p (o d) -> p o d", o=1).to_broadcast((P, NT, HD))
                                for j in range(2)]
                        pool.tensor_tensor(k_rows[:, :, :], normed[1][:, :, :], rows[0], ALU.mult)
                        pool.drain()
                        pool.wait_ge(mix_exped, n)
                        pool.tensor_tensor(k_rows[:, :, :], k_rows[:, :, :], rows[1], ALU.add).then_inc(k_rows_done, 1)
                        pool.affine_select(out=mix[:, :, :], in_=mix[:, :, :], compare_op=ALU.is_ge, fill=0.0, base=0,
                                           pattern=[[0, NT], [1, P]], channel_multiplier=-1).then_inc(masked, 1)
                        pool.drain()
                        pool.wait_ge(v_copied, n)
                        last = mix[:, :, P - 1:P].to_broadcast((P, NT, HD))
                        pool.tensor_tensor(v_dec[:, :, :], v_rows[1 - b][:, :, :], last, ALU.mult).then_inc(v_dec_done, 1)
                        pool.wait_ge(q_T_done, n)
                        pool.wait_ge(e_dec_done, n)
                        if a2:
                            pool.wait_ge(o_done, n - 1)
                        pool.tensor_tensor(q_dec[:, :], q_T[:, :], e_dec[:, :], ALU.mult).then_inc(q_dec_done, 1)

                pipeline(pool, step)


NX = 16
FX = 176
TOP = 4
FS = 2 * FX
GX = 8
GT = GX * FX // P
NG = NX // GX
ST = -(-FS // P)
SLOTS = 4
RSLOTS = 3


def top_router_block(nc, ident, gate_weight, earlier, xT, w_dram):
    with Scope(nc, "top") as s:
        gw = s.sb("gw", [NX, D])
        gw_T = s.sb("gw_T", [P, DK, NX])
        w = s.sb("w", [P, NT, NX])
        mask = s.sb("mask", [P, NT, NX])
        total = s.sb("total", [P, NT])
        greater = s.sb("greater", [P, NT, NX, NX])
        same = s.sb("same", [P, NT, NX, NX])
        w_rows = s.sb("w_rows", [NX, T])
        ps_t = s.ps("gw_turned", [P, DK, NX])
        logits = s.ps("logits", [P, NT, NX])
        w_turned = s.ps("w_turned", [NX, T])
        loaded, gw_turned, gw_copied = s.sem("loaded"), s.sem("gw_turned"), s.sem("gw_copied")
        scored, shifted, exped, w_ready = s.sem("scored"), s.sem("shifted"), s.sem("exped"), s.sem("w_ready")
        turned, rows_ready, stored = s.sem("turned"), s.sem("rows_ready"), s.sem("stored")
        with nc.Block() as block:

            @block.sync
            def _(sp):
                sp.dma_start(gw[:, :], gate_weight).then_inc(loaded, 16)
                sp.wait_ge(rows_ready, 1)
                sp.dma_start(w_dram, w_rows[:, :]).then_inc(stored, 16)
                sp.wait_ge(stored, 16)

            @block.tensor
            def _(pe):
                pe.wait_ge(loaded, 16)
                for k in range(DK):
                    i = pe.transpose(ps_t[:, k, :], gw[:, k * P:(k + 1) * P], ident[0:NX, 0:NX])
                i.then_inc(gw_turned, 1)
                pe.wait_ge(gw_copied, 1)
                for c in range(NT):
                    for k in range(DK):
                        i = pe.matmul(logits[:, c, :], xT[:, k, c * P:(c + 1) * P], gw_T[:, k, :], start=(k == 0),
                                      stop=(k == DK - 1))
                i.then_inc(scored, 1)
                pe.wait_ge(w_ready, 1)
                for c in range(NT):
                    i = pe.transpose(w_turned[:, c * P:(c + 1) * P], w[:, c, :], ident[:, :])
                i.then_inc(turned, 1)

            @block.scalar
            def _(act):
                act.wait_ge(gw_turned, 1)
                act.activation(gw_T[:, :, :], ps_t[:, :, :], ACT.Copy).then_inc(gw_copied, 1)
                act.wait_ge(shifted, 1)
                act.activation(w[:, :, :], w[:, :, :], ACT.Exp).then_inc(exped, 1)
                act.wait_ge(turned, 1)
                act.activation(w_rows[:, :], w_turned[:, :], ACT.Copy).then_inc(rows_ready, 1)

            @block.vector
            def _(dve):
                dve.wait_ge(scored, 1)
                dve.tensor_reduce(total[:, :], logits[:, :, :], axis=AX, op=ALU.max)
                dve.drain()
                dve.tensor_tensor(w[:, :, :], logits[:, :, :], col(total[:, :], NX), ALU.subtract).then_inc(shifted, 1)
                dve.wait_ge(exped, 1)
                dve.tensor_reduce(total[:, :], w[:, :, :], axis=AX, op=ALU.add)
                dve.drain()
                dve.reciprocal(total[:, :], total[:, :])
                dve.drain()
                dve.tensor_tensor(w[:, :, :], w[:, :, :], col(total[:, :], NX), ALU.mult)
                dve.drain()
                rank_mask(dve, w[:, :, :], mask[:, :, :], greater[:, :, :, :], same[:, :, :, :], earlier, NX, TOP)
                dve.tensor_tensor(w[:, :, :], w[:, :, :], mask[:, :, :], ALU.mult).then_inc(w_ready, 1)


def glu_block(nc, tag, ident, xT, mids, down_T, base, groups, tiles, loads, routing):
    N = len(tiles)
    with Scope(nc, tag) as s:
        natural = [s.sb(f"natural{b}", [P, 2, D]) for b in range(SLOTS)]
        down = [s.sb(f"down{b}", [P, DK, P]) for b in range(SLOTS)]
        w_T = [s.sb(f"w_T{b}", [P, 2, DK, P]) for b in range(2)]
        weight = [s.sb(f"weight{b}", [P, T]) for b in range(RSLOTS)] if routing else None
        gated = [s.sb(f"gated{b}", [P, HALF]) for b in range(2)]
        hidden = [s.sb(f"hidden{b}", [P, HALF]) for b in range(2)]
        ps_w = [s.ps(f"turned_w{b}", [P, 2, DK, P]) for b in range(2)]
        ps_d = [s.ps(f"turned_d{b}", [P, HALF]) for b in range(2)]
        ps_g = [s.ps(f"gate{b}", [P, HALF]) for b in range(2)]
        ps_u = [s.ps(f"up{b}", [P, HALF]) for b in range(2)]
        loaded = [s.sem(f"loaded{b}") for b in range(SLOTS)]
        r_loaded = [s.sem(f"r_loaded{b}") for b in range(RSLOTS)]
        w_turned, w_copied = s.sem("w_turned"), s.sem("w_copied")
        d_turned, d_copied = s.sem("d_turned"), s.sem("d_copied")
        gate_done, up_done = s.sem("gate_done"), s.sem("up_done")
        gate_taken, up_taken, weighted = s.sem("gate_taken"), s.sem("up_taken"), s.sem("weighted")

        def dmas(source, slots):
            parts = [list(source(0, n)) for n in range(N)]
            per_group = [16 * sum(len(parts[n]) for n in range(N) if n % slots == b) for b in range(slots)]
            upto = [16 * sum(len(parts[m]) for m in range(n + 1) if m % slots == n % slots) for n in range(N)]
            return per_group, upto

        def last_user(n, slots):
            return slots if n >= slots else n + N - max(m for m in range(N) if m % slots == n % slots)

        w_group, w_upto = dmas(loads, SLOTS)
        if routing:
            r_group, r_upto = dmas(routing, RSLOTS)

        def over_groups(eng, body):
            body(0, True)
            if groups > 1:
                with eng.Fori(1, groups) as g:
                    body(g, False)

        with nc.Block() as block:

            @block.sync
            def _(sp):
                def group(g, first):
                    for n in range(N):
                        at = g * N + n
                        back = last_user(n, SLOTS)
                        if not first or n >= SLOTS:
                            sp.wait_ge(w_turned, at - back + 1)
                            sp.wait_ge(d_turned, at - back + 1)
                        for what, rows, src in loads(g, n):
                            dst = {"gate": natural[n % SLOTS][rows, 0, :], "up": natural[n % SLOTS][rows, 1, :],
                                   "down": down[n % SLOTS][:, :, rows]}[what]
                            sp.dma_start(dst, src).then_inc(loaded[n % SLOTS], 16)
                        if routing:
                            if not first or n >= RSLOTS:
                                sp.wait_ge(weighted, 2 * (at - last_user(n, RSLOTS) + 1))
                            for _, rows, src in routing(g, n):
                                sp.dma_start(weight[n % RSLOTS][rows, :], src).then_inc(r_loaded[n % RSLOTS], 16)

                over_groups(sp, group)

            @block.tensor
            def _(pe):
                def turn(g, n, first):
                    at = g * N + n
                    rows = tiles[n]
                    pe.wait_ge(loaded[n % SLOTS], w_group[n % SLOTS] * g + w_upto[n])
                    if not first or n >= 2:
                        pe.wait_ge(w_copied, at - last_user(n, 2) + 1)
                    for m in range(2):
                        for k in range(DK):
                            i = pe.transpose(ps_w[n % 2][:, m, k, 0:rows], natural[n % SLOTS][0:rows, m, k * P:(k + 1) * P],
                                             ident[0:rows, 0:rows])
                    i.then_inc(w_turned, 1)
                    if not first or n >= 2:
                        pe.wait_ge(d_copied, at - last_user(n, 2) + 1)
                    for k in range(DK):
                        i = pe.transpose(ps_d[n % 2][0:rows, k * P:(k + 1) * P], down[n % SLOTS][:, k, 0:rows], ident[:, :])
                    i.then_inc(d_turned, 1)

                def group(g, first):
                    turn(g, 0, first)
                    for n in range(N):
                        at = g * N + n
                        if n + 1 < N:
                            turn(g, n + 1, first)
                        pe.wait_ge(w_copied, at + 1)
                        for half in range(2):
                            cols = slice(half * HALF, (half + 1) * HALF)
                            for m, (ps, taken, done) in enumerate(((ps_g, gate_taken, gate_done), (ps_u, up_taken, up_done))):
                                if not first or n:
                                    pe.wait_ge(taken, 2 * at + half - 1)
                                for k in range(DK):
                                    i = pe.matmul(ps[half][0:tiles[n], :], w_T[n % 2][:, m, k, 0:tiles[n]], xT[:, k, cols],
                                                  start=(k == 0), stop=(k == DK - 1))
                                i.then_inc(done, 1)

                over_groups(pe, group)

            @block.scalar
            def _(act):
                def copy(g, n, first):
                    at, rows = g * N + n, tiles[n]
                    act.wait_ge(w_turned, at + 1)
                    if not first or n >= 2:
                        act.wait_ge(up_done, 2 * (at - last_user(n, 2) + 1))
                    act.activation(w_T[n % 2][:, :, :, 0:rows], ps_w[n % 2][:, :, :, 0:rows], ACT.Copy).then_inc(w_copied, 1)

                def group(g, first):
                    copy(g, 0, first)
                    for n in range(N):
                        at, rows = g * N + n, tiles[n]
                        if n + 1 < N:
                            copy(g, n + 1, first)
                        for half in range(2):
                            if not first or n:
                                act.wait_ge(up_taken, 2 * at + half - 1)
                            act.wait_ge(gate_done, 2 * at + half + 1)
                            act.activation(gated[half][0:rows, :], ps_g[half][0:rows, :], ACT.Silu).then_inc(gate_taken, 1)

                over_groups(act, group)

            @block.vector
            def _(dve):
                def group(g, first):
                    for n in range(N):
                        at, rows = g * N + n, tiles[n]
                        dve.wait_ge(d_turned, at + 1)
                        dve.tensor_copy(down_T[0:rows, bass.ds(base + at, 1), :].rearrange("p o d -> p (o d)"),
                                        ps_d[n % 2][0:rows, 0:D]).then_inc(d_copied, 1)
                        for half in range(2):
                            cols = slice(half * HALF, (half + 1) * HALF)
                            if routing:
                                if not first or n:
                                    dve.wait_ge(weighted, 2 * at + half - 1)
                                out = hidden[half][0:rows, :]
                            else:
                                out = mids[0:rows, base + at, cols]
                            dve.wait_ge(gate_taken, 2 * at + half + 1)
                            dve.wait_ge(up_done, 2 * at + half + 1)
                            dve.tensor_tensor(out, gated[half][0:rows, :], ps_u[half][0:rows, :], ALU.mult)\
                                .then_inc(up_taken, 1)

                over_groups(dve, group)

            @block.gpsimd
            def _(pool):
                if not routing:
                    return

                def group(g, first):
                    for n in range(N):
                        at, rows = g * N + n, tiles[n]
                        pool.wait_ge(r_loaded[n % RSLOTS], r_group[n % RSLOTS] * g + r_upto[n])
                        for half in range(2):
                            cols = slice(half * HALF, (half + 1) * HALF)
                            pool.wait_ge(up_taken, 2 * at + half + 1)
                            out = mids[0:rows, bass.ds(base + at, 1), cols].rearrange("p o t -> p (o t)")
                            pool.tensor_tensor(out, hidden[half][0:rows, :], weight[n % RSLOTS][0:rows, cols], ALU.mult)\
                                .then_inc(weighted, 1)

                over_groups(pool, group)


def routed_tiles(gate_up, down_w, w_dram):
    gu = gate_up.rearrange("(g e) (m f) d -> g e m f d", e=GX, m=2)
    dw = down_w.rearrange("(g e) (k p) f -> g e p k f", e=GX, p=P)
    rw = w_dram.rearrange("(g e) t -> g e t", e=GX)

    def pieces(n):
        at = n * P
        while at < (n + 1) * P:
            e, r = divmod(at, FX)
            k = min(FX - r, (n + 1) * P - at)
            yield e, r, k, slice(at - n * P, at - n * P + k)
            at += k

    def loads(g, n):
        for e, r, k, rows in pieces(n):
            for m, what in enumerate(("gate", "up")):
                yield what, rows, gu[bass.ds(g, 1), e, m, r:r + k, :].rearrange("o f d -> (o f) d")
            yield "down", rows, dw[bass.ds(g, 1), e, :, :, r:r + k].rearrange("o p k f -> (o p) k f")

    def routing(g, n):
        for e, r, k, rows in pieces(n):
            yield "weight", rows, rw[bass.ds(g, 1), e, :].to_broadcast((k, T))

    return loads, routing


def shared_tiles(gate_up, down_w):
    gu = gate_up.rearrange("(m f) d -> m f d", m=2)
    dw = down_w.rearrange("(k p) f -> p k f", p=P)

    def loads(g, n):
        k = min(P, FS - n * P)
        for m, what in enumerate(("gate", "up")):
            yield what, slice(0, k), gu[m, n * P:n * P + k, :]
        yield "down", slice(0, k), dw[:, :, n * P:n * P + k]

    return loads


def load_block(nc, tag, pairs):
    with Scope(nc, tag) as s:
        loaded = s.sem("loaded")
        with nc.Block() as block:

            @block.sync
            def _(sp):
                for dst, src in pairs:
                    sp.dma_start(dst, src).then_inc(loaded, 16)
                sp.wait_ge(loaded, 16 * len(pairs))


def network(nc, a, rope_table, earlier_table, out):
    Scope.used.clear()
    gold_w = nc.dram_tensor("gold_weights", [NE, T], F32, kind="Internal").ap()
    decay_sums = nc.dram_tensor("decay_sums", [LH, T], F32, kind="Internal").ap()
    top_w = nc.dram_tensor("top_weights", [NX, T], F32, kind="Internal").ap()

    def row(ap):
        return ap.rearrange("(o n) -> o n", o=1).to_broadcast((P, ap.shape[0]))

    def column(ap):
        return ap.rearrange("(n o) -> n o", o=1)

    def by_tiles(ap):
        return ap.rearrange("(k p) n -> p k n", p=P)

    with Scope(nc, "net") as net:
        ident, identb = net.sb("ident", [P, P]), net.sb("identb", [P, P], BF16)
        neg_half = net.sb("neg_half", [P, 2 * NT])
        x = net.sb("x", [P, NT, D])
        xn = net.sb("xn", [P, NT, D])
        xT = net.sb("xT", [P, DK, T])
        earlier = net.sb("earlier", [P, NX, NX])
        norm_row = net.sb("norm_row", [P, 2, HD])
        norm_col = net.sb("norm_col", [P, 4])
        inner_wb = net.sb("inner_wb", [P, 2, DK])
        w_out = net.sb("w_out", [P, DK, D])
        rope = net.sb("rope", [P, NT, 2, ROT // 2])
        load_constants(nc, [
            (x[:, :, :], by_tiles(a["L0_attn_X"][0])),
            (inner_wb[:, 0, :], a["L0_attn_ln_w"].rearrange("(k p) -> p k", p=P)),
            (inner_wb[:, 1, :], a["L0_attn_ln_b"].rearrange("(k p) -> p k", p=P)),
            (rope[:, :, :, :], rope_table),
            (w_out[:, :, :], by_tiles(a["L0_attn_W_out"])),
            (earlier[:, :, :], earlier_table.to_broadcast((P, NX * NX)).rearrange("p (a b) -> p a b", a=NX)),
            (norm_row[:, 0, :], row(a["L1_attn_kn_w"])), (norm_row[:, 1, :], row(a["L1_attn_kn_b"])),
            (norm_col[:, 0:1], column(a["L1_attn_qn_w"])), (norm_col[:, 1:2], column(a["L1_attn_qn_b"])),
            (norm_col[:, 2:3], column(a["L1_attn_kn_w"])), (norm_col[:, 3:4], column(a["L1_attn_kn_b"])),
        ], ident, identb, neg_half)

        with Scope(nc, "s0") as s:
            context = s.sb("context", [P, NT, D])
            with Scope(nc, "s0a") as t:
                norm_block(nc, "norm0", ident, neg_half, x, normed=xn, normed_T=xT, inner=context, inner_wb=inner_wb)
                w_in = t.sb("w_in", [P, DK, 3 * D])
                qk = t.sb("qk", [P, NT, 2 * D])
                v = t.sb("v", [P, NT, NH, VW])
                k_stack = t.sb("k_stack", [P, NH, T], BF16)
                qkv_block(nc, a["L0_attn_W_in"], xT, w_in, rope, qk, v, k_stack)
                attention_block(nc, ident, identb, qk, v, k_stack, context)
            turn_block(nc, "turn0", ident, context, xT)
            down_block(nc, "out0", [(xT[:, k, :], w_out[:, k, :]) for k in range(DK)], context, add=xn)
            norm_block(nc, "norm1", ident, neg_half, x, y=context, normed=xn, normed_T=xT)

        with Scope(nc, "s1") as s:
            golden_router_block(nc, ident, a["L0_ffn_Wr"], a["L0_ffn_temperature"], earlier[:, 0:NE, 0:NE], xT, gold_w)
            mids = s.sb("mids", [P, NE * FK, T])
            w_down = s.sb("w_down", [P, NE, FK, D])
            rings = [[s.sb(f"ring{m}{b}", [P, DK, FE]) for b in range(2)] for m in range(2)]
            Wg, Wu, Wd = (a[f"L0_ffn_W{m}"] for m in "gud")
            low_rank_block(nc, ident, [(a[f"L0_ffn_{m}a"], a[f"L0_ffn_{m}b"]) for m in "GUD"], rings, w_down, Wg, Wu, Wd)
            experts_block(nc, rings, xT, gold_w, Wg, Wu, mids)
            down_block(nc, "out1", [(mids[:, k, :], w_down[:, k // FK, k % FK, :]) for k in range(NE * FK)], xn)
            norm_block(nc, "norm2", ident, neg_half, x, y=xn, normed=xn, normed_T=xT)

        clear_semaphores(nc)

        with Scope(nc, "s2") as s:
            gated = s.sb("gated", [P, LH, T])
            with Scope(nc, "s2a") as t:
                cols = t.sb("cols", [P, 2, NT, LH])
                decay_block(nc, ident, a["L1_attn_Wb"], a["L1_attn_bb"], xT, decay_sums, cols)
                w = {m: a[f"L1_attn_W{n}"] for m, n in (("q", "q"), ("k", "k"), ("v", "v"), ("gate", "g"))}
                w.update({f"{m}_taps": (a[f"L1_attn_{m}conv_w"], a[f"L1_attn_{m}conv_b"]) for m in "qk"})
                linear_attention_block(nc, ident, neg_half, w, xT, decay_sums, cols, norm_row, norm_col, gated)
            w_o = s.sb("w_o", [P, LH, D])
            load_block(nc, "load2", [(w_o[:, :, :], by_tiles(a["L1_attn_Wo"]))])
            down_block(nc, "out2", [(gated[:, k, :], w_o[:, k, :]) for k in range(LH)], xn)
            norm_block(nc, "norm3", ident, neg_half, x, y=xn, normed=xn, normed_T=xT)

        with Scope(nc, "s3") as s:
            top_router_block(nc, ident, a["L1_ffn_gate_weight"], earlier[:, :, :], xT, top_w)
            n = NG * GT + ST
            mids = s.sb("mids", [P, n, T])
            down_T = s.sb("down_T", [P, n, D])
            rows = [P] * (n - 1) + [FS - (ST - 1) * P]
            loads, routing = routed_tiles(a["L1_ffn_gate_up_weights"], a["L1_ffn_down_weights"], top_w)
            glu_block(nc, "routed", ident, xT, mids, down_T, 0, NG, rows[0:GT], loads, routing)
            loads = shared_tiles(a["L1_ffn_shared_gate_up"], a["L1_ffn_shared_down"])
            glu_block(nc, "shared", ident, xT, mids, down_T, NG * GT, 1, rows[NG * GT:], loads, None)
            down_block(nc, "out3", [(mids[0:rows[k], k, :], down_T[0:rows[k], k, :]) for k in range(n)], xn)
            norm_block(nc, "norm4", ident, neg_half, x, y=xn, store=out[0])


_INS = [
    "L0_attn_X", "L0_attn_ln_w", "L0_attn_ln_b", "L0_attn_W_in", "L0_attn_W_out",
    "L0_ffn_Wg", "L0_ffn_Wu", "L0_ffn_Wd", "L0_ffn_Ga", "L0_ffn_Gb", "L0_ffn_Ua", "L0_ffn_Ub", "L0_ffn_Da",
    "L0_ffn_Db", "L0_ffn_Wr", "L0_ffn_temperature",
    "L1_attn_Wq", "L1_attn_Wk", "L1_attn_Wv", "L1_attn_Wb", "L1_attn_bb", "L1_attn_Wg", "L1_attn_Wo",
    "L1_attn_qconv_w", "L1_attn_qconv_b", "L1_attn_kconv_w", "L1_attn_kconv_b",
    "L1_attn_qn_w", "L1_attn_qn_b", "L1_attn_kn_w", "L1_attn_kn_b",
    "L1_ffn_gate_weight", "L1_ffn_gate_up_weights", "L1_ffn_down_weights", "L1_ffn_shared_gate_up",
    "L1_ffn_shared_down",
]


def rope_constants():
    inverse = (1.0 / np.float32(10000.0) ** (np.arange(0, ROT, 2, dtype=np.float32) / ROT)).astype(np.float32)
    angle = np.arange(T, dtype=np.float32)[:, None] * inverse[None, :]
    table = np.stack([np.cos(angle), np.sin(angle)], axis=1).astype(np.float32)
    return np.ascontiguousarray(table.reshape(NT, P, 2, ROT // 2).transpose(1, 0, 2, 3))


def kernel(**inputs):
    import concourse.bacc as bacc
    from concourse.bass_utils import run_bass_kernel_spmd

    nc = bacc.Bacc("TRN2", target_bir_lowering=False, num_devices=1)
    arrays = {f"in_{name}": np.ascontiguousarray(inputs[name]) for name in _INS}
    arrays["rope_table"] = rope_constants()
    arrays["earlier_table"] = np.tril(np.ones((NX, NX), np.float32), -1).reshape(1, NX * NX)
    aps = {name: nc.dram_tensor(name, v.shape, mybir.dt.from_np(v.dtype), kind="ExternalInput").ap()
           for name, v in arrays.items()}
    out = nc.dram_tensor("out_0", (1, T, D), F32, kind="ExternalOutput").ap()
    network(nc, {name: aps[f"in_{name}"] for name in _INS}, aps["rope_table"], aps["earlier_table"], out)
    r = run_bass_kernel_spmd(nc, [arrays], core_ids=[0])
    return r.results[0]["out_0"]
```

```python
import math
from contextlib import ExitStack

import numpy as np
import concourse.bass as bass
import concourse.mybir as mybir

F32 = mybir.dt.float32
F32R = mybir.dt.float32r
BF16 = mybir.dt.bfloat16
ALU = mybir.AluOpType
ACT = mybir.ActivationFunctionType
AX = mybir.AxisListType.X

P = 128
T = 1024
NT = T // P
D = 256
DK = D // P
HALF = 512
EPS = 1e-5


class Scope:

    used = []

    def __init__(self, nc, tag):
        self.nc, self.tag, self.ctx = nc, tag, ExitStack()

    def __enter__(self):
        self.ctx.__enter__()
        return self

    def __exit__(self, *a):
        return self.ctx.__exit__(*a)

    def sb(self, name, shape, dt=F32):
        return self.ctx.enter_context(self.nc.sbuf_tensor(f"{self.tag}_{name}", shape, dt))

    def ps(self, name, shape, dt=F32):
        return self.ctx.enter_context(self.nc.psum_tensor(f"{self.tag}_{name}", shape, dt))

    def sem(self, name):
        handle = self.ctx.enter_context(self.nc.semaphore(f"{self.tag}_{name}"))
        Scope.used.append(handle.num)
        return handle


def clear_semaphores(nc):
    with nc.Block() as block:

        @block.gpsimd
        def _(pool):
            pool.sem_clear(range(min(Scope.used), max(Scope.used) + 1))

    Scope.used.clear()


def col(ap, n):
    p, a = ap.shape
    return ap.rearrange("p (a o) -> p a o", o=1).to_broadcast((p, a, n))


def load_constants(nc, consts, ident, identb, neg_half):
    with Scope(nc, "const") as s:
        zeroed, loaded = s.sem("zeroed"), s.sem("loaded")
        with nc.Block() as block:

            @block.gpsimd
            def _(pool):
                pool.memset(ident[:, :], 0.0)
                pool.memset(identb[:, :], 0.0)
                pool.memset(neg_half[:, :], -0.5).then_inc(zeroed, 1)
                pool.wait_ge(zeroed, 1)
                pool.drain()
                for m in (ident, identb):
                    pool.affine_select(out=m[:, :], in_=m[:, :], compare_op=ALU.not_equal, fill=1.0,
                                       base=0, pattern=[[-1, P]], channel_multiplier=1)

            @block.sync
            def _(sp):
                for n, (dst, src) in enumerate(consts):
                    sp.dma_start(dst, src, allow_slow_non_contiguous=True).then_inc(loaded, 16)
                sp.wait_ge(loaded, 16 * len(consts))


def norm_block(nc, tag, ident, neg_half, x, y=None, normed=None, normed_T=None, inner=None, inner_wb=None,
               store=None):
    with Scope(nc, tag) as s:
        stats = s.sb("stats", [P, NT, 6])
        mean_var = s.sb("mean_var", [P, NT, 2])
        var_eps = s.sb("var_eps", [P, NT])
        rstd = s.sb("rstd", [P, NT])
        turned = [s.ps(f"turned{k}", [P, T]) for k in range(DK)]
        var_ready, rstd_ready, tile_ready = s.sem("var_ready"), s.sem("rstd_ready"), s.sem("tile_ready")
        x_ready, stored = s.sem("x_ready"), s.sem("stored")
        turn_done, evacuated = s.sem("turn_done"), s.sem("evacuated")
        chain = []
        if y is not None:
            chain.append((y, y))
        if normed is not None:
            chain.append((x, normed))
        if inner is not None:
            chain.append((normed, inner))
        last = chain[-1][1]
        with nc.Block() as block:

            @block.vector
            def _(dve):
                for k, (src, dst) in enumerate(chain):
                    for c in range(NT):
                        dve.bn_stats(stats[:, c, :], src[:, c, :])
                    dve.drain()
                    for c in range(NT):
                        dve.bn_aggr(mean_var[:, c, :], stats[:, c, :])
                    dve.drain()
                    dve.tensor_scalar(var_eps[:, :], mean_var[:, :, 1], EPS, None, ALU.add).then_inc(var_ready, 1)
                    dve.wait_ge(rstd_ready, k + 1)
                    for c in range(NT):
                        i = dve.tensor_scalar(dst[:, c, :], src[:, c, :], mean_var[:, c, 0:1], rstd[:, c:c + 1],
                                              ALU.subtract, ALU.mult)
                        if k == len(chain) - 1 and normed_T is not None:
                            i.then_inc(tile_ready, 1)
                    dve.drain()
                    if y is not None and k == 0:
                        for c in range(NT):
                            dve.tensor_tensor(x[:, c, :], x[:, c, :], y[:, c, :], ALU.add).then_inc(x_ready, 1)
                        dve.drain()

            @block.gpsimd
            def _(pool):
                for k in range(len(chain)):
                    pool.wait_ge(var_ready, k + 1)
                    pool.tensor_tensor(rstd[:, :], var_eps[:, :], neg_half[:, 0:NT], ALU.pow).then_inc(rstd_ready, 1)

            @block.tensor
            def _(pe):
                if normed_T is None:
                    return
                for c in range(NT):
                    pe.wait_ge(tile_ready, c + 1)
                    for k in range(DK):
                        i = pe.transpose(turned[k][:, c * P:(c + 1) * P], last[:, c, k * P:(k + 1) * P], ident[:, :])
                    if c % 4 == 3:
                        i.then_inc(turn_done, 1)

            @block.scalar
            def _(act):
                if normed_T is None:
                    return
                for h in range(2):
                    act.wait_ge(turn_done, h + 1)
                    for k in range(DK):
                        cols = slice(h * HALF, (h + 1) * HALF)
                        if inner_wb is None:
                            act.activation(normed_T[:, k, cols], turned[k][:, cols], ACT.Identity)
                        else:
                            act.activation(normed_T[:, k, cols], turned[k][:, cols], ACT.Identity,
                                           scale=inner_wb[:, 0, k:k + 1], bias=inner_wb[:, 1, k:k + 1])

            @block.sync
            def _(sp):
                if store is None:
                    return
                for c in range(NT):
                    sp.wait_ge(x_ready, c + 1)
                    sp.dma_start(store[c * P:(c + 1) * P, :], x[:, c, :]).then_inc(stored, 16)
                sp.wait_ge(stored, 16 * NT)


def matmul3(pe, out, w, x, start, stop):
    pe.matmul(out, w[0], x[0], start=start, stop=False)
    pe.matmul(out, w[0], x[1], start=False, stop=False)
    return pe.matmul(out, w[1], x[0], start=False, stop=stop)


def split_small(dve, parts, src):
    dve.tensor_copy(parts[0], src)
    dve.drain()
    return dve.tensor_tensor(parts[1], src, parts[0].bitcast(F32), ALU.subtract)


class NormTail:

    JOBS = 4

    def __init__(self, s, ident, neg_half, x, acc, parts=None, xT=None, add=None, store=None):
        self.ident, self.neg_half, self.x, self.acc = ident, neg_half, x, acc
        self.parts, self.xT, self.add, self.store = parts, xT, add, store
        self.norms = 1 if parts is None else 2
        self.y = s.sb("y", [P, NT, D])
        self.stats = s.sb("tail_stats", [P, NT, 6])
        self.mean_var = s.sb("tail_mean_var", [P, NT, 2])
        self.var_eps = s.sb("tail_var_eps", [P, NT])
        self.rstd = s.sb("tail_rstd", [P, NT])
        (self.var_ready, self.rstd_ready, self.x_ready, self.xn_ready, self.x_turned, self.high_done,
         self.stored) = (s.sem(name) for name in (
             "var_ready", "rstd_ready", "x_ready", "xn_ready", "x_turned", "high_done", "stored"))
        if parts is not None:
            self.xn = s.sb("xn", [P, NT, D])
            self.turned = [s.ps(f"x_turned{j}", [P, DK, 2 * P]) for j in range(self.JOBS)]
        self.events = []

    def pe_x(self, pe, j):
        if self.parts is None:
            return
        pe.wait_ge(self.xn_ready, j + 1)
        for c in range(2):
            for k in range(DK):
                i = pe.transpose(self.turned[j][:, k, c * P:(c + 1) * P], self.xn[:, 2 * j + c, k * P:(k + 1) * P],
                                 self.ident[:, :])
        i.then_inc(self.x_turned, 1)

    def act_x(self, act, j):
        if self.parts is None:
            return
        act.wait_ge(self.x_turned, j + 1)
        cols = slice(2 * j * P, (2 * j + 2) * P)
        if self.xT is not None:
            act.activation(self.xT[:, :, cols], self.turned[j][:, :, :], ACT.Copy)
        act.activation(self.parts[0][:, :, cols], self.turned[j][:, :, :], ACT.Copy).then_inc(self.high_done, 1)

    def variances(self, dve, j, src):
        tiles = range(2 * j, 2 * j + 2)
        for c in tiles:
            dve.bn_stats(self.stats[:, c, :], src(c))
        dve.drain()
        for c in tiles:
            dve.bn_aggr(self.mean_var[:, c, :], self.stats[:, c, :])
        dve.drain()
        dve.tensor_scalar(self.var_eps[:, 2 * j:2 * j + 2], self.mean_var[:, 2 * j:2 * j + 2, 1], EPS, None, ALU.add)\
            .then_inc(self.var_ready, 1)
        self.events.append(j)

    def normalise(self, dve, j, event, src, dst):
        dve.wait_ge(self.rstd_ready, event + 1)
        for c in range(2 * j, 2 * j + 2):
            i = dve.tensor_scalar(dst(c), src(c), self.mean_var[:, c, 0:1], self.rstd[:, c:c + 1], ALU.subtract, ALU.mult)
        return i

    def dve_jobs(self, dve, jobs, summed, count):
        both = {j: slice(2 * j, 2 * j + 2) for j in jobs}
        at = len(self.events)
        y_tile = lambda c: self.y[:, c, :]
        sums = y_tile if self.add is not None else lambda c: self.acc[c // 4][:, c % 4, :]
        for j in jobs:
            dve.wait_ge(summed, count(j))
            if self.add is not None:
                dve.tensor_tensor(self.y[:, both[j], :], self.acc[j // 2][:, 2 * (j % 2):2 * (j % 2) + 2, :],
                                  self.add[:, both[j], :], ALU.add)
                dve.drain()
            self.variances(dve, j, sums)
        for n, j in enumerate(jobs):
            self.normalise(dve, j, at + n, sums, y_tile)
            dve.drain()
            dve.tensor_tensor(self.x[:, both[j], :], self.x[:, both[j], :], self.y[:, both[j], :], ALU.add)\
                .then_inc(self.x_ready, 1)
            if self.parts is not None:
                dve.drain()
                self.variances(dve, j, lambda c: self.x[:, c, :])
        if self.parts is None:
            return
        for n, j in enumerate(jobs):
            self.normalise(dve, j, at + len(jobs) + n, lambda c: self.x[:, c, :], lambda c: self.xn[:, c, :])\
                .then_inc(self.xn_ready, 1)
        for j in jobs:
            dve.wait_ge(self.high_done, j + 1)
            cols = slice(2 * j * P, (2 * j + 2) * P)
            dve.tensor_tensor(self.parts[1][:, :, cols], self.turned[j][:, :, :], self.parts[0][:, :, cols].bitcast(F32),
                              ALU.subtract)

    def pool_norm(self, pool, event):
        j = self.order[event]
        pool.wait_ge(self.var_ready, event + 1)
        pool.tensor_tensor(self.rstd[:, 2 * j:2 * j + 2], self.var_eps[:, 2 * j:2 * j + 2], self.neg_half[:, 0:2], ALU.pow)\
            .then_inc(self.rstd_ready, 1)

    def plan(self, groups):
        self.order = [j for jobs in groups for _ in range(self.norms) for j in jobs]

    def sp_all(self, sp):
        if self.store is None:
            return
        rows = self.store.rearrange("(c p) d -> p c d", p=P)
        for j in range(self.JOBS):
            sp.wait_ge(self.x_ready, j + 1)
            sp.dma_start(rows[:, 2 * j:2 * j + 2, :], self.x[:, 2 * j:2 * j + 2, :]).then_inc(self.stored, 16)
        sp.wait_ge(self.stored, 16 * self.JOBS)


def down_norm_block(nc, tag, ident, neg_half, x, sources, w_down=None, w_parts=None, load=None, **tail):
    with Scope(nc, tag) as s:
        n_src = len(sources)
        long = n_src > 8
        split_w = w_parts is None
        if split_w:
            w_parts = [s.sb(f"w_part{b}", [P, n_src, D], F32R) for b in range(2)]
        ring = 3
        parts = [[s.sb(f"part{m}{b}", [P, HALF], F32R) for m in range(2)] for b in range(ring)]
        acc = [s.ps(f"acc{h}", [P, 4, D]) for h in range(2)]
        loaded, w_high, w_ready = s.sem("loaded"), s.sem("w_high"), s.sem("w_ready")
        high, low, used = s.sem("high"), [s.sem(f"low{h}") for h in range(2)], s.sem("used")
        t = NormTail(s, ident, neg_half, x, acc, **tail)
        groups = [(0, 1), (2, 3)] if long else [(0, 1, 2, 3)]
        t.plan(groups)
        units = [(h, n) for h in range(2) for n in range(n_src)]
        rows = [q.shape[0] for q in sources]
        chunks = [slice(n, min(n + 4, n_src)) for n in range(0, n_src, 4)]
        pool_at = {1: 0, 2: 1, 6: 2, 7: 3} if t.norms == 2 else {1: 0, 2: 1}
        pe_at, act_at = {10: 0, 11: 1}, {12: 0, 13: 1}
        with nc.Block() as block:

            @block.sync
            def _(sp):
                if load is not None:
                    sp.dma_start(*load).then_inc(loaded, 16)
                t.sp_all(sp)

            @block.tensor
            def _(pe):
                for u, (h, n) in enumerate(units):
                    pe.wait_ge(low[h], n + 1)
                    if split_w and h == 0 and n % 4 == 0:
                        pe.wait_ge(w_ready, n // 4 + 1)
                    for c in range(4):
                        i = matmul3(pe, acc[h][:, c, :], [q[0:rows[n], c * P:(c + 1) * P] for q in parts[u % ring]],
                                    [w[0:rows[n], n, :] for w in w_parts],
                                    n == 0 and c % 2 == 0, n == n_src - 1 and c % 2 == 1)
                    i.then_inc(used, 1)
                    if long and h == 1 and n in pe_at:
                        t.pe_x(pe, pe_at[n])
                for j in range(2 if long else 0, 4):
                    t.pe_x(pe, j)

            @block.scalar
            def _(act):
                if load is not None:
                    act.wait_ge(loaded, 16)
                for u, (h, n) in enumerate(units):
                    if split_w and h == 0 and n % 4 == 0:
                        c, r = chunks[n // 4], rows[n]
                        act.activation(w_parts[0][0:r, c, :], w_down[0:r, c, :], ACT.Copy).then_inc(w_high, 1)
                    if u >= ring:
                        act.wait_ge(used, u - ring + 1)
                    act.activation(parts[u % ring][0][0:rows[n], :], sources[n][:, h * HALF:(h + 1) * HALF], ACT.Copy)\
                        .then_inc(high, 1)
                    if long and h == 1 and n in act_at:
                        t.act_x(act, act_at[n])
                for j in range(2 if long else 0, 4):
                    t.act_x(act, j)

            def low_part(eng, u):
                h, n = units[u]
                q = parts[u % ring]
                eng.wait_ge(high, u + 1)
                eng.tensor_tensor(q[1][0:rows[n], :], sources[n][:, h * HALF:(h + 1) * HALF],
                                  q[0][0:rows[n], :].bitcast(F32), ALU.subtract).then_inc(low[h], 1)

            @block.vector
            def _(dve):
                for u, (h, n) in enumerate(units):
                    if split_w and h == 0 and n % 4 == 0:
                        c, r = chunks[n // 4], rows[n]
                        dve.wait_ge(w_high, n // 4 + 1)
                        dve.tensor_tensor(w_parts[1][0:r, c, :], w_down[0:r, c, :], w_parts[0][0:r, c, :].bitcast(F32),
                                          ALU.subtract).then_inc(w_ready, 1)
                    if h == 0 or not long:
                        low_part(dve, u)
                for jobs in groups:
                    t.dve_jobs(dve, jobs, used, lambda j: n_src * (j // 2 + 1))

            @block.gpsimd
            def _(pool):
                done = 0
                if long:
                    for n in range(n_src):
                        low_part(pool, n_src + n)
                        if n in pool_at:
                            t.pool_norm(pool, done)
                            done += 1
                for e in range(done, len(t.order)):
                    t.pool_norm(pool, e)


NH, DH = 16, 16
ROT = DH // 2
TERMS = 6
QROWS = TERMS * DH
PB = 8
MROWS = 3
GH = 4
VW = 32


def qkv_block(nc, W_in, xT, w_in, rope, qk, v, k_stack):
    with Scope(nc, "qkv") as s:
        pq = [s.ps(f"qk{b}", [P, HALF]) for b in range(2)]
        pv = [s.ps(f"v{b}", [P, HALF]) for b in range(2)]
        prod = [s.sb(f"prod{b}", [P, 2 * NH, 4]) for b in range(4)]
        projected, taken, v_ones, w_loaded = s.sem("projected"), s.sem("taken"), s.sem("v_ones"), s.sem("w_loaded")
        copied = s.sem("copied")
        with nc.Block() as block:

            @block.sync
            def _(sp):
                sp.dma_start(w_in[:, :, :], W_in.rearrange("(k p) n -> p k n", p=P)).then_inc(w_loaded, 16)

            @block.tensor
            def _(pe):
                pe.wait_ge(w_loaded, 16)
                for c in range(NT):
                    if c >= 2:
                        pe.wait_ge(taken, c - 1)
                    for out, cols in ((pq[c % 2][:, :], slice(0, 2 * D)), (pv[c % 2][:, 0:D], slice(2 * D, 3 * D))):
                        for k in range(DK):
                            i = pe.matmul(out, xT[:, k, c * P:(c + 1) * P], w_in[:, k, cols], start=(k == 0),
                                          stop=(k == DK - 1))
                    i.then_inc(projected, 1)

            @block.scalar
            def _(act):
                act.wait_ge(v_ones, 1)
                for c in range(NT):
                    act.wait_ge(projected, c + 1)
                    act.activation(qk[:, c, 0:D], pq[c % 2][:, 0:D], ACT.Copy, scale=DH ** -0.5)
                    act.activation(qk[:, c, D:2 * D], pq[c % 2][:, D:2 * D], ACT.Copy).then_inc(copied, 1)
                    act.activation(v[:, c, :, 0:DH], pv[c % 2][:, 0:D].rearrange("p (h d) -> p h d", h=NH),
                                   ACT.Copy).then_inc(taken, 1)

            @block.gpsimd
            def _(pool):
                minus_ones = float(np.uint32(0xBF80BF80).view(np.float32))
                pool.memset(k_stack[QROWS:P, :, :].rearrange("p a b -> p (a b)").bitcast(F32), minus_ones)

            @block.vector
            def _(dve):
                dve.memset(v[:, :, :, :].rearrange("p a b c -> p (a b c)"), 0.0)
                dve.drain()
                dve.memset(v[:, :, :, DH:DH + 1].rearrange("p a b c -> p (a b) c"), 1.0).then_inc(v_ones, 1)
                for c in range(NT):
                    dve.wait_ge(copied, c + 1)
                    dve.drain()
                    pairs = qk[:, c, :].rearrange("p (h j e) -> p h j e", h=2 * NH, e=2)
                    x1, x2 = pairs[:, :, 0:ROT // 2, 0], pairs[:, :, 0:ROT // 2, 1]

                    def table(n):
                        return rope[:, c, n, :].rearrange("p (o j) -> p o j", o=1).to_broadcast((P, 2 * NH, ROT // 2))

                    cos, sin = table(0), table(1)
                    dve.tensor_tensor(prod[0][:, :, :], x1, cos, ALU.mult)
                    dve.tensor_tensor(prod[1][:, :, :], x2, sin, ALU.mult)
                    dve.tensor_tensor(prod[2][:, :, :], x2, cos, ALU.mult)
                    dve.tensor_tensor(prod[3][:, :, :], x1, sin, ALU.mult)
                    dve.drain()
                    dve.tensor_tensor(x1, prod[0][:, :, :], prod[1][:, :, :], ALU.subtract)
                    dve.tensor_tensor(x2, prod[2][:, :, :], prod[3][:, :, :], ALU.add)


def attention_block(nc, ident, identb, qk, v, k_stack, ctx_out):
    with Scope(nc, "attn") as s:
        q_tok = [s.sb(f"q_tok{b}", [P, NT, TERMS, DH], BF16) for b in range(2)]
        k_tok = [s.sb(f"k_tok{b}", [P, NT, TERMS, DH], BF16) for b in range(2)]
        rest = s.sb("rest", [P, NT, DH])
        q_stack = s.sb("q_stack", [P, NH, T], BF16)
        v_group = [s.sb(f"v_group{b}", [P, NT, GH, VW]) for b in range(2)]
        row_max = s.sb("row_max", [P, NT, 2])
        whole_max = s.sb("whole_max", [P, NT])
        max_rest = s.sb("max_rest", [P, NT])
        max_tok = s.sb("max_tok", [P, NT, MROWS], BF16)
        probs = s.sb("probs", [P, PB, T])
        ctx_T = s.sb("ctx_T", [P, T])
        inv = s.sb("inv", [P, 4, GH])
        ps_q = [s.ps(f"rows_q{b}", [P, HALF]) for b in range(2)]
        ps_k = [s.ps(f"rows_k{b}", [P, HALF]) for b in range(3)]
        ps_ctx = [s.ps(f"ctx{b}", [P, HALF]) for b in range(2)]
        ps_turn = s.ps("turn", [P, HALF])
        turn_b = ps_turn[:, :].bitcast(BF16)
        split_q, split_k = s.sem("split_q"), s.sem("split_k")
        q_turned, k_turned = s.sem("q_turned"), s.sem("k_turned")
        q_stacked, k_stacked = s.sem("q_stacked"), s.sem("k_stacked")
        scored_q, maxed = s.sem("scored_q"), s.sem("maxed")
        max_split, max_turned, max_stacked = s.sem("max_split"), s.sem("max_turned"), s.sem("max_stacked")
        scored_k, exped = s.sem("scored_k"), s.sem("exped")
        v_ready, summed, ctx_copied = s.sem("v_ready"), s.sem("summed"), s.sem("ctx_copied")
        ctx_turned, ctx_done = s.sem("ctx_turned"), s.sem("ctx_done")
        NG = NH // GH

        U_MAX, U_Q, U_K = 2, 4, 6

        with nc.Block() as block:

            @block.gpsimd
            def _(pool):
                one = dict(scalar1=1.0, scalar2=0.0, op0=ALU.mult, op1=ALU.add)

                def split(src, tok, places, done):
                    high, middle, low = places

                    def put(part, x):
                        for a, n, step in part:
                            dst = tok[:, :, a:a + (n - 1) * step + 1:step, :]
                            pool.tensor_scalar(dst, x.rearrange("p t (o d) -> p t o d", o=1).to_broadcast((P, NT, n, DH)),
                                               **one)
                        pool.drain()

                    put(high, src)
                    pool.tensor_tensor(rest[:, :, :], src, tok[:, :, high[0][0], :], ALU.subtract)
                    pool.drain()
                    put(middle, rest[:, :, :])
                    pool.tensor_tensor(rest[:, :, :], rest[:, :, :], tok[:, :, middle[0][0], :], ALU.subtract)
                    pool.drain()
                    (a, n, step), = low
                    pool.tensor_scalar(tok[:, :, a, :], rest[:, :, :], **one).then_inc(done, 1)
                    pool.drain()

                for h in range(NH):
                    b = h % 2
                    if h >= 2:
                        pool.wait_ge(q_turned, h - 1)
                        pool.wait_ge(k_turned, h - 1)
                    split(qk[:, :, h * DH:(h + 1) * DH], q_tok[b], ([(0, 2, 1), (5, 1, 1)], [(2, 2, 1)], [(4, 1, 1)]),
                          split_q)
                    split(qk[:, :, D + h * DH:D + (h + 1) * DH], k_tok[b], ([(0, 3, 2)], [(1, 2, 2)], [(5, 1, 1)]),
                          split_k)

            def slots():
                for n in range(NH + GH):
                    yield n, (n if n < NH else None), (n // GH - 1 if n >= GH else None), 2 * (n % GH)

            def weighed_at(unit):
                for n in range(max(0, unit - 6), unit - 3):
                    late = {0: 6, 1: 5, 2: 5}.get(n % (NT * GH), 4)
                    if n == unit - late:
                        yield n // (NT * GH), n // GH % NT, n % GH

            @block.tensor
            def _(pe):
                def turn_q(h):
                    pe.wait_ge(split_q, h + 1)
                    if h == 1:
                        pe.wait_ge(k_stacked, 1)
                    elif h > 1:
                        pe.wait_ge(max_stacked, h - 1)
                    for c in range(NT):
                        i = pe.transpose(turn_b[0:QROWS, c * P:(c + 1) * P],
                                         q_tok[h % 2][:, c, :, :].rearrange("p a b -> p (a b)"), identb[:, :])
                    i.then_inc(q_turned, 1)

                def turn_k(h):
                    pe.wait_ge(split_k, h + 1)
                    pe.wait_ge(q_stacked, h + 1)
                    for c in range(NT):
                        i = pe.transpose(turn_b[0:QROWS, c * P:(c + 1) * P],
                                         k_tok[h % 2][:, c, :, :].rearrange("p a b -> p (a b)"), identb[:, :])
                    i.then_inc(k_turned, 1)

                def turn_max(h):
                    pe.wait_ge(max_split, h + 1)
                    pe.wait_ge(k_stacked, min(h + 2, NH))
                    if h % GH == 0 and h >= 2 * GH:
                        pe.wait_ge(ctx_done, 2 * (h // GH - 1))
                    for c in range(NT):
                        i = pe.transpose(turn_b[0:MROWS, c * P:(c + 1) * P], max_tok[:, c, :], identb[:, :])
                    i.then_inc(max_turned, 1)

                def score_rows_q(h, r):
                    if r == 0:
                        pe.wait_ge(q_stacked, h + 1)
                        pe.wait_ge(k_stacked, h + 1)
                    for b in range(2):
                        n = 2 * (NT * h + r) + b
                        if n >= 2:
                            pe.wait_ge(maxed, n - 1)
                        pe.matmul(ps_q[b][:, :], q_stack[0:QROWS, h, r * P:(r + 1) * P],
                                  k_stack[0:QROWS, h, b * HALF:(b + 1) * HALF], start=True, stop=True)\
                            .then_inc(scored_q, 1)

                def score_rows_k(g, t, j):
                    h = g * GH + j
                    if t == 0:
                        pe.wait_ge(max_stacked, h + 1)
                    for b in range(2):
                        n = 2 * (g * NT * GH + t * GH + j) + b
                        if n >= 3:
                            pe.wait_ge(exped, n - 2)
                        pe.matmul(ps_k[n % 3][:, :], k_stack[0:QROWS + MROWS, h, t * P:(t + 1) * P],
                                  q_stack[0:QROWS + MROWS, h, b * HALF:(b + 1) * HALF], start=True, stop=True)\
                            .then_inc(scored_k, 1)

                def weigh(g, t, j):
                    pe.wait_ge(exped, 2 * (GH * (g * NT + t) + j + 1))
                    if t == 0 and j == 0:
                        pe.wait_ge(v_ready, g + 1)
                        if g >= 1:
                            pe.wait_ge(ctx_copied, g)
                    for b in range(2):
                        i = pe.matmul(ps_ctx[b][j * VW:(j + 1) * VW, :], v_group[g % 2][:, t, j, :],
                                      probs[:, (GH * (g * NT + t) + j) % PB, b * HALF:(b + 1) * HALF],
                                      start=(t == 0), stop=(t == NT - 1))
                    i.then_inc(summed, 1)

                def turn_ctx(g, half):
                    if half == 1:
                        pe.wait_ge(ctx_done, 2 * g + 1)
                    else:
                        pe.wait_ge(ctx_copied, g + 1)
                        if g < NG - 2:
                            pe.wait_ge(k_stacked, GH * (g + 2) + 2)
                        else:
                            pe.wait_ge(max_stacked, NH)
                            if g == NG - 1:
                                pe.wait_ge(ctx_done, 2 * g)
                    for c in range(4):
                        cc = 4 * half + c
                        i = pe.transpose(ps_turn[:, c * P:(c + 1) * P], ctx_T[:, cc * P:(cc + 1) * P], ident[:, :])
                    i.then_inc(ctx_turned, 1)

                turn_q(0)
                turn_k(0)
                for n, head, g, t0 in slots():
                    for u in range(NT):
                        if u == U_MAX and 1 <= n <= NH:
                            turn_max(n - 1)
                        if head is not None:
                            if u == U_Q and head + 1 < NH:
                                turn_q(head + 1)
                            if u == U_K and head + 1 < NH:
                                turn_k(head + 1)
                            score_rows_q(head, u)
                        if g is not None:
                            score_rows_k(g, t0 + u // GH, u % GH)
                            for piece in weighed_at(NT * (n - GH) + u):
                                weigh(*piece)
                        if u == 0 and n > 2 * GH and n % GH == 1:
                            turn_ctx(g - 1, 1)
                    if g is not None and g > 0 and n % GH == 0:
                        turn_ctx(g - 1, 0)
                for unit in range(NT * NH, NT * NH + 4):
                    for piece in weighed_at(unit):
                        weigh(*piece)
                turn_ctx(NG - 1, 0)
                turn_ctx(NG - 1, 1)

            @block.scalar
            def _(act):
                def stack_q(h):
                    act.wait_ge(q_turned, h + 1)
                    act.activation(q_stack[0:QROWS, h, :], turn_b[0:QROWS, :], ACT.Copy).then_inc(q_stacked, 1)

                def stack_k(h):
                    act.wait_ge(k_turned, h + 1)
                    act.activation(k_stack[0:QROWS, h, :], turn_b[0:QROWS, :], ACT.Copy).then_inc(k_stacked, 1)

                def stack_max(h):
                    act.wait_ge(max_turned, h + 1)
                    act.activation(q_stack[QROWS:QROWS + MROWS, h, :], turn_b[0:MROWS, :], ACT.Copy)\
                        .then_inc(max_stacked, 1)

                def copy_ctx(g):
                    act.wait_ge(summed, NT * GH * (g + 1))
                    if g >= 1:
                        act.wait_ge(ctx_turned, 2 * g)
                    for b in range(2):
                        i = act.activation(ctx_T[:, b * HALF:(b + 1) * HALF], ps_ctx[b][:, :], ACT.Copy)
                    i.then_inc(ctx_copied, 1)

                def exp(g, t, j):
                    for b in range(2):
                        n = 2 * (g * NT * GH + t * GH + j) + b
                        if b == 0 and n // 2 >= PB:
                            act.wait_ge(summed, n // 2 - PB + 1)
                        act.wait_ge(scored_k, n + 1)
                        act.activation(probs[:, (GH * (g * NT + t) + j) % PB, b * HALF:(b + 1) * HALF], ps_k[n % 3][:, :],
                                       ACT.Exp).then_inc(exped, 1)

                stack_q(0)
                stack_k(0)
                for n, head, g, t0 in slots():
                    for u in range(NT):
                        if u == U_MAX and 1 <= n <= NH:
                            stack_max(n - 1)
                        if head is not None and head + 1 < NH:
                            if u == U_Q:
                                stack_q(head + 1)
                            if u == U_K:
                                stack_k(head + 1)
                        if g is not None and g > 0 and u == GH and n % GH == 0:
                            copy_ctx(g - 1)
                        if g is not None:
                            exp(g, t0 + u // GH, u % GH)
                copy_ctx(NG - 1)

            @block.vector
            def _(dve):
                def row_maxima(h, r):
                    for b in range(2):
                        n = 2 * (NT * h + r) + b
                        dve.wait_ge(scored_q, n + 1)
                        dve.tensor_reduce(row_max[:, r, b:b + 1], ps_q[b][:, :], axis=AX, op=ALU.max)\
                            .then_inc(maxed, 1)

                def split_maxima(h):
                    dve.drain()
                    if h >= 1:
                        dve.wait_ge(max_turned, h)
                    dve.tensor_tensor(whole_max[:, :], row_max[:, :, 0], row_max[:, :, 1], ALU.max)
                    dve.drain()
                    dve.tensor_copy(max_tok[:, :, 0], whole_max[:, :])
                    dve.drain()
                    dve.tensor_tensor(max_rest[:, :], whole_max[:, :], max_tok[:, :, 0], ALU.subtract)
                    dve.drain()
                    dve.tensor_copy(max_tok[:, :, 1], max_rest[:, :])
                    dve.drain()
                    dve.tensor_tensor(max_tok[:, :, 2], max_rest[:, :], max_tok[:, :, 1], ALU.subtract)\
                        .then_inc(max_split, 1)

                def values(g):
                    if g >= 2:
                        dve.wait_ge(summed, NT * GH * (g - 1))
                    dve.tensor_copy(v_group[g % 2][:, :, :, :], v[:, :, g * GH:(g + 1) * GH, :]).then_inc(v_ready, 1)

                def norm_ctx(g, half):
                    dve.wait_ge(ctx_turned, 2 * g + half + 1)
                    view = ps_turn[:, :].rearrange("p (c j w) -> p c j w", c=4, j=GH)
                    dve.reciprocal(inv[:, :, :], view[:, :, :, DH])
                    dve.drain()
                    for c in range(4):
                        out = ctx_out[:, 4 * half + c, g * GH * DH:(g + 1) * GH * DH].rearrange(
                            "p (j d) -> p j d", j=GH)
                        i = dve.tensor_tensor(out, view[:, c, :, 0:DH], col(inv[:, c, :], DH), ALU.mult)
                    i.then_inc(ctx_done, 1)

                values(0)
                values(1)
                for n, head, g, t0 in slots():
                    for u in range(NT):
                        if head is not None:
                            row_maxima(head, u)
                        if u == 0 and n > 2 * GH and n % GH == 1:
                            norm_ctx(g - 1, 1)
                            if g + 1 < NG:
                                values(g + 1)
                    if head is not None:
                        split_maxima(head)
                    if g is not None and g > 0 and n % GH == 0:
                        norm_ctx(g - 1, 0)
                norm_ctx(NG - 1, 0)
                norm_ctx(NG - 1, 1)


def turn_block(nc, tag, ident, src, dst):
    with Scope(nc, tag) as s:
        turned = [s.ps(f"turned{k}", [P, T]) for k in range(DK)]
        turn_done = s.sem("turn_done")
        with nc.Block() as block:

            @block.tensor
            def _(pe):
                for h in range(2):
                    for c in range(4 * h, 4 * h + 4):
                        for k in range(DK):
                            i = pe.transpose(turned[k][:, c * P:(c + 1) * P], src[:, c, k * P:(k + 1) * P], ident[:, :])
                    i.then_inc(turn_done, 1)

            @block.scalar
            def _(act):
                for h in range(2):
                    act.wait_ge(turn_done, h + 1)
                    for k in range(DK):
                        act.activation(dst[:, k, h * HALF:(h + 1) * HALF], turned[k][:, h * HALF:(h + 1) * HALF],
                                       ACT.Copy)


NE = 8
FE = 256
FK = FE // P
NL, RANK = 2, 64
CENTER = 1.0 / math.e
LOWER = 0.5 - math.log(4.0 / 3.0)
Z_LOWER = math.log(LOWER / (1.0 - LOWER))
Z_UPPER = 2.0 ** -23


def rank_mask(dve, scores, mask, greater, same, earlier, n, top):
    a = scores.shape[1]
    other = scores.rearrange("p a (o j) -> p a o j", o=1).to_broadcast((P, a, n, n))
    own = scores.rearrange("p a (i o) -> p a i o", o=1).to_broadcast((P, a, n, n))
    dve.tensor_tensor(greater, other, own, ALU.is_gt)
    dve.tensor_tensor(same, other, own, ALU.is_equal)
    dve.drain()
    dve.tensor_tensor(same, same, earlier.rearrange("p (o i) j -> p o i j", o=1).to_broadcast((P, a, n, n)), ALU.mult)
    dve.drain()
    dve.tensor_tensor(greater, greater, same, ALU.add)
    dve.drain()
    dve.tensor_reduce(mask, greater, axis=AX, op=ALU.add)
    dve.drain()
    dve.tensor_scalar(mask, mask, float(top), None, ALU.is_lt)
    dve.drain()


def golden_router_block(nc, ident, Wr, temperature, earlier, x_parts, w_dram):
    with Scope(nc, "gold") as s:
        wr = s.sb("wr", [P, DK, NE])
        temp = s.sb("temp", [P, 1])
        wr_parts = [s.sb(f"wr_part{q}", [P, DK, NE], F32R) for q in range(2)]
        wr_split = s.sem("wr_split")
        inv_temp = s.sb("inv_temp", [P, 1])
        z = s.sb("z", [P, NT, NE])
        ez = s.sb("ez", [P, NT, NE])
        dist = s.sb("dist", [P, NT, NE])
        w = s.sb("w", [P, NT, NE])
        fb = s.sb("fb", [P, NT, NE])
        zone = s.sb("zone", [P, NT, NE])
        mask = s.sb("mask", [P, NT, NE])
        total = s.sb("total", [P, NT])
        none = s.sb("none", [P, NT])
        greater = s.sb("greater", [P, NT, NE, NE])
        same = s.sb("same", [P, NT, NE, NE])
        w_rows = s.sb("w_rows", [NE, T])
        logits = s.ps("logits", [P, NT, NE])
        w_turned = s.ps("w_turned", [NE, T])
        loaded, scored, z_ready, e_ready = s.sem("loaded"), s.sem("scored"), s.sem("z_ready"), s.sem("e_ready")
        d_ready, f_ready, w_ready = s.sem("d_ready"), s.sem("f_ready"), s.sem("w_ready")
        turned, rows_ready, stored = s.sem("turned"), s.sem("rows_ready"), s.sem("stored")
        flat = "p a b -> p (a b)"
        with nc.Block() as block:

            @block.sync
            def _(sp):
                sp.dma_start(wr[:, :, :], Wr.rearrange("(k p) n -> p k n", p=P)).then_inc(loaded, 16)
                sp.dma_start(temp[:, :], temperature.rearrange("(o n) -> o n", o=1).to_broadcast((P, 1)))\
                    .then_inc(loaded, 16)
                sp.wait_ge(rows_ready, 1)
                sp.dma_start(w_dram, w_rows[:, :]).then_inc(stored, 16)
                sp.wait_ge(stored, 16)

            @block.tensor
            def _(pe):
                pe.wait_ge(wr_split, 1)
                for c in range(NT):
                    for k in range(DK):
                        i = matmul3(pe, logits[:, c, :], [q[:, k, c * P:(c + 1) * P] for q in x_parts],
                                    [q[:, k, :] for q in wr_parts], k == 0, k == DK - 1)
                i.then_inc(scored, 1)
                pe.wait_ge(w_ready, 1)
                for c in range(NT):
                    i = pe.transpose(w_turned[:, c * P:(c + 1) * P], w[:, c, :], ident[:, :])
                i.then_inc(turned, 1)

            @block.scalar
            def _(act):
                act.wait_ge(z_ready, 1)
                act.activation(ez[:, :, :], z[:, :, :], ACT.Exp, scale=-1.0).then_inc(e_ready, 1)
                act.wait_ge(d_ready, 1)
                act.activation(w[:, :, :], dist[:, :, :], ACT.Exp, scale=-1.0 / 0.1)
                act.activation(fb[:, :, :], dist[:, :, :], ACT.Exp, scale=-1.0 / 0.3).then_inc(f_ready, 1)
                act.wait_ge(turned, 1)
                act.activation(w_rows[:, :], w_turned[:, :], ACT.Copy).then_inc(rows_ready, 1)

            @block.vector
            def _(dve):
                dve.wait_ge(loaded, 32)
                split_small(dve, [q[:, :, :] for q in wr_parts], wr[:, :, :]).then_inc(wr_split, 1)
                dve.reciprocal(inv_temp[:, :], temp[:, :])
                dve.wait_ge(scored, 1)
                dve.drain()
                dve.tensor_scalar(z[:, :, :], logits[:, :, :], inv_temp[:, 0:1], -80.0, ALU.mult, ALU.max).then_inc(z_ready, 1)
                dve.drain()
                dve.tensor_scalar(zone[:, :, :], z[:, :, :], Z_LOWER, None, ALU.is_ge)
                dve.tensor_scalar(mask[:, :, :], z[:, :, :], Z_UPPER, None, ALU.is_le)
                dve.drain()
                dve.tensor_tensor(zone[:, :, :], zone[:, :, :], mask[:, :, :], ALU.mult)
                dve.wait_ge(e_ready, 1)
                dve.tensor_scalar(ez[:, :, :], ez[:, :, :], 1.0, None, ALU.add)
                dve.drain()
                dve.reciprocal(ez[:, :, :].rearrange(flat), ez[:, :, :].rearrange(flat))
                dve.drain()
                dve.tensor_scalar(ez[:, :, :], ez[:, :, :], CENTER, None, ALU.subtract)
                dve.drain()
                dve.tensor_scalar(dist[:, :, :], ez[:, :, :], -1.0, None, ALU.mult)
                dve.drain()
                dve.tensor_tensor(dist[:, :, :], dist[:, :, :], ez[:, :, :], ALU.max).then_inc(d_ready, 1)
                dve.wait_ge(f_ready, 1)
                dve.tensor_tensor(w[:, :, :], w[:, :, :], zone[:, :, :], ALU.mult)
                dve.drain()
                dve.tensor_reduce(total[:, :], w[:, :, :], axis=AX, op=ALU.add)
                dve.drain()
                dve.tensor_scalar(none[:, :], total[:, :], 1e-8, None, ALU.is_lt)
                rank_mask(dve, fb[:, :, :], mask[:, :, :], greater[:, :, :, :], same[:, :, :, :], earlier, NE, 2)

                def normalise(a):
                    dve.tensor_reduce(total[:, :], a, axis=AX, op=ALU.add)
                    dve.drain()
                    dve.tensor_scalar(total[:, :], total[:, :], 1e-8, None, ALU.max)
                    dve.drain()
                    dve.reciprocal(total[:, :], total[:, :])
                    dve.drain()
                    return dve.tensor_tensor(a, a, col(total[:, :], NE), ALU.mult)

                dve.tensor_tensor(fb[:, :, :], fb[:, :, :], mask[:, :, :], ALU.mult)
                dve.drain()
                normalise(fb[:, :, :])
                dve.drain()
                dve.tensor_tensor(fb[:, :, :], fb[:, :, :], w[:, :, :], ALU.subtract)
                dve.drain()
                dve.tensor_tensor(fb[:, :, :], fb[:, :, :], col(none[:, :], NE), ALU.mult)
                dve.drain()
                dve.tensor_tensor(w[:, :, :], w[:, :, :], fb[:, :, :], ALU.add)
                dve.drain()
                normalise(w[:, :, :]).then_inc(w_ready, 1)


def low_rank_block(nc, ident, lora, rings, w_down, Wg, Wu, Wd):
    with Scope(nc, "lora") as s:
        a_sb = s.sb("a", [P, 3, NL, FK, RANK])
        b_sb = s.sb("b", [RANK, 3, NL, FE])
        a_T = s.sb("a_T", [RANK, 3, NL, FK, P])
        ps_t = [s.ps(f"turned{b}", [RANK, FK, P]) for b in range(2)]
        ps_w = [s.ps(f"product{b}", [P, FK, FE]) for b in range(2)]
        loaded, turned, copied = s.sem("loaded"), s.sem("turned"), s.sem("copied")
        producted, added = s.sem("producted"), s.sem("added")
        jobs = [(m, e) for e in range(NL) for m in range(3)]
        with nc.Block() as block:

            @block.sync
            def _(sp):
                n = 0
                for m, (A, B) in enumerate(lora):
                    for e in range(NL):
                        sp.dma_start(a_sb[:, m, e, :, :], A[e].rearrange("(k p) r -> p k r", p=P)).then_inc(loaded, 16)
                        sp.dma_start(b_sb[:, m, e, :], B[e]).then_inc(loaded, 16)
                        n += 2
                for e in range(NL):
                    for r, W in zip(rings, (Wg, Wu)):
                        sp.dma_start(r[e][:, :, :], W[e].rearrange("(k p) f -> p k f", p=P)).then_inc(loaded, 16)
                        n += 1
                sp.dma_start(w_down[:, :, :].rearrange("p (e k) d -> p e k d", e=NE), Wd.rearrange("e (k p) d -> p e k d", p=P)).then_inc(loaded, 16)
                assert n + 1 == 17

            @block.tensor
            def _(pe):
                pe.wait_ge(loaded, 16 * 17)
                for n, (m, e) in enumerate(jobs):
                    if n >= 2:
                        pe.wait_ge(copied, n - 1)
                    for k in range(FK):
                        i = pe.transpose(ps_t[n % 2][:, k, :], a_sb[:, m, e, k, :], ident[:, :])
                    i.then_inc(turned, 1)
                    pe.wait_ge(copied, n + 1)
                    if n >= 2:
                        pe.wait_ge(added, n - 1)
                    for k in range(FK):
                        i = pe.matmul(ps_w[n % 2][:, k, :], a_T[:, m, e, k, :], b_sb[:, m, e, :], start=True, stop=True)
                    i.then_inc(producted, 1)

            @block.scalar
            def _(act):
                for n, (m, e) in enumerate(jobs):
                    act.wait_ge(turned, n + 1)
                    act.activation(a_T[:, m, e, :, :], ps_t[n % 2][:, :, :], ACT.Copy).then_inc(copied, 1)

            @block.vector
            def _(dve):
                for n, (m, e) in enumerate(jobs):
                    dve.wait_ge(producted, n + 1)
                    dst = rings[m][e][:, :, :] if m < 2 else w_down[:, FK * e:FK * e + FK, :]
                    dve.tensor_tensor(dst, dst, ps_w[n % 2][:, :, :], ALU.add).then_inc(added, 1)


def experts_block(nc, rings, x_parts, w_dram, Wg, Wu, mids):
    with Scope(nc, "moe0") as s:
        w_parts = [[[s.sb(f"w_part{m}{b}{q}", [P, DK, FE], F32R) for q in range(2)] for b in range(2)] for m in range(2)]
        weight = [s.sb(f"weight{b}", [P, T]) for b in range(2)]
        gated = [s.sb(f"gated{b}", [P, HALF]) for b in range(2)]
        hidden = [s.sb(f"hidden{b}", [P, HALF]) for b in range(2)]
        ps_g = [s.ps(f"gate{b}", [P, HALF]) for b in range(2)]
        ps_u = [s.ps(f"up{b}", [P, HALF]) for b in range(2)]
        w_loaded = [s.sem(f"w_loaded{b}") for b in range(2)]
        r_loaded = [s.sem(f"r_loaded{b}") for b in range(2)]
        w_high, w_split = s.sem("w_high"), s.sem("w_split")
        gate_done, up_done = s.sem("gate_done"), s.sem("up_done")
        gate_free, up_free = s.sem("gate_free"), s.sem("up_free")
        hidden_free = s.sem("hidden_free")
        U = 2 * FK

        def over_experts(eng, expert):
            expert(0, 0, 0)
            with eng.Fori(0, NE // 2 - 1) as i:
                expert(2 * i + 1, i, 1)
                expert(2 * i + 2, i + 1, 0)
            expert(NE - 1, NE // 2 - 1, 1)

        def is_first(e):
            return isinstance(e, int) and e == 0

        def is_last(e):
            return isinstance(e, int) and e == NE - 1

        with nc.Block() as block:

            @block.sync
            def _(sp):
                for b in range(2):
                    sp.dma_start(weight[b][:, :], w_dram[b:b + 1, :].to_broadcast((P, T))).then_inc(r_loaded[b], 16)
                with sp.Fori(0, NE // 2 - 1) as i:
                    for b in range(2):
                        sp.wait_ge(w_split, 2 * i + b + 1)
                        for r, W in zip(rings, (Wg, Wu)):
                            src = W[bass.ds(2 * i + b + 2, 1), :, :].rearrange("o (k p) f -> p (o k) f", p=P)
                            sp.dma_start(r[b][:, :, :], src).then_inc(w_loaded[b], 16)
                        sp.wait_ge(hidden_free, U * (2 * i + b + 1))
                        sp.dma_start(weight[b][:, :], w_dram[bass.ds(2 * i + b + 2, 1), :].to_broadcast((P, T)))\
                            .then_inc(r_loaded[b], 16)

            @block.tensor
            def _(pe):
                def expert(e, pair, b):
                    pe.wait_ge(w_split, e + 1)
                    for u in range(U):
                        f, half = divmod(u, 2)
                        for m, ps, free, done in ((0, ps_g, gate_free, gate_done), (1, ps_u, up_free, up_done)):
                            if not (is_first(e) and u < 2):
                                pe.wait_ge(free, U * e + u - 1)
                            for k in range(DK):
                                i = matmul3(pe, ps[u % 2][:, :], [w[:, k, f * P:(f + 1) * P] for w in w_parts[m][b]],
                                            [q[:, k, half * HALF:(half + 1) * HALF] for q in x_parts],
                                            k == 0, k == DK - 1)
                            i.then_inc(done, 1)

                over_experts(pe, expert)

            @block.scalar
            def _(act):
                def high(b):
                    for m in range(2):
                        i = act.activation(w_parts[m][b][0][:, :, :], rings[m][b][:, :, :], ACT.Copy)
                    i.then_inc(w_high, 1)

                def expert(e, pair, b):
                    if is_first(e):
                        high(0)
                        high(1)
                    elif not is_last(e):
                        act.wait_ge(w_loaded[1 - b], 32 * (pair + b))
                        act.wait_ge(up_done, U * e)
                        high(1 - b)
                    for u in range(U):
                        if not (is_first(e) and u < 2):
                            act.wait_ge(up_free, U * e + u - 1)
                        act.wait_ge(gate_done, U * e + u + 1)
                        act.activation(gated[u % 2][:, :], ps_g[u % 2][:, :], ACT.Silu).then_inc(gate_free, 1)

                over_experts(act, expert)

            @block.vector
            def _(dve):
                def low(e, b):
                    dve.wait_ge(w_high, e + 1)
                    for m in range(2):
                        i = dve.tensor_tensor(w_parts[m][b][1][:, :, :], rings[m][b][:, :, :],
                                              w_parts[m][b][0][:, :, :].bitcast(F32), ALU.subtract)
                    i.then_inc(w_split, 1)

                def expert(e, pair, b):
                    if is_first(e):
                        low(0, 0)
                        low(1, 1)
                    elif not is_last(e):
                        low(e + 1, 1 - b)
                    for u in range(U):
                        if not (is_first(e) and u < 2):
                            dve.wait_ge(hidden_free, U * e + u - 1)
                        dve.wait_ge(gate_free, U * e + u + 1)
                        dve.wait_ge(up_done, U * e + u + 1)
                        dve.tensor_tensor(hidden[u % 2][:, :], gated[u % 2][:, :], ps_u[u % 2][:, :], ALU.mult)\
                            .then_inc(up_free, 1)

                over_experts(dve, expert)

            @block.gpsimd
            def _(pool):
                def expert(e, pair, b):
                    pool.wait_ge(r_loaded[b], 16 * pair + 16)
                    for u in range(U):
                        f, half = divmod(u, 2)
                        pool.wait_ge(up_free, U * e + u + 1)
                        cols = slice(half * HALF, (half + 1) * HALF)
                        out = mids[:, bass.ds(FK * e + f, 1), cols].rearrange("p o t -> p (o t)")
                        pool.tensor_tensor(out, hidden[u % 2][:, :], weight[b][:, cols], ALU.mult).then_inc(hidden_free, 1)

                over_experts(pool, expert)


LH = 16
HD = 128
TAPS = 4


def decay_block(nc, ident, Wb, bb, x_parts, decay_dram, cols):
    with Scope(nc, "decay") as s:
        wb = s.sb("wb", [P, DK, LH])
        wb_parts = [s.sb(f"wb_part{q}", [P, DK, LH], F32R) for q in range(2)]
        wb_split = s.sem("wb_split")
        bias = s.sb("bias", [LH, 1])
        z = s.sb("z", [LH, T])
        soft = s.sb("soft", [LH, T])
        log_b = s.sb("log_b", [LH, T])
        total = s.sb("total", [LH, T])
        one = s.sb("one", [LH, T])
        ps_z = s.ps("z_sum", [LH, T])
        ps_c = s.ps("turned", [P, 2, NT, LH])
        loaded, z_done, z_ready = s.sem("loaded"), s.sem("z_done"), s.sem("z_ready")
        soft_ready, sums_ready = s.sem("soft_ready"), s.sem("sums_ready")
        turned, stored, acts, one_ready = s.sem("turned"), s.sem("stored"), s.sem("acts"), s.sem("one_ready")
        with nc.Block() as block:

            @block.sync
            def _(sp):
                sp.dma_start(wb[:, :, :], Wb.rearrange("(k p) h -> p k h", p=P)).then_inc(loaded, 16)
                sp.dma_start(bias[:, :], bb.rearrange("(h o) -> h o", o=1)).then_inc(loaded, 16)
                sp.wait_ge(sums_ready, 1)
                sp.dma_start(decay_dram, total[:, :]).then_inc(stored, 16)
                sp.wait_ge(stored, 16)

            @block.tensor
            def _(pe):
                pe.wait_ge(wb_split, 1)
                for half in range(2):
                    for k in range(DK):
                        i = matmul3(pe, ps_z[:, half * HALF:(half + 1) * HALF], [q[:, k, :] for q in wb_parts],
                                    [q[:, k, half * HALF:(half + 1) * HALF] for q in x_parts], k == 0, k == DK - 1)
                i.then_inc(z_done, 1)
                pe.wait_ge(sums_ready, 1)
                for n, src in enumerate((total, log_b)):
                    for c in range(NT):
                        i = pe.transpose(ps_c[:, n, c, :], src[:, c * P:(c + 1) * P], ident[0:LH, 0:LH])
                i.then_inc(turned, 1)

            @block.scalar
            def _(act):
                act.wait_ge(loaded, 32)
                act.wait_ge(z_done, 1)
                act.activation(z[:, :], ps_z[:, :], ACT.Identity, bias=bias[:, 0:1]).then_inc(z_ready, 1)
                act.wait_ge(z_ready, 1)
                act.activation(soft[:, :], z[:, :], ACT.Abs).then_inc(acts, 1)
                act.wait_ge(acts, 1)
                act.activation(soft[:, :], soft[:, :], ACT.Exp, scale=-1.0).then_inc(acts, 1)
                act.wait_ge(acts, 2)
                act.wait_ge(one_ready, 1)
                act.activation(soft[:, :], soft[:, :], ACT.Ln, bias=one[:, 0:1]).then_inc(soft_ready, 1)

            @block.vector
            def _(dve):
                dve.memset(one[:, :], 1.0).then_inc(one_ready, 1)
                dve.wait_ge(loaded, 32)
                split_small(dve, [q[:, :, :] for q in wb_parts], wb[:, :, :]).then_inc(wb_split, 1)
                dve.wait_ge(z_ready, 1)
                dve.tensor_scalar(log_b[:, :], z[:, :], 0.0, None, ALU.min)
                dve.wait_ge(soft_ready, 1)
                dve.drain()
                dve.tensor_tensor(log_b[:, :], log_b[:, :], soft[:, :], ALU.subtract)
                dve.drain()
                dve.tensor_tensor(z[:, :], log_b[:, :], z[:, :], ALU.subtract)
                dve.drain()
                for c in range(NT):
                    i = dve.tensor_tensor_scan(total[:, c * P:(c + 1) * P], one[:, 0:P], z[:, c * P:(c + 1) * P], 0.0,
                                               ALU.mult, ALU.add)
                i.then_inc(sums_ready, 1)
                dve.wait_ge(turned, 1)
                dve.tensor_copy(cols[:, :, :, :], ps_c[:, :, :, :])


def linear_attention_block(nc, ident, neg_half, w, xT, x_parts, decay_dram, cols, norm_row, norm_col, gated_out):
    with Scope(nc, "lin") as s:
        Wq, Wk, Wv, Wg = w["q"], w["k"], w["v"], w["gate"]
        wq, wk, wv, wg = ([s.sb(f"w_{m}{b}", [P, DK, HD]) for b in range(2)] for m in ("q", "k", "v", "gate"))
        parts = {m: [s.sb(f"part_{m}{p}", [P, DK, HD], F32R) for p in range(2)] for m in ("q", "k", "gate")}
        taps = [s.sb(f"taps{b}", [P, 2, TAPS + 1]) for b in range(2)]
        decay = [s.sb(f"decay{b}", [P, T]) for b in range(2)]
        hcol = [s.sb(f"hcol{b}", [P, 2, NT]) for b in range(2)]
        conv = [s.sb(f"conv_{m}", [P, T]) for m in "qk"]
        stats = s.sb("stats", [P, 2, NT, 6])
        mean_var = s.sb("mean_var", [P, 2, NT, 2])
        var_eps = s.sb("var_eps", [P, 2, NT])
        rstd = s.sb("rstd", [P, 2, NT])
        k_shift = s.sb("k_shift", [P, NT])
        normed = [s.sb(f"normed_{m}", [P, NT, HD]) for m in "qk"]
        k_rows = s.sb("k_rows", [P, NT, HD])
        q_T = s.sb("q_T", [P, T])
        k_T = s.sb("k_T", [P, T])
        q_dec = s.sb("q_dec", [P, T])
        v_rows = [s.sb(f"v_rows{b}", [P, NT, HD]) for b in range(2)]
        v_dec = s.sb("v_dec", [P, NT, HD])
        gate = s.sb("gate", [P, T])
        arg = s.sb("arg", [P, NT, P])
        mix = s.sb("mix", [P, NT, P])
        e_dec = s.sb("e_dec", [P, T])
        probs = s.sb("probs", [P, NT, P])
        state = s.sb("state", [P, NT, HD])
        ps = [s.ps(f"pair{n}", [P, T]) for n in range(4)]
        tiled = [p[:, :].rearrange("p (c d) -> p c d", c=NT) for p in ps]
        sem = s.sem
        qk_loaded, v_loaded, g_loaded, d_loaded = ([sem(f"{m}_loaded{b}") for b in range(2)] for m in ("qk", "v", "g", "d"))
        q_high, k_high, g_high = (sem(f"{m}_high") for m in "qkg")
        q_split, k_split, g_split = (sem(f"{m}_split") for m in "qkg")
        q_projected, k_projected, v_projected, g_projected = (sem(f"{m}_projected") for m in "qkvg")
        q_tapped, q_conved, k_conved, q_acted, k_acted = (
            sem(x) for x in ("q_tapped", "q_conved", "k_conved", "q_acted", "k_acted"))
        q_rowed, k_rowed = sem("q_rowed"), sem("k_rowed")
        var_ready, rstd_ready, shift_ready = sem("var_ready"), sem("rstd_ready"), sem("shift_ready")
        q_normed, k_normed, k_rows_done = sem("q_normed"), sem("k_normed"), sem("k_rows_done")
        q_turned, k_turned, q_T_done, k_T_done = sem("q_turned"), sem("k_turned"), sem("q_T_done"), sem("k_T_done")
        v_copied, v_dec_done, g_acted = sem("v_copied"), sem("v_dec_done"), sem("g_acted")
        arg_ready, mix_exped, masked, e_dec_done, q_dec_done = (
            sem(x) for x in ("arg_ready", "mix_exped", "masked", "e_dec_done", "q_dec_done"))
        scored, kv_done, probs_done, states_done = (sem(x) for x in ("scored", "kv_done", "probs_done", "states_done"))
        o_done, gated = sem("o_done"), sem("gated")

        def pipeline(eng, step):
            step(0, 0, True, False, False)
            step(0, 1, True, True, False)
            for b in range(2):
                step(1, b, True, True, True)
            with eng.Fori(2, LH // 2) as i:
                for b in range(2):
                    step(i, b, True, True, True)
            step(LH // 2, 0, False, True, True)
            step(LH // 2, 1, False, False, True)

        def wait_for(eng, semaphore, count):
            if not (isinstance(count, int) and count < 1):
                eng.wait_ge(semaphore, count)

        def loads(i, b, lag):
            return i + (b - lag - (b - lag) % 2) // 2 + 1

        with nc.Block() as block:

            @block.sync
            def _(sp):
                def head(m, b, reuse):
                    def cols_of(W):
                        view = W.rearrange("(k p) (h c) -> p k h c", p=P, c=HD)
                        return view[:, :, bass.ds(m, 1), :].rearrange("p k o c -> p k (o c)")

                    if reuse:
                        sp.wait_ge(k_split, m - 1)
                        sp.wait_ge(k_conved, m - 1)
                    sp.dma_start(wq[b][:, :, :], cols_of(Wq)).then_inc(qk_loaded[b], 16)
                    sp.dma_start(wk[b][:, :, :], cols_of(Wk)).then_inc(qk_loaded[b], 16)
                    for j, (cw, cb) in enumerate((w["q_taps"], w["k_taps"])):
                        rows = cw.rearrange("(h p) t -> p h t", p=P)[:, bass.ds(m, 1), :].rearrange("p o t -> p (o t)")
                        sp.dma_start(taps[b][:, j, 0:TAPS], rows).then_inc(qk_loaded[b], 16)
                        bias = cb.rearrange("(h p o) -> p h o", p=P, o=1)[:, bass.ds(m, 1), :]
                        sp.dma_start(taps[b][:, j, TAPS:TAPS + 1], bias.rearrange("p a o -> p (a o)"))\
                            .then_inc(qk_loaded[b], 16)
                    if reuse:
                        sp.wait_ge(v_projected, m - 1)
                    sp.dma_start(wv[b][:, :, :], cols_of(Wv)).then_inc(v_loaded[b], 16)
                    if reuse:
                        sp.wait_ge(e_dec_done, m - 1)
                    sp.dma_start(decay[b][:, :], decay_dram[bass.ds(m, 1), :].to_broadcast((P, T))).then_inc(d_loaded[b], 16)
                    if reuse:
                        sp.wait_ge(g_split, m - 1)
                    sp.dma_start(wg[b][:, :, :], cols_of(Wg)).then_inc(g_loaded[b], 16)

                for b in range(2):
                    head(b, b, False)
                with sp.Fori(1, LH // 2) as i:
                    for b in range(2):
                        head(2 * i + b, b, True)

            @block.tensor
            def _(pe):
                def project(weights, out, done):
                    for half in range(2):
                        cols = slice(half * HALF, (half + 1) * HALF)
                        for k in range(DK):
                            i = matmul3(pe, out[:, cols], [q[:, k, :] for q in weights],
                                        [q[:, k, cols] for q in x_parts], k == 0, k == DK - 1)
                    i.then_inc(done, 1)

                def turn(out, src, done):
                    for c in range(NT):
                        i = pe.transpose(out[:, c * P:(c + 1) * P], src(c), ident[:, :])
                    i.then_inc(done, 1)

                def step(i_, b, a0, a1, a2):
                    n = 2 * i_ + b
                    if a1:
                        pe.wait_ge(v_loaded[1 - b], 16 * loads(i_, b, 1))
                        pe.wait_ge(q_conved, n)
                        for c in range(NT):
                            for k in range(DK):
                                i = pe.matmul(tiled[0][:, c, :], xT[:, k, c * P:(c + 1) * P], wv[1 - b][:, k, :],
                                              start=(k == 0), stop=(k == DK - 1))
                        i.then_inc(v_projected, 1)
                        pe.wait_ge(q_acted, n)
                        if a2:
                            pe.wait_ge(k_T_done, n - 1)
                        turn(ps[1], lambda c: conv[0][:, c * P:(c + 1) * P], q_rowed)
                        pe.wait_ge(k_acted, n)
                        turn(ps[2], lambda c: conv[1][:, c * P:(c + 1) * P], k_rowed)
                    if a2:
                        pe.wait_ge(g_split, n - 1)
                        wait_for(pe, gated, n - 2)
                        project(parts["gate"], ps[3], g_projected)
                        if a1:
                            pe.wait_ge(v_copied, n)
                        else:
                            wait_for(pe, probs_done, n - 2)
                        pe.wait_ge(q_T_done, n - 1)
                        pe.wait_ge(k_T_done, n - 1)
                        for c in range(NT):
                            cols = slice(c * P, (c + 1) * P)
                            i = pe.matmul(ps[0][:, cols], k_T[:, cols], q_T[:, cols], start=True, stop=True)
                        i.then_inc(scored, 1)
                        pe.wait_ge(g_acted, n - 1)
                        pe.wait_ge(k_rows_done, n - 1)
                        pe.wait_ge(v_dec_done, n - 1)
                        for c in range(NT - 1):
                            i = pe.matmul(tiled[3][:, c, :], k_rows[:, c, :], v_dec[:, c, :], start=True, stop=True)
                        i.then_inc(kv_done, 1)
                    if a0:
                        pe.wait_ge(q_split, n + 1)
                        if a2:
                            pe.wait_ge(probs_done, n - 1)
                        elif a1:
                            pe.wait_ge(v_copied, n)
                        project(parts["q"], ps[0], q_projected)
                    if a1:
                        pe.wait_ge(q_normed, n)
                        if a2:
                            pe.wait_ge(states_done, n - 1)
                        turn(ps[3], lambda c: normed[0][:, c, :], q_turned)
                        pe.wait_ge(k_normed, n)
                        turn(ps[1], lambda c: normed[1][:, c, :], k_turned)
                    if a0:
                        pe.wait_ge(k_split, n + 1)
                        project(parts["k"], ps[2], k_projected)
                    if a2:
                        pe.wait_ge(probs_done, n - 1)
                        pe.wait_ge(states_done, n - 1)
                        pe.wait_ge(q_dec_done, n - 1)
                        if a1:
                            pe.wait_ge(q_T_done, n)
                        for c in range(NT):
                            cols = slice(c * P, (c + 1) * P)
                            i = pe.matmul(ps[3][:, cols], v_rows[b][:, c, :], probs[:, c, :], start=True, stop=(c == 0))
                            if c:
                                i = pe.matmul(ps[3][:, cols], state[:, c, :], q_dec[:, cols], start=False, stop=True)
                        i.then_inc(o_done, 1)

                pipeline(pe, step)

            @block.scalar
            def _(act):
                def high(m, src, used, head, loaded, count, done):
                    act.wait_ge(loaded, count)
                    wait_for(act, used, head)
                    act.activation(parts[m][0][:, :, :], src[:, :, :], ACT.Copy).then_inc(done, 1)

                def step(i_, b, a0, a1, a2):
                    n = 2 * i_ + b
                    if a1:
                        act.wait_ge(v_projected, n)
                        if a2:
                            wait_for(act, o_done, n - 2)
                            wait_for(act, v_dec_done, n - 2)
                        act.activation(v_rows[1 - b][:, :, :], tiled[0], ACT.Copy).then_inc(v_copied, 1)
                    if a0:
                        high("q", wq[b], q_projected, n, qk_loaded[b], 96 * loads(i_, b, 0), q_high)
                        high("k", wk[b], k_projected, n, qk_loaded[b], 96 * loads(i_, b, 0), k_high)
                    if a2:
                        act.wait_ge(g_projected, n - 1)
                        wait_for(act, gated, n - 2)
                        act.activation(gate[:, :], ps[3][:, :], ACT.Silu).then_inc(g_acted, 1)
                    if a1:
                        act.wait_ge(shift_ready, n)
                        if a2:
                            act.wait_ge(k_turned, n - 1)
                            act.wait_ge(k_rows_done, n - 1)
                        for c in range(NT):
                            i = act.activation(normed[1][:, c, :], tiled[2][:, c, :], ACT.Identity,
                                               scale=rstd[:, 1, c:c + 1], bias=k_shift[:, c:c + 1])
                        i.then_inc(k_normed, 1)
                    if a0:
                        act.wait_ge(q_projected, n + 1)
                        act.activation(conv[0][:, :], ps[0][:, :], ACT.Identity, scale=taps[b][:, 0, TAPS - 1:TAPS],
                                       bias=taps[b][:, 0, TAPS:TAPS + 1]).then_inc(q_tapped, 1)
                    if a1:
                        act.wait_ge(q_turned, n)
                        if a2:
                            act.wait_ge(q_dec_done, n - 1)
                            act.wait_ge(scored, n - 1)
                        act.activation(q_T[:, :], ps[3][:, :], ACT.Identity, scale=norm_col[:, 0:1],
                                       bias=norm_col[:, 1:2]).then_inc(q_T_done, 1)
                        act.wait_ge(k_turned, n)
                        act.activation(k_T[:, :], ps[1][:, :], ACT.Identity, scale=norm_col[:, 2:3],
                                       bias=norm_col[:, 3:4]).then_inc(k_T_done, 1)
                        high("gate", wg[1 - b], g_projected, n - 1, g_loaded[1 - b], 16 * loads(i_, b, 1), g_high)
                    if a1:
                        act.wait_ge(arg_ready, n)
                        if a2:
                            act.wait_ge(probs_done, n - 1)
                            act.wait_ge(v_dec_done, n - 1)
                        for c in range(NT):
                            i = act.activation(mix[:, c, :], arg[:, c, :], ACT.Exp, bias=hcol[1 - b][:, 1, c:c + 1])
                        i.then_inc(mix_exped, 1)
                        if a2:
                            act.wait_ge(states_done, n - 1)
                            act.wait_ge(q_dec_done, n - 1)
                        act.activation(e_dec[:, :], decay[1 - b][:, :], ACT.Exp).then_inc(e_dec_done, 1)
                    if a0:
                        act.wait_ge(q_conved, n + 1)
                        act.activation(conv[0][:, :], conv[0][:, :], ACT.Silu).then_inc(q_acted, 1)
                        act.wait_ge(k_conved, n + 1)
                        act.activation(conv[1][:, :], conv[1][:, :], ACT.Silu).then_inc(k_acted, 1)

                pipeline(act, step)

            @block.vector
            def _(dve):
                def convolve(n, b, m, pair, tapped, done):
                    if m == 0:
                        dve.wait_ge(tapped, n + 1)
                    else:
                        dve.wait_ge(k_projected, n + 1)
                        if not (isinstance(n, int) and n < 1):
                            dve.wait_ge(k_rowed, n)
                        dve.tensor_scalar(conv[m][:, :], ps[pair][:, :], taps[b][:, m, TAPS - 1:TAPS],
                                          taps[b][:, m, TAPS:TAPS + 1], ALU.mult, ALU.add)
                        dve.drain()
                    for j in range(TAPS - 1):
                        back = TAPS - 1 - j
                        i = dve.scalar_tensor_tensor(conv[m][:, back:T], ps[pair][:, 0:T - back], taps[b][:, m, j:j + 1],
                                                     conv[m][:, back:T], ALU.mult, ALU.add)
                        if j < TAPS - 2:
                            dve.drain()
                    i.then_inc(done, 1)

                def step(i_, b, a0, a1, a2):
                    n = 2 * i_ + b
                    if a1:
                        m = n - 1
                        if a2:
                            dve.wait_ge(mix_exped, n - 1)
                        src = cols[:, :, :, bass.ds(m, 1)].rearrange("p a c o -> p a (c o)")
                        dve.tensor_copy(hcol[1 - b][:, :, :], src)
                        dve.drain()
                        dve.wait_ge(d_loaded[1 - b], 16 * loads(i_, b, 1))
                        for c in range(NT):
                            i = dve.tensor_scalar(arg[:, c, :], decay[1 - b][:, c * P:(c + 1) * P],
                                                  hcol[1 - b][:, 0, c:c + 1], 0.0, ALU.subtract, ALU.min)
                        i.then_inc(arg_ready, 1)
                        for m, (pair, rowed) in enumerate(((1, q_rowed), (2, k_rowed))):
                            dve.wait_ge(rowed, n)
                            for c in range(NT):
                                dve.bn_stats(stats[:, m, c, :], tiled[pair][:, c, :])
                        dve.drain()
                        for m in range(2):
                            for c in range(NT):
                                dve.bn_aggr(mean_var[:, m, c, :], stats[:, m, c, :])
                        dve.drain()
                        dve.tensor_scalar(var_eps[:, :, :], mean_var[:, :, :, 1], EPS, None, ALU.add).then_inc(var_ready, 1)
                    if a2:
                        dve.wait_ge(scored, n - 1)
                        dve.wait_ge(masked, n - 1)
                        wait_for(dve, o_done, n - 2)
                        dve.tensor_tensor(probs[:, :, :], tiled[0], mix[:, :, :], ALU.mult).then_inc(probs_done, 1)
                        dve.wait_ge(kv_done, n - 1)
                        dve.wait_ge(e_dec_done, n - 1)
                        dve.tensor_copy(state[:, 1, :], tiled[3][:, 0, :])
                        for c in range(1, NT - 1):
                            dve.drain()
                            i = dve.scalar_tensor_tensor(state[:, c + 1, :], state[:, c, :],
                                                         e_dec[:, (c + 1) * P - 1:(c + 1) * P], tiled[3][:, c, :],
                                                         ALU.mult, ALU.add)
                        i.then_inc(states_done, 1)
                    if a1:
                        dve.wait_ge(rstd_ready, n)
                        dve.scalar_tensor_tensor(k_shift[:, :], mean_var[:, 1, :, 0], -1.0, rstd[:, 1, :], ALU.mult,
                                                 ALU.mult).then_inc(shift_ready, 1)
                        if a2:
                            dve.wait_ge(q_turned, n - 1)
                        for c in range(NT):
                            i = dve.tensor_scalar(normed[0][:, c, :], tiled[1][:, c, :], mean_var[:, 0, c, 0:1],
                                                  rstd[:, 0, c:c + 1], ALU.subtract, ALU.mult)
                        i.then_inc(q_normed, 1)
                    if a0:
                        convolve(n, b, 0, 0, q_tapped, q_conved)
                        convolve(n, b, 1, 2, None, k_conved)
                    if a2:
                        dve.wait_ge(o_done, n - 1)
                        dve.wait_ge(g_acted, n - 1)
                        out = gated_out[:, bass.ds(n - 2, 1), :].rearrange("p o t -> p (o t)")
                        dve.tensor_tensor(out, gate[:, :], ps[3][:, :], ALU.mult).then_inc(gated, 1)

                pipeline(dve, step)

            @block.gpsimd
            def _(pool):
                def low(m, src, high, head, done):
                    pool.wait_ge(high, head + 1)
                    pool.tensor_tensor(parts[m][1][:, :, :], src[:, :, :], parts[m][0][:, :, :].bitcast(F32), ALU.subtract)\
                        .then_inc(done, 1)

                def step(i_, b, a0, a1, a2):
                    n = 2 * i_ + b
                    if a0:
                        low("q", wq[b], q_high, n, q_split)
                        low("k", wk[b], k_high, n, k_split)
                    if a1:
                        pool.wait_ge(var_ready, n)
                        if a2:
                            pool.wait_ge(k_normed, n - 1)
                        pool.tensor_tensor(rstd[:, :, :].rearrange("p a b -> p (a b)"),
                                           var_eps[:, :, :].rearrange("p a b -> p (a b)"), neg_half[:, 0:2 * NT],
                                           ALU.pow).then_inc(rstd_ready, 1)
                        pool.wait_ge(k_normed, n)
                        if a2:
                            pool.wait_ge(kv_done, n - 1)
                        rows = [norm_row[:, j, :].rearrange("p (o d) -> p o d", o=1).to_broadcast((P, NT, HD))
                                for j in range(2)]
                        pool.tensor_tensor(k_rows[:, :, :], normed[1][:, :, :], rows[0], ALU.mult)
                        low("gate", wg[1 - b], g_high, n - 1, g_split)
                        pool.drain()
                        pool.wait_ge(mix_exped, n)
                        pool.tensor_tensor(k_rows[:, :, :], k_rows[:, :, :], rows[1], ALU.add).then_inc(k_rows_done, 1)
                        pool.affine_select(out=mix[:, :, :], in_=mix[:, :, :], compare_op=ALU.is_ge, fill=0.0, base=0,
                                           pattern=[[0, NT], [1, P]], channel_multiplier=-1).then_inc(masked, 1)
                        pool.drain()
                        pool.wait_ge(v_copied, n)
                        last = mix[:, :, P - 1:P].to_broadcast((P, NT, HD))
                        pool.tensor_tensor(v_dec[:, :, :], v_rows[1 - b][:, :, :], last, ALU.mult).then_inc(v_dec_done, 1)
                        pool.wait_ge(q_T_done, n)
                        pool.wait_ge(e_dec_done, n)
                        if a2:
                            pool.wait_ge(o_done, n - 1)
                        pool.tensor_tensor(q_dec[:, :], q_T[:, :], e_dec[:, :], ALU.mult).then_inc(q_dec_done, 1)

                pipeline(pool, step)


NX = 16
FX = 176
TOP = 4
FS = 2 * FX
GX = 8
GT = GX * FX // P
NG = NX // GX
ST = -(-FS // P)
SLOTS = 3
RSLOTS = 2


def top_router_block(nc, ident, gate_weight, earlier, x_parts, w_dram):
    with Scope(nc, "top") as s:
        gw = s.sb("gw", [NX, D])
        gw_parts = [s.sb(f"gw_part{q}", [P, DK, NX], F32R) for q in range(2)]
        w = s.sb("w", [P, NT, NX])
        mask = s.sb("mask", [P, NT, NX])
        total = s.sb("total", [P, NT])
        greater = s.sb("greater", [P, NT, NX, NX])
        same = s.sb("same", [P, NT, NX, NX])
        w_rows = s.sb("w_rows", [NX, T])
        ps_t = s.ps("gw_turned", [P, DK, NX])
        logits = s.ps("logits", [P, NT, NX])
        w_turned = s.ps("w_turned", [NX, T])
        loaded, gw_turned, gw_copied = s.sem("loaded"), s.sem("gw_turned"), s.sem("gw_copied")
        scored, shifted, exped, w_ready = s.sem("scored"), s.sem("shifted"), s.sem("exped"), s.sem("w_ready")
        turned, rows_ready, stored = s.sem("turned"), s.sem("rows_ready"), s.sem("stored")
        with nc.Block() as block:

            @block.sync
            def _(sp):
                sp.dma_start(gw[:, :], gate_weight).then_inc(loaded, 16)
                sp.wait_ge(rows_ready, 1)
                sp.dma_start(w_dram, w_rows[:, :]).then_inc(stored, 16)
                sp.wait_ge(stored, 16)

            @block.tensor
            def _(pe):
                pe.wait_ge(loaded, 16)
                for k in range(DK):
                    i = pe.transpose(ps_t[:, k, :], gw[:, k * P:(k + 1) * P], ident[0:NX, 0:NX])
                i.then_inc(gw_turned, 1)
                pe.wait_ge(gw_copied, 1)
                for c in range(NT):
                    for k in range(DK):
                        i = matmul3(pe, logits[:, c, :], [q[:, k, c * P:(c + 1) * P] for q in x_parts],
                                    [q[:, k, :] for q in gw_parts], k == 0, k == DK - 1)
                i.then_inc(scored, 1)
                pe.wait_ge(w_ready, 1)
                for c in range(NT):
                    i = pe.transpose(w_turned[:, c * P:(c + 1) * P], w[:, c, :], ident[:, :])
                i.then_inc(turned, 1)

            @block.scalar
            def _(act):
                act.wait_ge(shifted, 1)
                act.activation(w[:, :, :], w[:, :, :], ACT.Exp).then_inc(exped, 1)
                act.wait_ge(turned, 1)
                act.activation(w_rows[:, :], w_turned[:, :], ACT.Copy).then_inc(rows_ready, 1)

            @block.vector
            def _(dve):
                dve.wait_ge(gw_turned, 1)
                split_small(dve, [q[:, :, :] for q in gw_parts], ps_t[:, :, :]).then_inc(gw_copied, 1)
                dve.wait_ge(scored, 1)
                dve.tensor_reduce(total[:, :], logits[:, :, :], axis=AX, op=ALU.max)
                dve.drain()
                dve.tensor_tensor(w[:, :, :], logits[:, :, :], col(total[:, :], NX), ALU.subtract).then_inc(shifted, 1)
                dve.wait_ge(exped, 1)
                dve.tensor_reduce(total[:, :], w[:, :, :], axis=AX, op=ALU.add)
                dve.drain()
                dve.reciprocal(total[:, :], total[:, :])
                dve.drain()
                dve.tensor_tensor(w[:, :, :], w[:, :, :], col(total[:, :], NX), ALU.mult)
                dve.drain()
                rank_mask(dve, w[:, :, :], mask[:, :, :], greater[:, :, :, :], same[:, :, :, :], earlier, NX, TOP)
                dve.tensor_tensor(w[:, :, :], w[:, :, :], mask[:, :, :], ALU.mult).then_inc(w_ready, 1)


def glu_block(nc, tag, ident, x_parts, mids, down_T, base, groups, tiles, loads, routing):
    N = len(tiles)
    with Scope(nc, tag) as s:
        natural = [s.sb(f"natural{b}", [P, 2, D]) for b in range(SLOTS)]
        down = [s.sb(f"down{b}", [P, DK, P]) for b in range(SLOTS)]
        w_T = [[s.sb(f"w_T{b}{q}", [P, 2, DK, P], F32R) for q in range(2)] for b in range(2)]
        weight = [s.sb(f"weight{b}", [P, T]) for b in range(RSLOTS)] if routing else None
        gated = [s.sb(f"gated{b}", [P, HALF]) for b in range(2)]
        ps_w = [s.ps(f"turned_w{b}", [P, 2, DK, P]) for b in range(2)]
        ps_d = [s.ps(f"turned_d{b}", [P, HALF]) for b in range(2)]
        ps_g = [s.ps(f"gate{b}", [P, HALF]) for b in range(2)]
        ps_u = [s.ps(f"up{b}", [P, HALF]) for b in range(2)]
        loaded = [s.sem(f"loaded{b}") for b in range(SLOTS)]
        r_loaded = [s.sem(f"r_loaded{b}") for b in range(RSLOTS)]
        w_high, d_high = s.sem("w_high"), s.sem("d_high")
        w_turned, w_copied = s.sem("w_turned"), s.sem("w_copied")
        d_turned, d_copied = s.sem("d_turned"), s.sem("d_copied")
        gate_done, up_done = s.sem("gate_done"), s.sem("up_done")
        gate_taken, up_taken, weighted = s.sem("gate_taken"), s.sem("up_taken"), s.sem("weighted")

        def dmas(source, slots):
            parts = [list(source(0, n)) for n in range(N)]
            per_group = [16 * sum(len(parts[n]) for n in range(N) if n % slots == b) for b in range(slots)]
            upto = [16 * sum(len(parts[m]) for m in range(n + 1) if m % slots == n % slots) for n in range(N)]
            return per_group, upto

        def last_user(n, slots):
            return slots if n >= slots else n + N - max(m for m in range(N) if m % slots == n % slots)

        w_group, w_upto = dmas(loads, SLOTS)
        if routing:
            r_group, r_upto = dmas(routing, RSLOTS)

        def over_groups(eng, body):
            body(0, True)
            if groups > 1:
                with eng.Fori(1, groups) as g:
                    body(g, False)

        with nc.Block() as block:

            @block.sync
            def _(sp):
                def group(g, first):
                    for n in range(N):
                        at = g * N + n
                        back = last_user(n, SLOTS)
                        if not first or n >= SLOTS:
                            sp.wait_ge(w_turned, at - back + 1)
                            sp.wait_ge(d_turned, at - back + 1)
                        for what, rows, src in loads(g, n):
                            dst = {"gate": natural[n % SLOTS][rows, 0, :], "up": natural[n % SLOTS][rows, 1, :],
                                   "down": down[n % SLOTS][:, :, rows]}[what]
                            sp.dma_start(dst, src).then_inc(loaded[n % SLOTS], 16)
                        if routing:
                            if not first or n >= RSLOTS:
                                sp.wait_ge(weighted, 2 * (at - last_user(n, RSLOTS) + 1))
                            for _, rows, src in routing(g, n):
                                sp.dma_start(weight[n % RSLOTS][rows, :], src).then_inc(r_loaded[n % RSLOTS], 16)

                over_groups(sp, group)

            @block.tensor
            def _(pe):
                def turn(g, n, first):
                    at = g * N + n
                    rows = tiles[n]
                    pe.wait_ge(loaded[n % SLOTS], w_group[n % SLOTS] * g + w_upto[n])
                    if not first or n >= 2:
                        pe.wait_ge(w_copied, at - last_user(n, 2) + 1)
                    for m in range(2):
                        for k in range(DK):
                            i = pe.transpose(ps_w[n % 2][:, m, k, 0:rows], natural[n % SLOTS][0:rows, m, k * P:(k + 1) * P],
                                             ident[0:rows, 0:rows])
                    i.then_inc(w_turned, 1)
                    if not first or n >= 2:
                        pe.wait_ge(d_copied, at - last_user(n, 2) + 1)
                    for k in range(DK):
                        i = pe.transpose(ps_d[n % 2][0:rows, k * P:(k + 1) * P], down[n % SLOTS][:, k, 0:rows], ident[:, :])
                    i.then_inc(d_turned, 1)

                def group(g, first):
                    turn(g, 0, first)
                    for n in range(N):
                        at = g * N + n
                        if n + 1 < N:
                            turn(g, n + 1, first)
                        pe.wait_ge(w_copied, at + 1)
                        for half in range(2):
                            cols = slice(half * HALF, (half + 1) * HALF)
                            for m, (ps, taken, done) in enumerate(((ps_g, gate_taken, gate_done), (ps_u, up_taken, up_done))):
                                if not first or n:
                                    pe.wait_ge(taken, 2 * at + half - 1)
                                for k in range(DK):
                                    i = matmul3(pe, ps[half][0:tiles[n], :], [w[:, m, k, 0:tiles[n]] for w in w_T[n % 2]],
                                                [q[:, k, cols] for q in x_parts], k == 0, k == DK - 1)
                                i.then_inc(done, 1)

                over_groups(pe, group)

            @block.scalar
            def _(act):
                def copy(g, n, first):
                    at, rows = g * N + n, tiles[n]
                    act.wait_ge(w_turned, at + 1)
                    if not first or n >= 2:
                        act.wait_ge(up_done, 2 * (at - last_user(n, 2) + 1))
                    act.activation(w_T[n % 2][0][:, :, :, 0:rows], ps_w[n % 2][:, :, :, 0:rows], ACT.Copy).then_inc(w_high, 1)
                    act.wait_ge(d_turned, at + 1)
                    act.activation(down_T[0][0:rows, bass.ds(base + at, 1), :].rearrange("p o d -> p (o d)"),
                                   ps_d[n % 2][0:rows, 0:D], ACT.Copy).then_inc(d_high, 1)

                def group(g, first):
                    copy(g, 0, first)
                    for n in range(N):
                        at, rows = g * N + n, tiles[n]
                        if n + 1 < N:
                            copy(g, n + 1, first)
                        for half in range(2):
                            if not first or n:
                                act.wait_ge(up_taken, 2 * at + half - 1)
                            act.wait_ge(gate_done, 2 * at + half + 1)
                            act.activation(gated[half][0:rows, :], ps_g[half][0:rows, :], ACT.Silu).then_inc(gate_taken, 1)

                over_groups(act, group)

            @block.vector
            def _(dve):
                def low(g, n):
                    at, rows = g * N + n, tiles[n]
                    w = w_T[n % 2]
                    dve.wait_ge(w_high, at + 1)
                    dve.tensor_tensor(w[1][:, :, :, 0:rows], ps_w[n % 2][:, :, :, 0:rows], w[0][:, :, :, 0:rows].bitcast(F32),
                                      ALU.subtract).then_inc(w_copied, 1)
                    dve.wait_ge(d_high, at + 1)
                    high, out = (q[0:rows, bass.ds(base + at, 1), :].rearrange("p o d -> p (o d)") for q in down_T)
                    dve.tensor_tensor(out, ps_d[n % 2][0:rows, 0:D], high.bitcast(F32), ALU.subtract).then_inc(d_copied, 1)

                def group(g, first):
                    low(g, 0)
                    for n in range(N):
                        at, rows = g * N + n, tiles[n]
                        if n + 1 < N:
                            low(g, n + 1)
                        for half in range(2):
                            cols = slice(half * HALF, (half + 1) * HALF)
                            out = mids[0:rows, bass.ds(base + at, 1), cols].rearrange("p o t -> p (o t)")
                            dve.wait_ge(gate_taken, 2 * at + half + 1)
                            dve.wait_ge(up_done, 2 * at + half + 1)
                            dve.tensor_tensor(out, gated[half][0:rows, :], ps_u[half][0:rows, :], ALU.mult)\
                                .then_inc(up_taken, 1)

                over_groups(dve, group)

            @block.gpsimd
            def _(pool):
                if not routing:
                    return

                def group(g, first):
                    for n in range(N):
                        at, rows = g * N + n, tiles[n]
                        pool.wait_ge(r_loaded[n % RSLOTS], r_group[n % RSLOTS] * g + r_upto[n])
                        for half in range(2):
                            cols = slice(half * HALF, (half + 1) * HALF)
                            pool.wait_ge(up_taken, 2 * at + half + 1)
                            out = mids[0:rows, bass.ds(base + at, 1), cols].rearrange("p o t -> p (o t)")
                            pool.tensor_tensor(out, out, weight[n % RSLOTS][0:rows, cols], ALU.mult)\
                                .then_inc(weighted, 1)

                over_groups(pool, group)


def routed_tiles(gate_up, down_w, w_dram):
    gu = gate_up.rearrange("(g e) (m f) d -> g e m f d", e=GX, m=2)
    dw = down_w.rearrange("(g e) (k p) f -> g e p k f", e=GX, p=P)
    rw = w_dram.rearrange("(g e) t -> g e t", e=GX)

    def pieces(n):
        at = n * P
        while at < (n + 1) * P:
            e, r = divmod(at, FX)
            k = min(FX - r, (n + 1) * P - at)
            yield e, r, k, slice(at - n * P, at - n * P + k)
            at += k

    def loads(g, n):
        for e, r, k, rows in pieces(n):
            for m, what in enumerate(("gate", "up")):
                yield what, rows, gu[bass.ds(g, 1), e, m, r:r + k, :].rearrange("o f d -> (o f) d")
            yield "down", rows, dw[bass.ds(g, 1), e, :, :, r:r + k].rearrange("o p k f -> (o p) k f")

    def routing(g, n):
        for e, r, k, rows in pieces(n):
            yield "weight", rows, rw[bass.ds(g, 1), e, :].to_broadcast((k, T))

    return loads, routing


def shared_tiles(gate_up, down_w):
    gu = gate_up.rearrange("(m f) d -> m f d", m=2)
    dw = down_w.rearrange("(k p) f -> p k f", p=P)

    def loads(g, n):
        k = min(P, FS - n * P)
        for m, what in enumerate(("gate", "up")):
            yield what, slice(0, k), gu[m, n * P:n * P + k, :]
        yield "down", slice(0, k), dw[:, :, n * P:n * P + k]

    return loads


def network(nc, a, rope_table, earlier_table, out):
    Scope.used.clear()
    gold_w = nc.dram_tensor("gold_weights", [NE, T], F32, kind="Internal").ap()
    decay_sums = nc.dram_tensor("decay_sums", [LH, T], F32, kind="Internal").ap()
    top_w = nc.dram_tensor("top_weights", [NX, T], F32, kind="Internal").ap()

    def row(ap):
        return ap.rearrange("(o n) -> o n", o=1).to_broadcast((P, ap.shape[0]))

    def column(ap):
        return ap.rearrange("(n o) -> n o", o=1)

    def by_tiles(ap):
        return ap.rearrange("(k p) n -> p k n", p=P)

    with Scope(nc, "net") as net:
        ident, identb = net.sb("ident", [P, P]), net.sb("identb", [P, P], BF16)
        neg_half = net.sb("neg_half", [P, 2 * NT])
        x = net.sb("x", [P, NT, D])
        x_parts = [net.sb(f"x_part{m}", [P, DK, T], F32R) for m in range(2)]
        earlier = net.sb("earlier", [P, NX, NX])
        norm_row = net.sb("norm_row", [P, 2, HD])
        norm_col = net.sb("norm_col", [P, 4])
        inner_wb = net.sb("inner_wb", [P, 2, DK])
        rope = net.sb("rope", [P, NT, 2, ROT // 2])
        load_constants(nc, [
            (x[:, :, :], by_tiles(a["L0_attn_X"][0])),
            (inner_wb[:, 0, :], a["L0_attn_ln_w"].rearrange("(k p) -> p k", p=P)),
            (inner_wb[:, 1, :], a["L0_attn_ln_b"].rearrange("(k p) -> p k", p=P)),
            (rope[:, :, :, :], rope_table),
            (earlier[:, :, :], earlier_table.to_broadcast((P, NX * NX)).rearrange("p (a b) -> p a b", a=NX)),
            (norm_row[:, 0, :], row(a["L1_attn_kn_w"])), (norm_row[:, 1, :], row(a["L1_attn_kn_b"])),
            (norm_col[:, 0:1], column(a["L1_attn_qn_w"])), (norm_col[:, 1:2], column(a["L1_attn_qn_b"])),
            (norm_col[:, 2:3], column(a["L1_attn_kn_w"])), (norm_col[:, 3:4], column(a["L1_attn_kn_b"])),
        ], ident, identb, neg_half)

        with Scope(nc, "early") as early:
            xT = early.sb("xT", [P, DK, T])

            with Scope(nc, "s0") as s:
                xn = s.sb("xn", [P, NT, D])
                w_out = s.sb("w_out", [P, DK, D])
                context = s.sb("context", [P, NT, D])
                with Scope(nc, "s0a") as t:
                    norm_block(nc, "norm0", ident, neg_half, x, normed=xn, normed_T=xT, inner=context, inner_wb=inner_wb)
                    w_in = t.sb("w_in", [P, DK, 3 * D])
                    qk = t.sb("qk", [P, NT, 2 * D])
                    v = t.sb("v", [P, NT, NH, VW])
                    k_stack = t.sb("k_stack", [P, NH, T], BF16)
                    qkv_block(nc, a["L0_attn_W_in"], xT, w_in, rope, qk, v, k_stack)
                    attention_block(nc, ident, identb, qk, v, k_stack, context)
                turn_block(nc, "turn0", ident, context, xT)
                down_norm_block(nc, "out0", ident, neg_half, x, [xT[:, k, :] for k in range(DK)], w_down=w_out, add=xn,
                                load=(w_out[:, :, :], by_tiles(a["L0_attn_W_out"])), parts=x_parts)

            with Scope(nc, "s1") as s:
                golden_router_block(nc, ident, a["L0_ffn_Wr"], a["L0_ffn_temperature"], earlier[:, 0:NE, 0:NE], x_parts, gold_w)
                mids = s.sb("mids", [P, NE * FK, T])
                w_down = s.sb("w_down", [P, NE * FK, D])
                rings = [[s.sb(f"ring{m}{b}", [P, DK, FE]) for b in range(2)] for m in range(2)]
                Wg, Wu, Wd = (a[f"L0_ffn_W{m}"] for m in "gud")
                low_rank_block(nc, ident, [(a[f"L0_ffn_{m}a"], a[f"L0_ffn_{m}b"]) for m in "GUD"], rings, w_down, Wg, Wu, Wd)
                experts_block(nc, rings, x_parts, gold_w, Wg, Wu, mids)
                down_norm_block(nc, "out1", ident, neg_half, x, [mids[:, k, :] for k in range(NE * FK)], w_down=w_down,
                                parts=x_parts, xT=xT)

            clear_semaphores(nc)

            with Scope(nc, "s2") as s:
                gated = s.sb("gated", [P, LH, T])
                with Scope(nc, "s2a") as t:
                    cols = t.sb("cols", [P, 2, NT, LH])
                    decay_block(nc, ident, a["L1_attn_Wb"], a["L1_attn_bb"], x_parts, decay_sums, cols)
                    w = {m: a[f"L1_attn_W{n}"] for m, n in (("q", "q"), ("k", "k"), ("v", "v"), ("gate", "g"))}
                    w.update({f"{m}_taps": (a[f"L1_attn_{m}conv_w"], a[f"L1_attn_{m}conv_b"]) for m in "qk"})
                    linear_attention_block(nc, ident, neg_half, w, xT, x_parts, decay_sums, cols, norm_row, norm_col, gated)
                w_o = s.sb("w_o", [P, LH, D])
                down_norm_block(nc, "out2", ident, neg_half, x, [gated[:, k, :] for k in range(LH)], w_down=w_o,
                                load=(w_o[:, :, :], by_tiles(a["L1_attn_Wo"])), parts=x_parts)

        with Scope(nc, "s3") as s:
            top_router_block(nc, ident, a["L1_ffn_gate_weight"], earlier[:, :, :], x_parts, top_w)
            n = NG * GT + ST
            mids = s.sb("mids", [P, n, T])
            down_T = [s.sb(f"down_T{m}", [P, n, D], F32R) for m in range(2)]
            rows = [P] * (n - 1) + [FS - (ST - 1) * P]
            loads, routing = routed_tiles(a["L1_ffn_gate_up_weights"], a["L1_ffn_down_weights"], top_w)
            glu_block(nc, "routed", ident, x_parts, mids, down_T, 0, NG, rows[0:GT], loads, routing)
            loads = shared_tiles(a["L1_ffn_shared_gate_up"], a["L1_ffn_shared_down"])
            glu_block(nc, "shared", ident, x_parts, mids, down_T, NG * GT, 1, rows[NG * GT:], loads, None)
            down_norm_block(nc, "out3", ident, neg_half, x, [mids[0:rows[k], k, :] for k in range(n)], w_parts=down_T,
                            store=out[0])


_INS = [
    "L0_attn_X", "L0_attn_ln_w", "L0_attn_ln_b", "L0_attn_W_in", "L0_attn_W_out",
    "L0_ffn_Wg", "L0_ffn_Wu", "L0_ffn_Wd", "L0_ffn_Ga", "L0_ffn_Gb", "L0_ffn_Ua", "L0_ffn_Ub", "L0_ffn_Da",
    "L0_ffn_Db", "L0_ffn_Wr", "L0_ffn_temperature",
    "L1_attn_Wq", "L1_attn_Wk", "L1_attn_Wv", "L1_attn_Wb", "L1_attn_bb", "L1_attn_Wg", "L1_attn_Wo",
    "L1_attn_qconv_w", "L1_attn_qconv_b", "L1_attn_kconv_w", "L1_attn_kconv_b",
    "L1_attn_qn_w", "L1_attn_qn_b", "L1_attn_kn_w", "L1_attn_kn_b",
    "L1_ffn_gate_weight", "L1_ffn_gate_up_weights", "L1_ffn_down_weights", "L1_ffn_shared_gate_up",
    "L1_ffn_shared_down",
]


def rope_constants():
    inverse = (1.0 / np.float32(10000.0) ** (np.arange(0, ROT, 2, dtype=np.float32) / ROT)).astype(np.float32)
    angle = np.arange(T, dtype=np.float32)[:, None] * inverse[None, :]
    table = np.stack([np.cos(angle), np.sin(angle)], axis=1).astype(np.float32)
    return np.ascontiguousarray(table.reshape(NT, P, 2, ROT // 2).transpose(1, 0, 2, 3))


def kernel(**inputs):
    import concourse.bacc as bacc
    from concourse.bass_utils import run_bass_kernel_spmd

    nc = bacc.Bacc("TRN2", target_bir_lowering=False, num_devices=1)
    arrays = {f"in_{name}": np.ascontiguousarray(inputs[name]) for name in _INS}
    arrays["rope_table"] = rope_constants()
    arrays["earlier_table"] = np.tril(np.ones((NX, NX), np.float32), -1).reshape(1, NX * NX)
    aps = {name: nc.dram_tensor(name, v.shape, mybir.dt.from_np(v.dtype), kind="ExternalInput").ap()
           for name, v in arrays.items()}
    out = nc.dram_tensor("out_0", (1, T, D), F32, kind="ExternalOutput").ap()
    network(nc, {name: aps[f"in_{name}"] for name in _INS}, aps["rope_table"], aps["earlier_table"], out)
    r = run_bass_kernel_spmd(nc, [arrays], core_ids=[0])
    return r.results[0]["out_0"]
```

```python
import math
from contextlib import ExitStack

import numpy as np
import concourse.bass as bass
import concourse.mybir as mybir

F32 = mybir.dt.float32
F32R = mybir.dt.float32r
BF16 = mybir.dt.bfloat16
ALU = mybir.AluOpType
ACT = mybir.ActivationFunctionType
AX = mybir.AxisListType.X

P = 128
T = 1024
NT = T // P
D = 256
DK = D // P
HALF = 512
EPS = 1e-5


class Scope:

    used = []

    def __init__(self, nc, tag):
        self.nc, self.tag, self.ctx = nc, tag, ExitStack()

    def __enter__(self):
        self.ctx.__enter__()
        return self

    def __exit__(self, *a):
        return self.ctx.__exit__(*a)

    def sb(self, name, shape, dt=F32):
        return self.ctx.enter_context(self.nc.sbuf_tensor(f"{self.tag}_{name}", shape, dt))

    def ps(self, name, shape, dt=F32):
        return self.ctx.enter_context(self.nc.psum_tensor(f"{self.tag}_{name}", shape, dt))

    def sem(self, name):
        handle = self.ctx.enter_context(self.nc.semaphore(f"{self.tag}_{name}"))
        Scope.used.append(handle.num)
        return handle


def clear_semaphores(nc):
    with nc.Block() as block:

        @block.gpsimd
        def _(pool):
            pool.sem_clear(range(min(Scope.used), max(Scope.used) + 1))

    Scope.used.clear()


def col(ap, n):
    p, a = ap.shape
    return ap.rearrange("p (a o) -> p a o", o=1).to_broadcast((p, a, n))


def load_constants(nc, consts, ident, identb, neg_half):
    with Scope(nc, "const") as s:
        zeroed, loaded = s.sem("zeroed"), s.sem("loaded")
        with nc.Block() as block:

            @block.gpsimd
            def _(pool):
                pool.memset(ident[:, :], 0.0)
                pool.memset(identb[:, :], 0.0)
                pool.memset(neg_half[:, :], -0.5).then_inc(zeroed, 1)
                pool.wait_ge(zeroed, 1)
                pool.drain()
                for m in (ident, identb):
                    pool.affine_select(out=m[:, :], in_=m[:, :], compare_op=ALU.not_equal, fill=1.0,
                                       base=0, pattern=[[-1, P]], channel_multiplier=1)

            @block.sync
            def _(sp):
                for n, (dst, src) in enumerate(consts):
                    sp.dma_start(dst, src, allow_slow_non_contiguous=True).then_inc(loaded, 16)
                sp.wait_ge(loaded, 16 * len(consts))


def norm_block(nc, tag, ident, neg_half, x, normed, normed_T, inner, inner_wb, prefetch):
    with Scope(nc, tag) as s:
        stats = s.sb("stats", [P, NT, 6])
        mean_var = s.sb("mean_var", [P, NT, 2])
        var_eps = s.sb("var_eps", [P, NT])
        rstd = s.sb("rstd", [P, NT])
        turned = [s.ps(f"turned{k}", [P, T]) for k in range(DK)]
        var_ready, rstd_ready, tile_ready = s.sem("var_ready"), s.sem("rstd_ready"), s.sem("tile_ready")
        turn_done = s.sem("turn_done")
        chain = [(x, normed), (normed, inner)]
        with nc.Block() as block:

            @block.vector
            def _(dve):
                for k, (src, dst) in enumerate(chain):
                    for c in range(NT):
                        dve.bn_stats(stats[:, c, :], src[:, c, :])
                    dve.drain()
                    for c in range(NT):
                        dve.bn_aggr(mean_var[:, c, :], stats[:, c, :])
                    dve.drain()
                    dve.tensor_scalar(var_eps[:, :], mean_var[:, :, 1], EPS, None, ALU.add).then_inc(var_ready, 1)
                    dve.wait_ge(rstd_ready, k + 1)
                    for c in range(NT):
                        i = dve.tensor_scalar(dst[:, c, :], src[:, c, :], mean_var[:, c, 0:1], rstd[:, c:c + 1],
                                              ALU.subtract, ALU.mult)
                        if k == len(chain) - 1:
                            i.then_inc(tile_ready, 1)
                    dve.drain()

            @block.gpsimd
            def _(pool):
                for k in range(len(chain)):
                    pool.wait_ge(var_ready, k + 1)
                    pool.tensor_tensor(rstd[:, :], var_eps[:, :], neg_half[:, 0:NT], ALU.pow).then_inc(rstd_ready, 1)

            @block.tensor
            def _(pe):
                for c in range(NT):
                    pe.wait_ge(tile_ready, c + 1)
                    for k in range(DK):
                        i = pe.transpose(turned[k][:, c * P:(c + 1) * P], inner[:, c, k * P:(k + 1) * P], ident[:, :])
                    if c % 4 == 3:
                        i.then_inc(turn_done, 1)

            @block.scalar
            def _(act):
                for h in range(2):
                    act.wait_ge(turn_done, h + 1)
                    for k in range(DK):
                        cols = slice(h * HALF, (h + 1) * HALF)
                        act.activation(normed_T[:, k, cols], turned[k][:, cols], ACT.Identity,
                                       scale=inner_wb[:, 0, k:k + 1], bias=inner_wb[:, 1, k:k + 1])

            @block.sync
            def _(sp):
                prefetch(sp)


def matmul3(pe, out, w, x, start, stop):
    pe.matmul(out, w[0], x[0], start=start, stop=False)
    pe.matmul(out, w[0], x[1], start=False, stop=False)
    return pe.matmul(out, w[1], x[0], start=False, stop=stop)


def split_small(dve, parts, src):
    dve.tensor_copy(parts[0], src)
    dve.drain()
    return dve.tensor_tensor(parts[1], src, parts[0].bitcast(F32), ALU.subtract)


def score_tokens(pe, x_parts, w_parts, rows, ident, rows_ps, logits, rows_scored, rows_copied):
    n = w_parts[0].shape[-1]
    for half in range(2):
        cols = slice(half * HALF, (half + 1) * HALF)
        for k in range(DK):
            i = matmul3(pe, rows_ps[half], [q[:, k, :] for q in w_parts], [q[:, k, cols] for q in x_parts],
                        k == 0, k == DK - 1)
        i.then_inc(rows_scored, 1)
    for c in range(NT):
        if c % 4 == 0:
            pe.wait_ge(rows_copied, c // 4 + 1)
        i = pe.transpose(logits[:, c, :], rows[:, c * P:(c + 1) * P], ident[0:n, 0:n])
    return i


def copy_rows(act, rows, rows_ps, rows_scored, rows_copied):
    for half in range(2):
        cols = slice(half * HALF, (half + 1) * HALF)
        act.wait_ge(rows_scored, half + 1)
        act.activation(rows[:, cols], rows_ps[half], ACT.Copy).then_inc(rows_copied, 1)


class NormTail:

    JOBS = 4

    def __init__(self, s, ident, neg_half, x, acc, parts=None, xT=None, add=None, store=None, y=None, xn=None):
        self.ident, self.neg_half, self.x, self.acc = ident, neg_half, x, acc
        self.parts, self.xT, self.add, self.store = parts, xT, add, store
        self.norms = 1 if parts is None else 2
        self.y = y if y is not None else s.sb("y", [P, NT, D])
        self.stats = s.sb("tail_stats", [P, NT, 6])
        self.mean_var = s.sb("tail_mean_var", [P, NT, 2])
        self.var_eps = s.sb("tail_var_eps", [P, NT])
        self.rstd = s.sb("tail_rstd", [P, NT])
        (self.var_ready, self.rstd_ready, self.x_ready, self.xn_ready, self.x_turned, self.high_done,
         self.stored) = (s.sem(name) for name in (
             "var_ready", "rstd_ready", "x_ready", "xn_ready", "x_turned", "high_done", "stored"))
        if parts is not None:
            self.xn = xn if xn is not None else s.sb("xn", [P, NT, D])
            self.turned = [s.ps(f"x_turned{j}", [P, DK, 2 * P]) for j in range(self.JOBS)]
        self.events = []

    def pe_x(self, pe, j):
        if self.parts is None:
            return
        pe.wait_ge(self.xn_ready, j + 1)
        for c in range(2):
            for k in range(DK):
                i = pe.transpose(self.turned[j][:, k, c * P:(c + 1) * P], self.xn[:, 2 * j + c, k * P:(k + 1) * P],
                                 self.ident[:, :])
        i.then_inc(self.x_turned, 1)

    def act_x(self, act, j):
        if self.parts is None:
            return
        act.wait_ge(self.x_turned, j + 1)
        cols = slice(2 * j * P, (2 * j + 2) * P)
        if self.xT is not None:
            act.activation(self.xT[:, :, cols], self.turned[j][:, :, :], ACT.Copy)
        act.activation(self.parts[0][:, :, cols], self.turned[j][:, :, :], ACT.Copy).then_inc(self.high_done, 1)

    def variances(self, dve, j, src):
        tiles = range(2 * j, 2 * j + 2)
        for c in tiles:
            dve.bn_stats(self.stats[:, c, :], src(c))
        dve.drain()
        for c in tiles:
            dve.bn_aggr(self.mean_var[:, c, :], self.stats[:, c, :])
        dve.drain()
        dve.tensor_scalar(self.var_eps[:, 2 * j:2 * j + 2], self.mean_var[:, 2 * j:2 * j + 2, 1], EPS, None, ALU.add)\
            .then_inc(self.var_ready, 1)
        self.events.append(j)

    def normalise(self, dve, j, event, src, dst):
        dve.wait_ge(self.rstd_ready, event + 1)
        for c in range(2 * j, 2 * j + 2):
            i = dve.tensor_scalar(dst(c), src(c), self.mean_var[:, c, 0:1], self.rstd[:, c:c + 1], ALU.subtract, ALU.mult)
        return i

    def dve_jobs(self, dve, jobs, summed, count):
        both = {j: slice(2 * j, 2 * j + 2) for j in jobs}
        at = len(self.events)
        y_tile = lambda c: self.y[:, c, :]
        sums = y_tile if self.add is not None else lambda c: self.acc[c // 4][:, c % 4, :]
        for j in jobs:
            dve.wait_ge(summed, count(j))
            if self.add is not None:
                dve.tensor_tensor(self.y[:, both[j], :], self.acc[j // 2][:, 2 * (j % 2):2 * (j % 2) + 2, :],
                                  self.add[:, both[j], :], ALU.add)
                dve.drain()
            self.variances(dve, j, sums)
        for n, j in enumerate(jobs):
            self.normalise(dve, j, at + n, sums, y_tile)
            dve.drain()
            dve.tensor_tensor(self.x[:, both[j], :], self.x[:, both[j], :], self.y[:, both[j], :], ALU.add)\
                .then_inc(self.x_ready, 1)
            if self.parts is not None:
                dve.drain()
                self.variances(dve, j, lambda c: self.x[:, c, :])
        if self.parts is None:
            return
        for n, j in enumerate(jobs):
            self.normalise(dve, j, at + len(jobs) + n, lambda c: self.x[:, c, :], lambda c: self.xn[:, c, :])\
                .then_inc(self.xn_ready, 1)
        for j in jobs:
            dve.wait_ge(self.high_done, j + 1)
            cols = slice(2 * j * P, (2 * j + 2) * P)
            dve.tensor_tensor(self.parts[1][:, :, cols], self.turned[j][:, :, :], self.parts[0][:, :, cols].bitcast(F32),
                              ALU.subtract)

    def pool_norm(self, pool, event):
        j = self.order[event]
        pool.wait_ge(self.var_ready, event + 1)
        pool.tensor_tensor(self.rstd[:, 2 * j:2 * j + 2], self.var_eps[:, 2 * j:2 * j + 2], self.neg_half[:, 0:2], ALU.pow)\
            .then_inc(self.rstd_ready, 1)

    def plan(self, groups):
        self.order = [j for jobs in groups for _ in range(self.norms) for j in jobs]

    def sp_all(self, sp):
        if self.store is None:
            return
        rows = self.store.rearrange("(c p) d -> p c d", p=P)
        for j in range(self.JOBS):
            sp.wait_ge(self.x_ready, j + 1)
            sp.dma_start(rows[:, 2 * j:2 * j + 2, :], self.x[:, 2 * j:2 * j + 2, :]).then_inc(self.stored, 16)
        sp.wait_ge(self.stored, 16 * self.JOBS)


def down_norm_block(nc, tag, ident, neg_half, x, sources, w_down=None, w_parts=None, loaded=None, prefetch=None, **tail):
    with Scope(nc, tag) as s:
        n_src = len(sources)
        long = n_src > 8
        split_w = w_parts is None
        if split_w:
            w_parts = [s.sb(f"w_part{b}", [P, n_src, D], F32R) for b in range(2)]
        ring = 3
        parts = [[s.sb(f"part{m}{b}", [P, HALF], F32R) for m in range(2)] for b in range(ring)]
        acc = [s.ps(f"acc{h}", [P, 4, D]) for h in range(2)]
        w_high, w_ready = s.sem("w_high"), s.sem("w_ready")
        high, low, used = s.sem("high"), [s.sem(f"low{h}") for h in range(2)], s.sem("used")
        t = NormTail(s, ident, neg_half, x, acc, **tail)
        groups = [(0, 1), (2, 3)] if long else [(0, 1, 2, 3)]
        t.plan(groups)
        units = [(h, n) for h in range(2) for n in range(n_src)]
        rows = [q.shape[0] for q in sources]
        chunks = [slice(n, min(n + 4, n_src)) for n in range(0, n_src, 4)]
        pool_at = {1: 0, 2: 1, 6: 2, 7: 3} if t.norms == 2 else {1: 0, 2: 1}
        pe_at, act_at = {10: 0, 11: 1}, {12: 0, 13: 1}
        with nc.Block() as block:

            @block.sync
            def _(sp):
                if prefetch is not None:
                    prefetch(sp)
                t.sp_all(sp)

            @block.tensor
            def _(pe):
                for u, (h, n) in enumerate(units):
                    pe.wait_ge(low[h], n + 1)
                    if split_w and h == 0 and n % 4 == 0:
                        pe.wait_ge(w_ready, n // 4 + 1)
                    for c in range(4):
                        i = matmul3(pe, acc[h][:, c, :], [q[0:rows[n], c * P:(c + 1) * P] for q in parts[u % ring]],
                                    [w[0:rows[n], n, :] for w in w_parts],
                                    n == 0 and c % 2 == 0, n == n_src - 1 and c % 2 == 1)
                    i.then_inc(used, 1)
                    if long and h == 1 and n in pe_at:
                        t.pe_x(pe, pe_at[n])
                for j in range(2 if long else 0, 4):
                    t.pe_x(pe, j)

            @block.scalar
            def _(act):
                if loaded is not None:
                    act.wait_ge(loaded, 16)
                for u, (h, n) in enumerate(units):
                    if split_w and h == 0 and n % 4 == 0:
                        c, r = chunks[n // 4], rows[n]
                        act.activation(w_parts[0][0:r, c, :], w_down[0:r, c, :], ACT.Copy).then_inc(w_high, 1)
                    if u >= ring:
                        act.wait_ge(used, u - ring + 1)
                    act.activation(parts[u % ring][0][0:rows[n], :], sources[n][:, h * HALF:(h + 1) * HALF], ACT.Copy)\
                        .then_inc(high, 1)
                    if long and h == 1 and n in act_at:
                        t.act_x(act, act_at[n])
                for j in range(2 if long else 0, 4):
                    t.act_x(act, j)

            def low_part(eng, u):
                h, n = units[u]
                q = parts[u % ring]
                eng.wait_ge(high, u + 1)
                eng.tensor_tensor(q[1][0:rows[n], :], sources[n][:, h * HALF:(h + 1) * HALF],
                                  q[0][0:rows[n], :].bitcast(F32), ALU.subtract).then_inc(low[h], 1)

            @block.vector
            def _(dve):
                for u, (h, n) in enumerate(units):
                    if split_w and h == 0 and n % 4 == 0:
                        c, r = chunks[n // 4], rows[n]
                        dve.wait_ge(w_high, n // 4 + 1)
                        dve.tensor_tensor(w_parts[1][0:r, c, :], w_down[0:r, c, :], w_parts[0][0:r, c, :].bitcast(F32),
                                          ALU.subtract).then_inc(w_ready, 1)
                    if h == 0 or not long:
                        low_part(dve, u)
                for jobs in groups:
                    t.dve_jobs(dve, jobs, used, lambda j: n_src * (j // 2 + 1))

            @block.gpsimd
            def _(pool):
                done = 0
                if long:
                    for n in range(n_src):
                        low_part(pool, n_src + n)
                        if n in pool_at:
                            t.pool_norm(pool, done)
                            done += 1
                for e in range(done, len(t.order)):
                    t.pool_norm(pool, e)


NH, DH = 16, 16
ROT = DH // 2
TERMS = 6
QROWS = TERMS * DH
PB = 8
MROWS = 3
GH = 4
VW = 32


def qkv_block(nc, w_loaded, xT, w_in, rope, qk, v, k_stack, prefetch):
    with Scope(nc, "qkv") as s:
        pq = [s.ps(f"qk{b}", [P, HALF]) for b in range(2)]
        pv = [s.ps(f"v{b}", [P, HALF]) for b in range(2)]
        prod = [s.sb(f"prod{b}", [P, 2 * NH, 4]) for b in range(4)]
        projected, taken, v_ones = s.sem("projected"), s.sem("taken"), s.sem("v_ones")
        copied = s.sem("copied")
        with nc.Block() as block:

            @block.sync
            def _(sp):
                prefetch(sp)

            @block.tensor
            def _(pe):
                pe.wait_ge(w_loaded, 16)
                for c in range(NT):
                    if c >= 2:
                        pe.wait_ge(taken, c - 1)
                    for out, cols in ((pq[c % 2][:, :], slice(0, 2 * D)), (pv[c % 2][:, 0:D], slice(2 * D, 3 * D))):
                        for k in range(DK):
                            i = pe.matmul(out, xT[:, k, c * P:(c + 1) * P], w_in[:, k, cols], start=(k == 0),
                                          stop=(k == DK - 1))
                    i.then_inc(projected, 1)

            @block.scalar
            def _(act):
                for c in range(NT):
                    act.wait_ge(projected, c + 1)
                    act.activation(qk[:, c, 0:D], pq[c % 2][:, 0:D], ACT.Copy, scale=DH ** -0.5)
                    act.activation(qk[:, c, D:2 * D], pq[c % 2][:, D:2 * D], ACT.Copy).then_inc(copied, 1)
                    if c == 0:
                        act.wait_ge(v_ones, 1)
                    act.activation(v[:, c, :, 0:DH], pv[c % 2][:, 0:D].rearrange("p (h d) -> p h d", h=NH),
                                   ACT.Copy).then_inc(taken, 1)

            @block.gpsimd
            def _(pool):
                minus_ones = float(np.uint32(0xBF80BF80).view(np.float32))
                pool.memset(k_stack[QROWS:P, :, :].rearrange("p a b -> p (a b)").bitcast(F32), minus_ones)

            @block.vector
            def _(dve):
                dve.memset(v[:, :, :, DH:VW].rearrange("p a b c -> p (a b) c"), 0.0)
                dve.drain()
                dve.memset(v[:, :, :, DH:DH + 1].rearrange("p a b c -> p (a b) c"), 1.0).then_inc(v_ones, 1)
                for c in range(NT):
                    dve.wait_ge(copied, c + 1)
                    dve.drain()
                    pairs = qk[:, c, :].rearrange("p (h j e) -> p h j e", h=2 * NH, e=2)
                    x1, x2 = pairs[:, :, 0:ROT // 2, 0], pairs[:, :, 0:ROT // 2, 1]

                    def table(n):
                        return rope[:, c, n, :].rearrange("p (o j) -> p o j", o=1).to_broadcast((P, 2 * NH, ROT // 2))

                    cos, sin = table(0), table(1)
                    dve.tensor_tensor(prod[0][:, :, :], x1, cos, ALU.mult)
                    dve.tensor_tensor(prod[1][:, :, :], x2, sin, ALU.mult)
                    dve.tensor_tensor(prod[2][:, :, :], x2, cos, ALU.mult)
                    dve.tensor_tensor(prod[3][:, :, :], x1, sin, ALU.mult)
                    dve.drain()
                    dve.tensor_tensor(x1, prod[0][:, :, :], prod[1][:, :, :], ALU.subtract)
                    dve.tensor_tensor(x2, prod[2][:, :, :], prod[3][:, :, :], ALU.add)


def attention_block(nc, ident, identb, qk, v, k_stack, ctx_out):
    with Scope(nc, "attn") as s:
        q_tok = [s.sb(f"q_tok{b}", [P, NT, TERMS, DH], BF16) for b in range(2)]
        k_tok = [s.sb(f"k_tok{b}", [P, NT, TERMS, DH], BF16) for b in range(2)]
        rest = s.sb("rest", [P, NT, DH])
        q_stack = s.sb("q_stack", [P, NH, T], BF16)
        v_group = [s.sb(f"v_group{b}", [P, NT, GH, VW]) for b in range(2)]
        row_max = s.sb("row_max", [P, NT, 2])
        whole_max = s.sb("whole_max", [P, NT])
        max_rest = s.sb("max_rest", [P, NT])
        max_tok = s.sb("max_tok", [P, NT, MROWS], BF16)
        probs = s.sb("probs", [P, PB, T])
        ctx_T = s.sb("ctx_T", [P, T])
        inv = s.sb("inv", [P, 4, GH])
        ps_q = [s.ps(f"rows_q{b}", [P, HALF]) for b in range(2)]
        ps_k = [s.ps(f"rows_k{b}", [P, HALF]) for b in range(3)]
        ps_ctx = [s.ps(f"ctx{b}", [P, HALF]) for b in range(2)]
        ps_turn = s.ps("turn", [P, HALF])
        turn_b = ps_turn[:, :].bitcast(BF16)
        split_q, split_k = s.sem("split_q"), s.sem("split_k")
        q_turned, k_turned = s.sem("q_turned"), s.sem("k_turned")
        q_stacked, k_stacked = s.sem("q_stacked"), s.sem("k_stacked")
        scored_q, maxed = s.sem("scored_q"), s.sem("maxed")
        max_split, max_turned, max_stacked = s.sem("max_split"), s.sem("max_turned"), s.sem("max_stacked")
        scored_k, exped = s.sem("scored_k"), s.sem("exped")
        v_ready, summed, ctx_copied = s.sem("v_ready"), s.sem("summed"), s.sem("ctx_copied")
        ctx_turned, ctx_done = s.sem("ctx_turned"), s.sem("ctx_done")
        NG = NH // GH

        U_MAX, U_Q, U_K = 2, 4, 6

        with nc.Block() as block:

            @block.gpsimd
            def _(pool):
                one = dict(scalar1=1.0, scalar2=0.0, op0=ALU.mult, op1=ALU.add)

                def split(src, tok, places, done):
                    high, middle, low = places

                    def put(part, x):
                        for a, n, step in part:
                            dst = tok[:, :, a:a + (n - 1) * step + 1:step, :]
                            pool.tensor_scalar(dst, x.rearrange("p t (o d) -> p t o d", o=1).to_broadcast((P, NT, n, DH)),
                                               **one)
                        pool.drain()

                    put(high, src)
                    pool.tensor_tensor(rest[:, :, :], src, tok[:, :, high[0][0], :], ALU.subtract)
                    pool.drain()
                    put(middle, rest[:, :, :])
                    pool.tensor_tensor(rest[:, :, :], rest[:, :, :], tok[:, :, middle[0][0], :], ALU.subtract)
                    pool.drain()
                    (a, n, step), = low
                    pool.tensor_scalar(tok[:, :, a, :], rest[:, :, :], **one).then_inc(done, 1)
                    pool.drain()

                for h in range(NH):
                    b = h % 2
                    if h >= 2:
                        pool.wait_ge(q_turned, h - 1)
                        pool.wait_ge(k_turned, h - 1)
                    split(qk[:, :, h * DH:(h + 1) * DH], q_tok[b], ([(0, 2, 1), (5, 1, 1)], [(2, 2, 1)], [(4, 1, 1)]),
                          split_q)
                    split(qk[:, :, D + h * DH:D + (h + 1) * DH], k_tok[b], ([(0, 3, 2)], [(1, 2, 2)], [(5, 1, 1)]),
                          split_k)

            def slots():
                for n in range(NH + GH):
                    yield n, (n if n < NH else None), (n // GH - 1 if n >= GH else None), 2 * (n % GH)

            def weighed_at(unit):
                for n in range(max(0, unit - 6), unit - 3):
                    late = {0: 6, 1: 5, 2: 5}.get(n % (NT * GH), 4)
                    if n == unit - late:
                        yield n // (NT * GH), n // GH % NT, n % GH

            @block.tensor
            def _(pe):
                def turn_q(h):
                    pe.wait_ge(split_q, h + 1)
                    if h == 1:
                        pe.wait_ge(k_stacked, 1)
                    elif h > 1:
                        pe.wait_ge(max_stacked, h - 1)
                    for c in range(NT):
                        i = pe.transpose(turn_b[0:QROWS, c * P:(c + 1) * P],
                                         q_tok[h % 2][:, c, :, :].rearrange("p a b -> p (a b)"), identb[:, :])
                    i.then_inc(q_turned, 1)

                def turn_k(h):
                    pe.wait_ge(split_k, h + 1)
                    pe.wait_ge(q_stacked, h + 1)
                    for c in range(NT):
                        i = pe.transpose(turn_b[0:QROWS, c * P:(c + 1) * P],
                                         k_tok[h % 2][:, c, :, :].rearrange("p a b -> p (a b)"), identb[:, :])
                    i.then_inc(k_turned, 1)

                def turn_max(h):
                    pe.wait_ge(max_split, h + 1)
                    pe.wait_ge(k_stacked, min(h + 2, NH))
                    if h % GH == 0 and h >= 2 * GH:
                        pe.wait_ge(ctx_done, 2 * (h // GH - 1))
                    for c in range(NT):
                        i = pe.transpose(turn_b[0:MROWS, c * P:(c + 1) * P], max_tok[:, c, :], identb[:, :])
                    i.then_inc(max_turned, 1)

                def score_rows_q(h, r):
                    if r == 0:
                        pe.wait_ge(q_stacked, h + 1)
                        pe.wait_ge(k_stacked, h + 1)
                    for b in range(2):
                        n = 2 * (NT * h + r) + b
                        if n >= 2:
                            pe.wait_ge(maxed, n - 1)
                        pe.matmul(ps_q[b][:, :], q_stack[0:QROWS, h, r * P:(r + 1) * P],
                                  k_stack[0:QROWS, h, b * HALF:(b + 1) * HALF], start=True, stop=True)\
                            .then_inc(scored_q, 1)

                def score_rows_k(g, t, j):
                    h = g * GH + j
                    if t == 0:
                        pe.wait_ge(max_stacked, h + 1)
                    for b in range(2):
                        n = 2 * (g * NT * GH + t * GH + j) + b
                        if n >= 3:
                            pe.wait_ge(exped, n - 2)
                        pe.matmul(ps_k[n % 3][:, :], k_stack[0:QROWS + MROWS, h, t * P:(t + 1) * P],
                                  q_stack[0:QROWS + MROWS, h, b * HALF:(b + 1) * HALF], start=True, stop=True)\
                            .then_inc(scored_k, 1)

                def weigh(g, t, j):
                    pe.wait_ge(exped, 2 * (GH * (g * NT + t) + j + 1))
                    if t == 0 and j == 0:
                        pe.wait_ge(v_ready, g + 1)
                        if g >= 1:
                            pe.wait_ge(ctx_copied, g)
                    for b in range(2):
                        i = pe.matmul(ps_ctx[b][j * VW:(j + 1) * VW, :], v_group[g % 2][:, t, j, :],
                                      probs[:, (GH * (g * NT + t) + j) % PB, b * HALF:(b + 1) * HALF],
                                      start=(t == 0), stop=(t == NT - 1))
                    i.then_inc(summed, 1)

                def turn_ctx(g, half):
                    if half == 1:
                        pe.wait_ge(ctx_done, 2 * g + 1)
                    else:
                        pe.wait_ge(ctx_copied, g + 1)
                        if g < NG - 2:
                            pe.wait_ge(k_stacked, GH * (g + 2) + 2)
                        else:
                            pe.wait_ge(max_stacked, NH)
                            if g == NG - 1:
                                pe.wait_ge(ctx_done, 2 * g)
                    for c in range(4):
                        cc = 4 * half + c
                        i = pe.transpose(ps_turn[:, c * P:(c + 1) * P], ctx_T[:, cc * P:(cc + 1) * P], ident[:, :])
                    i.then_inc(ctx_turned, 1)

                turn_q(0)
                turn_k(0)
                for n, head, g, t0 in slots():
                    for u in range(NT):
                        if u == U_MAX and 1 <= n <= NH:
                            turn_max(n - 1)
                        if head is not None:
                            if u == U_Q and head + 1 < NH:
                                turn_q(head + 1)
                            if u == U_K and head + 1 < NH:
                                turn_k(head + 1)
                            score_rows_q(head, u)
                        if g is not None:
                            score_rows_k(g, t0 + u // GH, u % GH)
                            for piece in weighed_at(NT * (n - GH) + u):
                                weigh(*piece)
                        if u == 0 and n > 2 * GH and n % GH == 1:
                            turn_ctx(g - 1, 1)
                    if g is not None and g > 0 and n % GH == 0:
                        turn_ctx(g - 1, 0)
                for unit in range(NT * NH, NT * NH + 4):
                    for piece in weighed_at(unit):
                        weigh(*piece)
                turn_ctx(NG - 1, 0)
                turn_ctx(NG - 1, 1)

            @block.scalar
            def _(act):
                def stack_q(h):
                    act.wait_ge(q_turned, h + 1)
                    act.activation(q_stack[0:QROWS, h, :], turn_b[0:QROWS, :], ACT.Copy).then_inc(q_stacked, 1)

                def stack_k(h):
                    act.wait_ge(k_turned, h + 1)
                    act.activation(k_stack[0:QROWS, h, :], turn_b[0:QROWS, :], ACT.Copy).then_inc(k_stacked, 1)

                def stack_max(h):
                    act.wait_ge(max_turned, h + 1)
                    act.activation(q_stack[QROWS:QROWS + MROWS, h, :], turn_b[0:MROWS, :], ACT.Copy)\
                        .then_inc(max_stacked, 1)

                def copy_ctx(g):
                    act.wait_ge(summed, NT * GH * (g + 1))
                    if g >= 1:
                        act.wait_ge(ctx_turned, 2 * g)
                    for b in range(2):
                        i = act.activation(ctx_T[:, b * HALF:(b + 1) * HALF], ps_ctx[b][:, :], ACT.Copy)
                    i.then_inc(ctx_copied, 1)

                def exp(g, t, j):
                    for b in range(2):
                        n = 2 * (g * NT * GH + t * GH + j) + b
                        if b == 0 and n // 2 >= PB:
                            act.wait_ge(summed, n // 2 - PB + 1)
                        act.wait_ge(scored_k, n + 1)
                        act.activation(probs[:, (GH * (g * NT + t) + j) % PB, b * HALF:(b + 1) * HALF], ps_k[n % 3][:, :],
                                       ACT.Exp).then_inc(exped, 1)

                stack_q(0)
                stack_k(0)
                for n, head, g, t0 in slots():
                    for u in range(NT):
                        if u == U_MAX and 1 <= n <= NH:
                            stack_max(n - 1)
                        if head is not None and head + 1 < NH:
                            if u == U_Q:
                                stack_q(head + 1)
                            if u == U_K:
                                stack_k(head + 1)
                        if g is not None and g > 0 and u == GH and n % GH == 0:
                            copy_ctx(g - 1)
                        if g is not None:
                            exp(g, t0 + u // GH, u % GH)
                copy_ctx(NG - 1)

            @block.vector
            def _(dve):
                def row_maxima(h, r):
                    for b in range(2):
                        n = 2 * (NT * h + r) + b
                        dve.wait_ge(scored_q, n + 1)
                        dve.tensor_reduce(row_max[:, r, b:b + 1], ps_q[b][:, :], axis=AX, op=ALU.max)\
                            .then_inc(maxed, 1)

                def split_maxima(h):
                    dve.drain()
                    if h >= 1:
                        dve.wait_ge(max_turned, h)
                    dve.tensor_tensor(whole_max[:, :], row_max[:, :, 0], row_max[:, :, 1], ALU.max)
                    dve.drain()
                    dve.tensor_copy(max_tok[:, :, 0], whole_max[:, :])
                    dve.drain()
                    dve.tensor_tensor(max_rest[:, :], whole_max[:, :], max_tok[:, :, 0], ALU.subtract)
                    dve.drain()
                    dve.tensor_copy(max_tok[:, :, 1], max_rest[:, :])
                    dve.drain()
                    dve.tensor_tensor(max_tok[:, :, 2], max_rest[:, :], max_tok[:, :, 1], ALU.subtract)\
                        .then_inc(max_split, 1)

                def values(g):
                    if g >= 2:
                        dve.wait_ge(summed, NT * GH * (g - 1))
                    dve.tensor_copy(v_group[g % 2][:, :, :, :], v[:, :, g * GH:(g + 1) * GH, :]).then_inc(v_ready, 1)

                def norm_ctx(g, half):
                    dve.wait_ge(ctx_turned, 2 * g + half + 1)
                    view = ps_turn[:, :].rearrange("p (c j w) -> p c j w", c=4, j=GH)
                    dve.reciprocal(inv[:, :, :], view[:, :, :, DH])
                    dve.drain()
                    for c in range(4):
                        out = ctx_out[:, 4 * half + c, g * GH * DH:(g + 1) * GH * DH].rearrange(
                            "p (j d) -> p j d", j=GH)
                        i = dve.tensor_tensor(out, view[:, c, :, 0:DH], col(inv[:, c, :], DH), ALU.mult)
                    i.then_inc(ctx_done, 1)

                values(0)
                values(1)
                for n, head, g, t0 in slots():
                    for u in range(NT):
                        if head is not None:
                            row_maxima(head, u)
                        if u == 0 and n > 2 * GH and n % GH == 1:
                            norm_ctx(g - 1, 1)
                            if g + 1 < NG:
                                values(g + 1)
                    if head is not None:
                        split_maxima(head)
                    if g is not None and g > 0 and n % GH == 0:
                        norm_ctx(g - 1, 0)
                norm_ctx(NG - 1, 0)
                norm_ctx(NG - 1, 1)


def turn_block(nc, tag, ident, src, dst):
    with Scope(nc, tag) as s:
        turned = [s.ps(f"turned{k}", [P, T]) for k in range(DK)]
        turn_done = s.sem("turn_done")
        with nc.Block() as block:

            @block.tensor
            def _(pe):
                for h in range(2):
                    for c in range(4 * h, 4 * h + 4):
                        for k in range(DK):
                            i = pe.transpose(turned[k][:, c * P:(c + 1) * P], src[:, c, k * P:(k + 1) * P], ident[:, :])
                    i.then_inc(turn_done, 1)

            @block.scalar
            def _(act):
                for h in range(2):
                    act.wait_ge(turn_done, h + 1)
                    for k in range(DK):
                        act.activation(dst[:, k, h * HALF:(h + 1) * HALF], turned[k][:, h * HALF:(h + 1) * HALF],
                                       ACT.Copy)


NE = 8
FE = 256
FK = FE // P
NL, RANK = 2, 64
CENTER = 1.0 / math.e
LOWER = 0.5 - math.log(4.0 / 3.0)
Z_LOWER = math.log(LOWER / (1.0 - LOWER))
Z_UPPER = 2.0 ** -23


def rank_mask(dve, scores, mask, greater, same, earlier, n, top):
    a = scores.shape[1]
    other = scores.rearrange("p a (o j) -> p a o j", o=1).to_broadcast((P, a, n, n))
    own = scores.rearrange("p a (i o) -> p a i o", o=1).to_broadcast((P, a, n, n))
    dve.tensor_tensor(greater, other, own, ALU.is_gt)
    dve.tensor_tensor(same, other, own, ALU.is_equal)
    dve.drain()
    dve.tensor_tensor(same, same, earlier.rearrange("p (o i) j -> p o i j", o=1).to_broadcast((P, a, n, n)), ALU.mult)
    dve.drain()
    dve.tensor_tensor(greater, greater, same, ALU.add)
    dve.drain()
    dve.tensor_reduce(mask, greater, axis=AX, op=ALU.add)
    dve.drain()
    dve.tensor_scalar(mask, mask, float(top), None, ALU.is_lt)
    dve.drain()


class LowRank:

    def __init__(self, s, ident, lora, rings, w_down, Wg, Wu, Wd):
        self.ident, self.lora, self.rings, self.w_down, self.W = ident, lora, rings, w_down, (Wg, Wu, Wd)
        self.a_sb = s.sb("a", [P, 3, NL, FK, RANK])
        self.b_sb = s.sb("b", [RANK, 3, NL, FE])
        self.a_T = s.sb("a_T", [RANK, 3, NL, FK, P])
        self.product = [s.sb(f"product_sb{b}", [P, FK, FE]) for b in range(2)]
        self.a_loaded, self.w_loaded, self.a_turned, self.copied, self.producted, self.evacuated, self.added = (
            s.sem(name) for name in ("a_loaded", "w_loaded", "a_turned", "copied", "producted", "evacuated", "added"))
        self.jobs = [(m, e) for e in range(NL) for m in range(3)]

    def open(self, s):
        self.ps_t = [s.ps(f"a_turned{b}", [RANK, FK, P]) for b in range(2)]
        self.ps_w = [s.ps(f"product{b}", [P, FK, FE]) for b in range(2)]

    def sp(self, sp):
        for m, (A, B) in enumerate(self.lora):
            for e in range(NL):
                sp.dma_start(self.a_sb[:, m, e, :, :], A[e].rearrange("(k p) r -> p k r", p=P)).then_inc(self.a_loaded, 16)
                sp.dma_start(self.b_sb[:, m, e, :], B[e]).then_inc(self.a_loaded, 16)
        Wg, Wu, Wd = self.W
        for e in range(NL):
            for r, W in zip(self.rings, (Wg, Wu)):
                sp.dma_start(r[e][:, :, :], W[e].rearrange("(k p) f -> p k f", p=P)).then_inc(self.w_loaded, 16)
        sp.dma_start(self.w_down[:, :, :].rearrange("p (e k) d -> p e k d", e=NE),
                     Wd.rearrange("e (k p) d -> p e k d", p=P)).then_inc(self.w_loaded, 16)

    def pe(self, pe):
        pe.wait_ge(self.a_loaded, 16 * 4 * len(self.lora))

        def turn(n):
            m, e = self.jobs[n]
            if n >= 2:
                pe.wait_ge(self.copied, n - 1)
            for k in range(FK):
                i = pe.transpose(self.ps_t[n % 2][:, k, :], self.a_sb[:, m, e, k, :], self.ident[:, :])
            i.then_inc(self.a_turned, 1)

        turn(0)
        for n, (m, e) in enumerate(self.jobs):
            if n + 1 < len(self.jobs):
                turn(n + 1)
            pe.wait_ge(self.copied, n + 1)
            if n >= 2:
                pe.wait_ge(self.evacuated, n - 1)
            for k in range(FK):
                i = pe.matmul(self.ps_w[n % 2][:, k, :], self.a_T[:, m, e, k, :], self.b_sb[:, m, e, :], start=True,
                              stop=True)
            i.then_inc(self.producted, 1)

    def act(self, act, jobs):

        def copy(n):
            m, e = self.jobs[n]
            act.wait_ge(self.a_turned, n + 1)
            act.activation(self.a_T[:, m, e, :, :], self.ps_t[n % 2][:, :, :], ACT.Copy).then_inc(self.copied, 1)

        for n in jobs:
            if n == 0:
                copy(0)
            if n + 1 < len(self.jobs):
                copy(n + 1)
            act.wait_ge(self.producted, n + 1)
            if n >= 2:
                act.wait_ge(self.added, n - 1)
            act.activation(self.product[n % 2][:, :, :], self.ps_w[n % 2][:, :, :], ACT.Copy).then_inc(self.evacuated, 1)

    def pool(self, pool):
        pool.wait_ge(self.w_loaded, 16 * (2 * NL + 1))
        for n, (m, e) in enumerate(self.jobs):
            pool.wait_ge(self.evacuated, n + 1)
            dst = self.rings[m][e][:, :, :] if m < 2 else self.w_down[:, FK * e:FK * e + FK, :]
            pool.tensor_tensor(dst, dst, self.product[n % 2][:, :, :], ALU.add).then_inc(self.added, 1)


def golden_router_block(nc, ident, Wr, temperature, earlier, x_parts, w_dram, low_rank):
    with Scope(nc, "gold") as s:
        low_rank.open(s)
        wr = s.sb("wr", [P, DK, NE])
        temp = s.sb("temp", [P, 1])
        wr_parts = [s.sb(f"wr_part{q}", [P, DK, NE], F32R) for q in range(2)]
        wr_split, rows_scored, rows_copied = s.sem("wr_split"), s.sem("rows_scored"), s.sem("rows_copied")
        order = s.sb("order", [P, NE, NE])
        inv_temp = s.sb("inv_temp", [P, 1])
        z = s.sb("z", [P, NT, NE])
        ez = s.sb("ez", [P, NT, NE])
        dist = s.sb("dist", [P, NT, NE])
        w = s.sb("w", [P, NT, NE])
        fb = s.sb("fb", [P, NT, NE])
        zone = s.sb("zone", [P, NT, NE])
        mask = s.sb("mask", [P, NT, NE])
        total = s.sb("total", [P, NT])
        none = s.sb("none", [P, NT])
        greater = s.sb("greater", [P, NT, NE, NE])
        same = s.sb("same", [P, NT, NE, NE])
        w_rows = s.sb("w_rows", [NE, T])
        logits = s.ps("logits", [P, NT, NE])
        w_turned = s.ps("w_turned", [NE, T])
        turned_halves = [w_turned[:, h * HALF:(h + 1) * HALF] for h in range(2)]
        loaded, scored, z_ready, e_ready = s.sem("loaded"), s.sem("scored"), s.sem("z_ready"), s.sem("e_ready")
        d_ready, f_ready, w_ready = s.sem("d_ready"), s.sem("f_ready"), s.sem("w_ready")
        turned, rows_ready, stored = s.sem("turned"), s.sem("rows_ready"), s.sem("stored")
        flat = "p a b -> p (a b)"
        with nc.Block() as block:

            @block.sync
            def _(sp):
                sp.dma_start(wr[:, :, :], Wr.rearrange("(k p) n -> p k n", p=P)).then_inc(loaded, 16)
                sp.dma_start(temp[:, :], temperature.rearrange("(o n) -> o n", o=1).to_broadcast((P, 1)))\
                    .then_inc(loaded, 16)
                sp.dma_start(order[:, :, :], earlier[0:NE, 0:NE].rearrange("(o a) b -> o a b", o=1).to_broadcast((P, NE, NE)))\
                    .then_inc(loaded, 16)
                sp.wait_ge(rows_ready, 1)
                sp.dma_start(w_dram, w_rows[:, :]).then_inc(stored, 16)
                sp.wait_ge(stored, 16)

            @block.tensor
            def _(pe):
                pe.wait_ge(wr_split, 1)
                score_tokens(pe, x_parts, wr_parts, w_rows, ident, turned_halves, logits, rows_scored, rows_copied)\
                    .then_inc(scored, 1)
                low_rank.pe(pe)
                pe.wait_ge(w_ready, 1)
                for c in range(NT):
                    i = pe.transpose(w_turned[:, c * P:(c + 1) * P], w[:, c, :], ident[:, :])
                i.then_inc(turned, 1)

            @block.gpsimd
            def _(pool):
                low_rank.pool(pool)

            @block.scalar
            def _(act):
                copy_rows(act, w_rows, turned_halves, rows_scored, rows_copied)
                act.wait_ge(z_ready, 1)
                act.activation(ez[:, :, :], z[:, :, :], ACT.Exp, scale=-1.0).then_inc(e_ready, 1)
                low_rank.act(act, range(0, 2))
                act.wait_ge(d_ready, 1)
                act.activation(w[:, :, :], dist[:, :, :], ACT.Exp, scale=-1.0 / 0.1)
                act.activation(fb[:, :, :], dist[:, :, :], ACT.Exp, scale=-1.0 / 0.3).then_inc(f_ready, 1)
                low_rank.act(act, range(2, 6))
                act.wait_ge(turned, 1)
                act.activation(w_rows[:, :], w_turned[:, :], ACT.Copy).then_inc(rows_ready, 1)

            @block.vector
            def _(dve):
                dve.wait_ge(loaded, 48)
                split_small(dve, [q[:, :, :] for q in wr_parts], wr[:, :, :]).then_inc(wr_split, 1)
                dve.reciprocal(inv_temp[:, :], temp[:, :])
                dve.wait_ge(scored, 1)
                dve.drain()
                dve.tensor_scalar(z[:, :, :], logits[:, :, :], inv_temp[:, 0:1], -80.0, ALU.mult, ALU.max).then_inc(z_ready, 1)
                dve.drain()
                dve.tensor_scalar(zone[:, :, :], z[:, :, :], Z_LOWER, None, ALU.is_ge)
                dve.tensor_scalar(mask[:, :, :], z[:, :, :], Z_UPPER, None, ALU.is_le)
                dve.drain()
                dve.tensor_tensor(zone[:, :, :], zone[:, :, :], mask[:, :, :], ALU.mult)
                dve.wait_ge(e_ready, 1)
                dve.tensor_scalar(ez[:, :, :], ez[:, :, :], 1.0, None, ALU.add)
                dve.drain()
                dve.reciprocal(ez[:, :, :].rearrange(flat), ez[:, :, :].rearrange(flat))
                dve.drain()
                dve.tensor_scalar(ez[:, :, :], ez[:, :, :], CENTER, None, ALU.subtract)
                dve.drain()
                dve.tensor_scalar(dist[:, :, :], ez[:, :, :], -1.0, None, ALU.mult)
                dve.drain()
                dve.tensor_tensor(dist[:, :, :], dist[:, :, :], ez[:, :, :], ALU.max).then_inc(d_ready, 1)
                dve.wait_ge(f_ready, 1)
                dve.tensor_tensor(w[:, :, :], w[:, :, :], zone[:, :, :], ALU.mult)
                dve.drain()
                dve.tensor_reduce(total[:, :], w[:, :, :], axis=AX, op=ALU.add)
                dve.drain()
                dve.tensor_scalar(none[:, :], total[:, :], 1e-8, None, ALU.is_lt)
                rank_mask(dve, fb[:, :, :], mask[:, :, :], greater[:, :, :, :], same[:, :, :, :], order[:, :, :], NE, 2)

                def normalise(a):
                    dve.tensor_reduce(total[:, :], a, axis=AX, op=ALU.add)
                    dve.drain()
                    dve.tensor_scalar(total[:, :], total[:, :], 1e-8, None, ALU.max)
                    dve.drain()
                    dve.reciprocal(total[:, :], total[:, :])
                    dve.drain()
                    return dve.tensor_tensor(a, a, col(total[:, :], NE), ALU.mult)

                dve.tensor_tensor(fb[:, :, :], fb[:, :, :], mask[:, :, :], ALU.mult)
                dve.drain()
                normalise(fb[:, :, :])
                dve.drain()
                dve.tensor_tensor(fb[:, :, :], fb[:, :, :], w[:, :, :], ALU.subtract)
                dve.drain()
                dve.tensor_tensor(fb[:, :, :], fb[:, :, :], col(none[:, :], NE), ALU.mult)
                dve.drain()
                dve.tensor_tensor(w[:, :, :], w[:, :, :], fb[:, :, :], ALU.add)
                dve.drain()
                normalise(w[:, :, :]).then_inc(w_ready, 1)


def experts_block(nc, rings, x_parts, w_dram, Wg, Wu, mids):
    with Scope(nc, "moe0") as s:
        w_parts = [[[s.sb(f"w_part{m}{b}{q}", [P, DK, FE], F32R) for q in range(2)] for b in range(2)] for m in range(2)]
        weight = [s.sb(f"weight{b}", [P, T]) for b in range(2)]
        gated = [s.sb(f"gated{b}", [P, HALF]) for b in range(2)]
        hidden = [s.sb(f"hidden{b}", [P, HALF]) for b in range(2)]
        ps_g = [s.ps(f"gate{b}", [P, HALF]) for b in range(2)]
        ps_u = [s.ps(f"up{b}", [P, HALF]) for b in range(2)]
        w_loaded = [s.sem(f"w_loaded{b}") for b in range(2)]
        r_loaded = [s.sem(f"r_loaded{b}") for b in range(2)]
        w_high, w_split = s.sem("w_high"), s.sem("w_split")
        gate_done, up_done = s.sem("gate_done"), s.sem("up_done")
        gate_free, up_free = s.sem("gate_free"), s.sem("up_free")
        hidden_free = s.sem("hidden_free")
        U = 2 * FK

        def over_experts(eng, expert):
            expert(0, 0, 0)
            with eng.Fori(0, NE // 2 - 1) as i:
                expert(2 * i + 1, i, 1)
                expert(2 * i + 2, i + 1, 0)
            expert(NE - 1, NE // 2 - 1, 1)

        def is_first(e):
            return isinstance(e, int) and e == 0

        def is_last(e):
            return isinstance(e, int) and e == NE - 1

        with nc.Block() as block:

            @block.sync
            def _(sp):
                for b in range(2):
                    sp.dma_start(weight[b][:, :], w_dram[b:b + 1, :].to_broadcast((P, T))).then_inc(r_loaded[b], 16)
                with sp.Fori(0, NE // 2 - 1) as i:
                    for b in range(2):
                        sp.wait_ge(w_split, 2 * i + b + 1)
                        for r, W in zip(rings, (Wg, Wu)):
                            src = W[bass.ds(2 * i + b + 2, 1), :, :].rearrange("o (k p) f -> p (o k) f", p=P)
                            sp.dma_start(r[b][:, :, :], src).then_inc(w_loaded[b], 16)
                        sp.wait_ge(hidden_free, U * (2 * i + b + 1))
                        sp.dma_start(weight[b][:, :], w_dram[bass.ds(2 * i + b + 2, 1), :].to_broadcast((P, T)))\
                            .then_inc(r_loaded[b], 16)

            @block.tensor
            def _(pe):
                def expert(e, pair, b):
                    pe.wait_ge(w_split, e + 1)
                    for u in range(U):
                        f, half = divmod(u, 2)
                        for m, ps, free, done in ((0, ps_g, gate_free, gate_done), (1, ps_u, up_free, up_done)):
                            if not (is_first(e) and u < 2):
                                pe.wait_ge(free, U * e + u - 1)
                            for k in range(DK):
                                i = matmul3(pe, ps[u % 2][:, :], [w[:, k, f * P:(f + 1) * P] for w in w_parts[m][b]],
                                            [q[:, k, half * HALF:(half + 1) * HALF] for q in x_parts],
                                            k == 0, k == DK - 1)
                            i.then_inc(done, 1)

                over_experts(pe, expert)

            @block.scalar
            def _(act):
                def high(b):
                    for m in range(2):
                        i = act.activation(w_parts[m][b][0][:, :, :], rings[m][b][:, :, :], ACT.Copy)
                    i.then_inc(w_high, 1)

                def expert(e, pair, b):
                    if is_first(e):
                        high(0)
                        high(1)
                    elif not is_last(e):
                        act.wait_ge(w_loaded[1 - b], 32 * (pair + b))
                        act.wait_ge(up_done, U * e)
                        high(1 - b)
                    for u in range(U):
                        if not (is_first(e) and u < 2):
                            act.wait_ge(up_free, U * e + u - 1)
                        act.wait_ge(gate_done, U * e + u + 1)
                        act.activation(gated[u % 2][:, :], ps_g[u % 2][:, :], ACT.Silu).then_inc(gate_free, 1)

                over_experts(act, expert)

            @block.vector
            def _(dve):
                def low(e, b):
                    dve.wait_ge(w_high, e + 1)
                    for m in range(2):
                        i = dve.tensor_tensor(w_parts[m][b][1][:, :, :], rings[m][b][:, :, :],
                                              w_parts[m][b][0][:, :, :].bitcast(F32), ALU.subtract)
                    i.then_inc(w_split, 1)

                def expert(e, pair, b):
                    if is_first(e):
                        low(0, 0)
                        low(1, 1)
                    elif not is_last(e):
                        low(e + 1, 1 - b)
                    for u in range(U):
                        if not (is_first(e) and u < 2):
                            dve.wait_ge(hidden_free, U * e + u - 1)
                        dve.wait_ge(gate_free, U * e + u + 1)
                        dve.wait_ge(up_done, U * e + u + 1)
                        dve.tensor_tensor(hidden[u % 2][:, :], gated[u % 2][:, :], ps_u[u % 2][:, :], ALU.mult)\
                            .then_inc(up_free, 1)

                over_experts(dve, expert)

            @block.gpsimd
            def _(pool):
                def expert(e, pair, b):
                    pool.wait_ge(r_loaded[b], 16 * pair + 16)
                    for u in range(U):
                        f, half = divmod(u, 2)
                        pool.wait_ge(up_free, U * e + u + 1)
                        cols = slice(half * HALF, (half + 1) * HALF)
                        out = mids[:, bass.ds(FK * e + f, 1), cols].rearrange("p o t -> p (o t)")
                        pool.tensor_tensor(out, hidden[u % 2][:, :], weight[b][:, cols], ALU.mult).then_inc(hidden_free, 1)

                over_experts(pool, expert)


LH = 16
HD = 128
TAPS = 4


def decay_block(nc, ident, Wb, bb, x_parts, decay_dram, cols, prefetch):
    with Scope(nc, "decay") as s:
        wb = s.sb("wb", [P, DK, LH])
        wb_parts = [s.sb(f"wb_part{q}", [P, DK, LH], F32R) for q in range(2)]
        wb_split = s.sem("wb_split")
        bias = s.sb("bias", [LH, 1])
        z = s.sb("z", [LH, T])
        soft = s.sb("soft", [LH, T])
        log_b = s.sb("log_b", [LH, T])
        total = s.sb("total", [LH, T])
        one = s.sb("one", [LH, T])
        ps_z = s.ps("z_sum", [LH, T])
        ps_c = s.ps("turned", [P, 2, NT, LH])
        loaded, z_done, z_ready = s.sem("loaded"), s.sem("z_done"), s.sem("z_ready")
        soft_ready, sums_ready = s.sem("soft_ready"), s.sem("sums_ready")
        turned, stored, acts, one_ready = s.sem("turned"), s.sem("stored"), s.sem("acts"), s.sem("one_ready")
        with nc.Block() as block:

            @block.sync
            def _(sp):
                sp.dma_start(wb[:, :, :], Wb.rearrange("(k p) h -> p k h", p=P)).then_inc(loaded, 16)
                sp.dma_start(bias[:, :], bb.rearrange("(h o) -> h o", o=1)).then_inc(loaded, 16)
                prefetch(sp)
                sp.wait_ge(sums_ready, 1)
                sp.dma_start(decay_dram, total[:, :]).then_inc(stored, 16)
                sp.wait_ge(stored, 16)

            @block.tensor
            def _(pe):
                pe.wait_ge(wb_split, 1)
                for half in range(2):
                    for k in range(DK):
                        i = matmul3(pe, ps_z[:, half * HALF:(half + 1) * HALF], [q[:, k, :] for q in wb_parts],
                                    [q[:, k, half * HALF:(half + 1) * HALF] for q in x_parts], k == 0, k == DK - 1)
                i.then_inc(z_done, 1)
                pe.wait_ge(sums_ready, 1)
                for n, src in enumerate((total, log_b)):
                    for c in range(NT):
                        i = pe.transpose(ps_c[:, n, c, :], src[:, c * P:(c + 1) * P], ident[0:LH, 0:LH])
                i.then_inc(turned, 1)

            @block.scalar
            def _(act):
                act.wait_ge(loaded, 32)
                act.wait_ge(z_done, 1)
                act.activation(z[:, :], ps_z[:, :], ACT.Identity, bias=bias[:, 0:1]).then_inc(z_ready, 1)
                act.wait_ge(z_ready, 1)
                act.activation(soft[:, :], z[:, :], ACT.Abs).then_inc(acts, 1)
                act.wait_ge(acts, 1)
                act.activation(soft[:, :], soft[:, :], ACT.Exp, scale=-1.0).then_inc(acts, 1)
                act.wait_ge(acts, 2)
                act.wait_ge(one_ready, 1)
                act.activation(soft[:, :], soft[:, :], ACT.Ln, bias=one[:, 0:1]).then_inc(soft_ready, 1)

            @block.vector
            def _(dve):
                dve.memset(one[:, :], 1.0).then_inc(one_ready, 1)
                dve.wait_ge(loaded, 32)
                split_small(dve, [q[:, :, :] for q in wb_parts], wb[:, :, :]).then_inc(wb_split, 1)
                dve.wait_ge(z_ready, 1)
                dve.tensor_scalar(log_b[:, :], z[:, :], 0.0, None, ALU.min)
                dve.wait_ge(soft_ready, 1)
                dve.drain()
                dve.tensor_tensor(log_b[:, :], log_b[:, :], soft[:, :], ALU.subtract)
                dve.drain()
                dve.tensor_tensor(z[:, :], log_b[:, :], z[:, :], ALU.subtract)
                dve.drain()
                for c in range(NT):
                    i = dve.tensor_tensor_scan(total[:, c * P:(c + 1) * P], one[:, 0:P], z[:, c * P:(c + 1) * P], 0.0,
                                               ALU.mult, ALU.add)
                i.then_inc(sums_ready, 1)
                dve.wait_ge(turned, 1)
                dve.tensor_copy(cols[:, :, :, :], ps_c[:, :, :, :])


def linear_attention_block(nc, ident, neg_half, w, xT, x_parts, decay_dram, cols, norm_row, norm_col, gated_out):
    with Scope(nc, "lin") as s:
        Wq, Wk, Wv, Wg = w["q"], w["k"], w["v"], w["gate"]
        wq, wk, wv, wg = ([s.sb(f"w_{m}{b}", [P, DK, HD]) for b in range(2)] for m in ("q", "k", "v", "gate"))
        parts = {m: [s.sb(f"part_{m}{p}", [P, DK, HD], F32R) for p in range(2)] for m in ("q", "k", "gate")}
        taps = [s.sb(f"taps{b}", [P, 2, TAPS + 1]) for b in range(2)]
        decay = [s.sb(f"decay{b}", [P, T]) for b in range(2)]
        hcol = [s.sb(f"hcol{b}", [P, 2, NT]) for b in range(2)]
        conv = [s.sb(f"conv_{m}", [P, T]) for m in "qk"]
        stats = s.sb("stats", [P, 2, NT, 6])
        mean_var = s.sb("mean_var", [P, 2, NT, 2])
        var_eps = s.sb("var_eps", [P, 2, NT])
        rstd = s.sb("rstd", [P, 2, NT])
        k_shift = s.sb("k_shift", [P, NT])
        normed = [s.sb(f"normed_{m}", [P, NT, HD]) for m in "qk"]
        k_rows = s.sb("k_rows", [P, NT, HD])
        q_T = s.sb("q_T", [P, T])
        k_T = s.sb("k_T", [P, T])
        q_dec = s.sb("q_dec", [P, T])
        v_rows = [s.sb(f"v_rows{b}", [P, NT, HD]) for b in range(2)]
        v_dec = s.sb("v_dec", [P, NT, HD])
        gate = s.sb("gate", [P, T])
        arg = s.sb("arg", [P, NT, P])
        mix = s.sb("mix", [P, NT, P])
        e_dec = s.sb("e_dec", [P, T])
        probs = s.sb("probs", [P, NT, P])
        state = s.sb("state", [P, NT, HD])
        ps = [s.ps(f"pair{n}", [P, T]) for n in range(4)]
        tiled = [p[:, :].rearrange("p (c d) -> p c d", c=NT) for p in ps]
        sem = s.sem
        qk_loaded, v_loaded, g_loaded, d_loaded = ([sem(f"{m}_loaded{b}") for b in range(2)] for m in ("qk", "v", "g", "d"))
        q_high, k_high, g_high = (sem(f"{m}_high") for m in "qkg")
        q_split, k_split, g_split = (sem(f"{m}_split") for m in "qkg")
        q_projected, k_projected, v_projected, g_projected = (sem(f"{m}_projected") for m in "qkvg")
        q_tapped, q_conved, k_conved, q_acted, k_acted = (
            sem(x) for x in ("q_tapped", "q_conved", "k_conved", "q_acted", "k_acted"))
        q_rowed, k_rowed = sem("q_rowed"), sem("k_rowed")
        var_ready, rstd_ready, shift_ready = sem("var_ready"), sem("rstd_ready"), sem("shift_ready")
        q_normed, k_normed, k_rows_done = sem("q_normed"), sem("k_normed"), sem("k_rows_done")
        q_turned, k_turned, q_T_done, k_T_done = sem("q_turned"), sem("k_turned"), sem("q_T_done"), sem("k_T_done")
        v_copied, v_dec_done, g_acted = sem("v_copied"), sem("v_dec_done"), sem("g_acted")
        hcol_ready = sem("hcol_ready")
        arg_ready, mix_exped, masked, e_dec_done, q_dec_done = (
            sem(x) for x in ("arg_ready", "mix_exped", "masked", "e_dec_done", "q_dec_done"))
        scored, kv_done, probs_done, states_done = (sem(x) for x in ("scored", "kv_done", "probs_done", "states_done"))
        o_done, gated = sem("o_done"), sem("gated")

        def pipeline(eng, step):
            step(0, 0, True, False, False)
            step(0, 1, True, True, False)
            for b in range(2):
                step(1, b, True, True, True)
            with eng.Fori(2, LH // 2) as i:
                for b in range(2):
                    step(i, b, True, True, True)
            step(LH // 2, 0, False, True, True)
            step(LH // 2, 1, False, False, True)

        def wait_for(eng, semaphore, count):
            if not (isinstance(count, int) and count < 1):
                eng.wait_ge(semaphore, count)

        def loads(i, b, lag):
            return i + (b - lag - (b - lag) % 2) // 2 + 1

        with nc.Block() as block:

            @block.sync
            def _(sp):
                def head(m, b, reuse):
                    def cols_of(W):
                        view = W.rearrange("(k p) (h c) -> p k h c", p=P, c=HD)
                        return view[:, :, bass.ds(m, 1), :].rearrange("p k o c -> p k (o c)")

                    if reuse:
                        sp.wait_ge(k_split, m - 1)
                        sp.wait_ge(k_conved, m - 1)
                    sp.dma_start(wq[b][:, :, :], cols_of(Wq)).then_inc(qk_loaded[b], 16)
                    sp.dma_start(wk[b][:, :, :], cols_of(Wk)).then_inc(qk_loaded[b], 16)
                    for j, (cw, cb) in enumerate((w["q_taps"], w["k_taps"])):
                        rows = cw.rearrange("(h p) t -> p h t", p=P)[:, bass.ds(m, 1), :].rearrange("p o t -> p (o t)")
                        sp.dma_start(taps[b][:, j, 0:TAPS], rows).then_inc(qk_loaded[b], 16)
                        bias = cb.rearrange("(h p o) -> p h o", p=P, o=1)[:, bass.ds(m, 1), :]
                        sp.dma_start(taps[b][:, j, TAPS:TAPS + 1], bias.rearrange("p a o -> p (a o)"))\
                            .then_inc(qk_loaded[b], 16)
                    if reuse:
                        sp.wait_ge(v_projected, m - 1)
                    sp.dma_start(wv[b][:, :, :], cols_of(Wv)).then_inc(v_loaded[b], 16)
                    if reuse:
                        sp.wait_ge(e_dec_done, m - 1)
                    sp.dma_start(decay[b][:, :], decay_dram[bass.ds(m, 1), :].to_broadcast((P, T))).then_inc(d_loaded[b], 16)
                    if reuse:
                        sp.wait_ge(g_split, m - 1)
                    sp.dma_start(wg[b][:, :, :], cols_of(Wg)).then_inc(g_loaded[b], 16)

                for b in range(2):
                    head(b, b, False)
                with sp.Fori(1, LH // 2) as i:
                    for b in range(2):
                        head(2 * i + b, b, True)

            @block.tensor
            def _(pe):
                def project(weights, out, done):
                    for half in range(2):
                        cols = slice(half * HALF, (half + 1) * HALF)
                        for k in range(DK):
                            i = matmul3(pe, out[:, cols], [q[:, k, :] for q in weights],
                                        [q[:, k, cols] for q in x_parts], k == 0, k == DK - 1)
                    i.then_inc(done, 1)

                def turn(out, src, done):
                    for c in range(NT):
                        i = pe.transpose(out[:, c * P:(c + 1) * P], src(c), ident[:, :])
                    i.then_inc(done, 1)

                def step(i_, b, a0, a1, a2):
                    n = 2 * i_ + b
                    if a1:
                        pe.wait_ge(v_loaded[1 - b], 16 * loads(i_, b, 1))
                        pe.wait_ge(q_conved, n)
                        for c in range(NT):
                            for k in range(DK):
                                i = pe.matmul(tiled[0][:, c, :], xT[:, k, c * P:(c + 1) * P], wv[1 - b][:, k, :],
                                              start=(k == 0), stop=(k == DK - 1))
                        i.then_inc(v_projected, 1)
                        pe.wait_ge(q_acted, n)
                        if a2:
                            pe.wait_ge(k_T_done, n - 1)
                        turn(ps[1], lambda c: conv[0][:, c * P:(c + 1) * P], q_rowed)
                        pe.wait_ge(k_acted, n)
                        turn(ps[2], lambda c: conv[1][:, c * P:(c + 1) * P], k_rowed)
                    if a2:
                        pe.wait_ge(g_split, n - 1)
                        wait_for(pe, gated, n - 2)
                        project(parts["gate"], ps[3], g_projected)
                        if a1:
                            pe.wait_ge(v_copied, n)
                        else:
                            wait_for(pe, probs_done, n - 2)
                        pe.wait_ge(q_T_done, n - 1)
                        pe.wait_ge(k_T_done, n - 1)
                        for c in range(NT):
                            cols = slice(c * P, (c + 1) * P)
                            i = pe.matmul(ps[0][:, cols], k_T[:, cols], q_T[:, cols], start=True, stop=True)
                        i.then_inc(scored, 1)
                        pe.wait_ge(g_acted, n - 1)
                        pe.wait_ge(k_rows_done, n - 1)
                        pe.wait_ge(v_dec_done, n - 1)
                        for c in range(NT - 1):
                            i = pe.matmul(tiled[3][:, c, :], k_rows[:, c, :], v_dec[:, c, :], start=True, stop=True)
                        i.then_inc(kv_done, 1)
                    if a0:
                        pe.wait_ge(q_split, n + 1)
                        if a2:
                            pe.wait_ge(probs_done, n - 1)
                        elif a1:
                            pe.wait_ge(v_copied, n)
                        project(parts["q"], ps[0], q_projected)
                    if a1:
                        pe.wait_ge(q_normed, n)
                        if a2:
                            pe.wait_ge(states_done, n - 1)
                        turn(ps[3], lambda c: normed[0][:, c, :], q_turned)
                        pe.wait_ge(k_normed, n)
                        turn(ps[1], lambda c: normed[1][:, c, :], k_turned)
                    if a0:
                        pe.wait_ge(k_split, n + 1)
                        project(parts["k"], ps[2], k_projected)
                    if a2:
                        pe.wait_ge(probs_done, n - 1)
                        pe.wait_ge(states_done, n - 1)
                        pe.wait_ge(q_dec_done, n - 1)
                        if a1:
                            pe.wait_ge(q_T_done, n)
                        for c in range(NT):
                            cols = slice(c * P, (c + 1) * P)
                            i = pe.matmul(ps[3][:, cols], v_rows[b][:, c, :], probs[:, c, :], start=True, stop=(c == 0))
                            if c:
                                i = pe.matmul(ps[3][:, cols], state[:, c, :], q_dec[:, cols], start=False, stop=True)
                        i.then_inc(o_done, 1)

                pipeline(pe, step)

            @block.scalar
            def _(act):
                def high(m, src, used, head, loaded, count, done):
                    act.wait_ge(loaded, count)
                    wait_for(act, used, head)
                    act.activation(parts[m][0][:, :, :], src[:, :, :], ACT.Copy).then_inc(done, 1)

                def step(i_, b, a0, a1, a2):
                    n = 2 * i_ + b
                    if a1:
                        act.wait_ge(v_projected, n)
                        if a2:
                            wait_for(act, o_done, n - 2)
                            wait_for(act, v_dec_done, n - 2)
                        act.activation(v_rows[1 - b][:, :, :], tiled[0], ACT.Copy).then_inc(v_copied, 1)
                    if a0:
                        high("q", wq[b], q_projected, n, qk_loaded[b], 96 * loads(i_, b, 0), q_high)
                        high("k", wk[b], k_projected, n, qk_loaded[b], 96 * loads(i_, b, 0), k_high)
                    if a2:
                        act.wait_ge(g_projected, n - 1)
                        wait_for(act, gated, n - 2)
                        act.activation(gate[:, :], ps[3][:, :], ACT.Silu).then_inc(g_acted, 1)
                    if a1:
                        act.wait_ge(shift_ready, n)
                        if a2:
                            act.wait_ge(k_turned, n - 1)
                            act.wait_ge(k_rows_done, n - 1)
                        for c in range(NT):
                            i = act.activation(normed[1][:, c, :], tiled[2][:, c, :], ACT.Identity,
                                               scale=rstd[:, 1, c:c + 1], bias=k_shift[:, c:c + 1])
                        i.then_inc(k_normed, 1)
                    if a0:
                        act.wait_ge(q_projected, n + 1)
                        act.activation(conv[0][:, :], ps[0][:, :], ACT.Identity, scale=taps[b][:, 0, TAPS - 1:TAPS],
                                       bias=taps[b][:, 0, TAPS:TAPS + 1]).then_inc(q_tapped, 1)
                    if a1:
                        act.wait_ge(q_turned, n)
                        if a2:
                            act.wait_ge(q_dec_done, n - 1)
                            act.wait_ge(scored, n - 1)
                        act.activation(q_T[:, :], ps[3][:, :], ACT.Identity, scale=norm_col[:, 0:1],
                                       bias=norm_col[:, 1:2]).then_inc(q_T_done, 1)
                        act.wait_ge(k_turned, n)
                        act.activation(k_T[:, :], ps[1][:, :], ACT.Identity, scale=norm_col[:, 2:3],
                                       bias=norm_col[:, 3:4]).then_inc(k_T_done, 1)
                        high("gate", wg[1 - b], g_projected, n - 1, g_loaded[1 - b], 16 * loads(i_, b, 1), g_high)
                    if a1:
                        act.wait_ge(arg_ready, n)
                        if a2:
                            act.wait_ge(probs_done, n - 1)
                            act.wait_ge(v_dec_done, n - 1)
                        for c in range(NT):
                            i = act.activation(mix[:, c, :], arg[:, c, :], ACT.Exp, bias=hcol[1 - b][:, 1, c:c + 1])
                        i.then_inc(mix_exped, 1)
                        if a2:
                            act.wait_ge(states_done, n - 1)
                            act.wait_ge(q_dec_done, n - 1)
                        act.activation(e_dec[:, :], decay[1 - b][:, :], ACT.Exp).then_inc(e_dec_done, 1)
                    if a0:
                        act.wait_ge(q_conved, n + 1)
                        act.activation(conv[0][:, :], conv[0][:, :], ACT.Silu).then_inc(q_acted, 1)
                        act.wait_ge(k_conved, n + 1)
                        act.activation(conv[1][:, :], conv[1][:, :], ACT.Silu).then_inc(k_acted, 1)

                pipeline(act, step)

            @block.vector
            def _(dve):
                def convolve(n, b, m, pair, tapped, done):
                    if m == 0:
                        dve.wait_ge(tapped, n + 1)
                    else:
                        dve.wait_ge(k_projected, n + 1)
                        if not (isinstance(n, int) and n < 1):
                            dve.wait_ge(k_rowed, n)
                        dve.tensor_scalar(conv[m][:, :], ps[pair][:, :], taps[b][:, m, TAPS - 1:TAPS],
                                          taps[b][:, m, TAPS:TAPS + 1], ALU.mult, ALU.add)
                        dve.drain()
                    for j in range(TAPS - 1):
                        back = TAPS - 1 - j
                        i = dve.scalar_tensor_tensor(conv[m][:, back:T], ps[pair][:, 0:T - back], taps[b][:, m, j:j + 1],
                                                     conv[m][:, back:T], ALU.mult, ALU.add)
                        if j < TAPS - 2:
                            dve.drain()
                    i.then_inc(done, 1)

                def step(i_, b, a0, a1, a2):
                    n = 2 * i_ + b
                    if a1:
                        m = n - 1
                        if a2:
                            dve.wait_ge(mix_exped, n - 1)
                        src = cols[:, :, :, bass.ds(m, 1)].rearrange("p a c o -> p a (c o)")
                        dve.tensor_copy(hcol[1 - b][:, :, :], src).then_inc(hcol_ready, 1)
                        for m, (pair, rowed) in enumerate(((1, q_rowed), (2, k_rowed))):
                            dve.wait_ge(rowed, n)
                            for c in range(NT):
                                dve.bn_stats(stats[:, m, c, :], tiled[pair][:, c, :])
                        dve.drain()
                        for m in range(2):
                            for c in range(NT):
                                dve.bn_aggr(mean_var[:, m, c, :], stats[:, m, c, :])
                        dve.drain()
                        dve.tensor_scalar(var_eps[:, :, :], mean_var[:, :, :, 1], EPS, None, ALU.add).then_inc(var_ready, 1)
                    if a2:
                        dve.wait_ge(scored, n - 1)
                        dve.wait_ge(masked, n - 1)
                        wait_for(dve, o_done, n - 2)
                        dve.tensor_tensor(probs[:, :, :], tiled[0], mix[:, :, :], ALU.mult).then_inc(probs_done, 1)
                        dve.wait_ge(kv_done, n - 1)
                        dve.wait_ge(e_dec_done, n - 1)
                        dve.tensor_copy(state[:, 1, :], tiled[3][:, 0, :])
                        for c in range(1, NT - 1):
                            dve.drain()
                            i = dve.scalar_tensor_tensor(state[:, c + 1, :], state[:, c, :],
                                                         e_dec[:, (c + 1) * P - 1:(c + 1) * P], tiled[3][:, c, :],
                                                         ALU.mult, ALU.add)
                        i.then_inc(states_done, 1)
                    if a1:
                        dve.wait_ge(rstd_ready, n)
                        dve.scalar_tensor_tensor(k_shift[:, :], mean_var[:, 1, :, 0], -1.0, rstd[:, 1, :], ALU.mult,
                                                 ALU.mult).then_inc(shift_ready, 1)
                        if a2:
                            dve.wait_ge(q_turned, n - 1)
                        for c in range(NT):
                            i = dve.tensor_scalar(normed[0][:, c, :], tiled[1][:, c, :], mean_var[:, 0, c, 0:1],
                                                  rstd[:, 0, c:c + 1], ALU.subtract, ALU.mult)
                        i.then_inc(q_normed, 1)
                    if a0:
                        convolve(n, b, 0, 0, q_tapped, q_conved)
                        convolve(n, b, 1, 2, None, k_conved)
                    if a2:
                        dve.wait_ge(o_done, n - 1)
                        dve.wait_ge(g_acted, n - 1)
                        out = gated_out[:, bass.ds(n - 2, 1), :].rearrange("p o t -> p (o t)")
                        dve.tensor_tensor(out, gate[:, :], ps[3][:, :], ALU.mult).then_inc(gated, 1)

                pipeline(dve, step)

            @block.gpsimd
            def _(pool):
                def low(m, src, high, head, done):
                    pool.wait_ge(high, head + 1)
                    pool.tensor_tensor(parts[m][1][:, :, :], src[:, :, :], parts[m][0][:, :, :].bitcast(F32), ALU.subtract)\
                        .then_inc(done, 1)

                def step(i_, b, a0, a1, a2):
                    n = 2 * i_ + b
                    if a0:
                        low("q", wq[b], q_high, n, q_split)
                        low("k", wk[b], k_high, n, k_split)
                    if a1:
                        pool.wait_ge(hcol_ready, n)
                        pool.wait_ge(d_loaded[1 - b], 16 * loads(i_, b, 1))
                        if a2:
                            pool.wait_ge(mix_exped, n - 1)
                        pool.wait_ge(var_ready, n)
                        if a2:
                            pool.wait_ge(k_normed, n - 1)
                        pool.tensor_tensor(rstd[:, :, :].rearrange("p a b -> p (a b)"),
                                           var_eps[:, :, :].rearrange("p a b -> p (a b)"), neg_half[:, 0:2 * NT],
                                           ALU.pow).then_inc(rstd_ready, 1)
                        for c in range(NT):
                            i = pool.tensor_scalar(arg[:, c, :], decay[1 - b][:, c * P:(c + 1) * P],
                                                   hcol[1 - b][:, 0, c:c + 1], 0.0, ALU.subtract, ALU.min)
                        i.then_inc(arg_ready, 1)
                        pool.wait_ge(k_normed, n)
                        if a2:
                            pool.wait_ge(kv_done, n - 1)
                        rows = [norm_row[:, j, :].rearrange("p (o d) -> p o d", o=1).to_broadcast((P, NT, HD))
                                for j in range(2)]
                        pool.tensor_tensor(k_rows[:, :, :], normed[1][:, :, :], rows[0], ALU.mult)
                        low("gate", wg[1 - b], g_high, n - 1, g_split)
                        pool.drain()
                        pool.wait_ge(mix_exped, n)
                        pool.tensor_tensor(k_rows[:, :, :], k_rows[:, :, :], rows[1], ALU.add).then_inc(k_rows_done, 1)
                        pool.affine_select(out=mix[:, :, :], in_=mix[:, :, :], compare_op=ALU.is_ge, fill=0.0, base=0,
                                           pattern=[[0, NT], [1, P]], channel_multiplier=-1).then_inc(masked, 1)
                        pool.drain()
                        pool.wait_ge(v_copied, n)
                        last = mix[:, :, P - 1:P].to_broadcast((P, NT, HD))
                        pool.tensor_tensor(v_dec[:, :, :], v_rows[1 - b][:, :, :], last, ALU.mult).then_inc(v_dec_done, 1)
                        pool.wait_ge(q_T_done, n)
                        pool.wait_ge(e_dec_done, n)
                        if a2:
                            pool.wait_ge(o_done, n - 1)
                        pool.tensor_tensor(q_dec[:, :], q_T[:, :], e_dec[:, :], ALU.mult).then_inc(q_dec_done, 1)

                pipeline(pool, step)


NX = 16
FX = 176
TOP = 4
FS = 2 * FX
GX = 8
GT = GX * FX // P
NG = NX // GX
ST = -(-FS // P)
SLOTS = 3
RSLOTS = 3


class TopRouter:

    def __init__(self, s, ident, gate_weight, earlier, x_parts, w_dram, scratch):
        self.ident, self.gate_weight, self.earlier, self.x_parts, self.w_dram = ident, gate_weight, earlier, x_parts, w_dram
        self.greater, self.same, self.w_rows = scratch
        self.gw = s.sb("gw", [NX, D])
        self.gw_parts = [s.sb(f"gw_part{q}", [P, DK, NX], F32R) for q in range(2)]
        self.order = s.sb("order", [P, NX, NX])
        self.w = s.sb("w", [P, NT, NX])
        self.mask = s.sb("mask", [P, NT, NX])
        self.total = s.sb("total", [P, NT])
        self.ps_t = s.ps("gw_turned", [P, DK, NX])
        self.logits = s.ps("logits", [P, NT, NX])
        (self.loaded, self.gw_turned, self.gw_copied, self.rows_scored, self.rows_copied, self.scored, self.shifted,
         self.exped, self.w_ready, self.turned, self.rows_ready, self.stored) = (s.sem(name) for name in (
             "r_loaded", "gw_turned", "gw_copied", "rows_scored", "rows_copied", "scored", "shifted",
             "exped", "w_ready", "turned", "rows_ready", "stored"))

    def use(self, banks):
        self.rows_ps = [b[0:NX, :] for b in banks]

    def sp_start(self, sp):
        sp.dma_start(self.gw[:, :], self.gate_weight).then_inc(self.loaded, 16)
        sp.dma_start(self.order[:, :, :], self.earlier.rearrange("(o a) b -> o a b", o=1).to_broadcast((P, NX, NX)))\
            .then_inc(self.loaded, 16)

    def sp_end(self, sp):
        sp.wait_ge(self.rows_ready, 1)
        sp.dma_start(self.w_dram, self.w_rows[:, :]).then_inc(self.stored, 16)
        sp.wait_ge(self.stored, 16)

    def pe_start(self, pe):
        pe.wait_ge(self.loaded, 32)
        for k in range(DK):
            i = pe.transpose(self.ps_t[:, k, :], self.gw[:, k * P:(k + 1) * P], self.ident[0:NX, 0:NX])
        i.then_inc(self.gw_turned, 1)
        pe.wait_ge(self.gw_copied, 1)
        score_tokens(pe, self.x_parts, self.gw_parts, self.w_rows, self.ident, self.rows_ps, self.logits,
                     self.rows_scored, self.rows_copied).then_inc(self.scored, 1)

    def pe_end(self, pe):
        pe.wait_ge(self.w_ready, 1)
        for c in range(NT):
            i = pe.transpose(self.rows_ps[c // 4][:, c % 4 * P:(c % 4 + 1) * P], self.w[:, c, :], self.ident[:, :])
        i.then_inc(self.turned, 1)

    def act_start(self, act):
        copy_rows(act, self.w_rows, self.rows_ps, self.rows_scored, self.rows_copied)
        act.wait_ge(self.shifted, 1)
        act.activation(self.w[:, :, :], self.w[:, :, :], ACT.Exp).then_inc(self.exped, 1)

    def act_end(self, act):
        act.wait_ge(self.turned, 1)
        for h in range(2):
            i = act.activation(self.w_rows[:, h * HALF:(h + 1) * HALF], self.rows_ps[h], ACT.Copy)
        i.then_inc(self.rows_ready, 1)

    def dve(self, dve):
        w, total = self.w[:, :, :], self.total[:, :]
        dve.wait_ge(self.loaded, 32)
        dve.wait_ge(self.gw_turned, 1)
        split_small(dve, [q[:, :, :] for q in self.gw_parts], self.ps_t[:, :, :]).then_inc(self.gw_copied, 1)
        dve.wait_ge(self.scored, 1)
        dve.tensor_reduce(total, self.logits[:, :, :], axis=AX, op=ALU.max)
        dve.drain()
        dve.tensor_tensor(w, self.logits[:, :, :], col(total, NX), ALU.subtract).then_inc(self.shifted, 1)
        dve.wait_ge(self.exped, 1)
        dve.tensor_reduce(total, w, axis=AX, op=ALU.add)
        dve.drain()
        dve.reciprocal(total, total)
        dve.drain()
        dve.tensor_tensor(w, w, col(total, NX), ALU.mult)
        dve.drain()
        rank_mask(dve, w, self.mask[:, :, :], self.greater, self.same, self.order[:, :, :], NX, TOP)
        dve.tensor_tensor(w, w, self.mask[:, :, :], ALU.mult).then_inc(self.w_ready, 1)


def glu_block(nc, tag, ident, x_parts, mids, down_T, base, groups, tiles, loads, routing, router=None):
    N = len(tiles)
    B = 1 if router else 2
    with Scope(nc, tag) as s:
        natural = [s.sb(f"natural{b}", [P, 2, D]) for b in range(SLOTS)]
        down = [s.sb(f"down{b}", [P, DK, P]) for b in range(SLOTS)]
        w_T = [[s.sb(f"w_T{b}{q}", [P, 2, DK, P], F32R) for q in range(2)] for b in range(2)]
        weight = [s.sb(f"weight{b}", [P, T]) for b in range(RSLOTS)] if routing else None
        gated = [s.sb(f"gated{b}", [P, HALF]) for b in range(2)]
        if router:
            raw_w, raw_d = s.sb("raw_w", [P, 2, DK, P]), s.sb("raw_d", [P, D])
            ups = [s.sb(f"up_copy{b}", [P, HALF]) for b in range(2)]
            up_copied = s.sem("up_copied")
        ps_w = [s.ps(f"turned_w{b}", [P, 2, DK, P]) for b in range(B)]
        ps_d = [s.ps(f"turned_d{b}", [P, HALF]) for b in range(B)]
        ps_g = [s.ps(f"gate{b}", [P, HALF]) for b in range(2)]
        ps_u = [s.ps(f"up{b}", [P, HALF]) for b in range(2)]
        loaded = [s.sem(f"loaded{b}") for b in range(SLOTS)]
        r_loaded = [s.sem(f"r_loaded{b}") for b in range(RSLOTS)]
        w_high, d_high = s.sem("w_high"), s.sem("d_high")
        w_turned, w_copied = s.sem("w_turned"), s.sem("w_copied")
        d_turned, d_copied = s.sem("d_turned"), s.sem("d_copied")
        if router:
            router = TopRouter(s, ident, *router)
            router.use([p[:, :] for p in ps_g])
        gate_done, up_done = s.sem("gate_done"), s.sem("up_done")
        gate_taken, up_taken, weighted = s.sem("gate_taken"), s.sem("up_taken"), s.sem("weighted")

        def dmas(source, slots):
            parts = [list(source(0, n)) for n in range(N)]
            per_group = [16 * sum(len(parts[n]) for n in range(N) if n % slots == b) for b in range(slots)]
            upto = [16 * sum(len(parts[m]) for m in range(n + 1) if m % slots == n % slots) for n in range(N)]
            return per_group, upto

        def last_user(n, slots):
            return slots if n >= slots else n + N - max(m for m in range(N) if m % slots == n % slots)

        w_group, w_upto = dmas(loads, SLOTS)
        if routing:
            r_group, r_upto = dmas(routing, RSLOTS)

        def over_groups(eng, body):
            body(0, True)
            if groups > 1:
                with eng.Fori(1, groups) as g:
                    body(g, False)

        with nc.Block() as block:

            @block.sync
            def _(sp):
                def weights(g, n, first):
                    at, back = g * N + n, last_user(n, SLOTS)
                    if not first or n >= SLOTS:
                        sp.wait_ge(w_turned, at - back + 1)
                        sp.wait_ge(d_turned, at - back + 1)
                    for what, rows, src in loads(g, n):
                        dst = {"gate": natural[n % SLOTS][rows, 0, :], "up": natural[n % SLOTS][rows, 1, :],
                               "down": down[n % SLOTS][:, :, rows]}[what]
                        sp.dma_start(dst, src).then_inc(loaded[n % SLOTS], 16)

                def group(g, first):
                    weights(g, 0, first)
                    for n in range(N):
                        if n + 1 < N:
                            weights(g, n + 1, first)
                        if routing:
                            if not first or n >= RSLOTS:
                                sp.wait_ge(weighted, 2 * (g * N + n - last_user(n, RSLOTS) + 1))
                            for _, rows, src in routing(g, n):
                                sp.dma_start(weight[n % RSLOTS][rows, :], src).then_inc(r_loaded[n % RSLOTS], 16)

                if router:
                    router.sp_start(sp)
                over_groups(sp, group)
                if router:
                    router.sp_end(sp)

            @block.tensor
            def _(pe):
                def turn(g, n, first):
                    at = g * N + n
                    rows = tiles[n]
                    pe.wait_ge(loaded[n % SLOTS], w_group[n % SLOTS] * g + w_upto[n])
                    if not first or n >= B:
                        pe.wait_ge(w_copied, at - last_user(n, B) + 1)
                    for m in range(2):
                        for k in range(DK):
                            i = pe.transpose(ps_w[n % B][:, m, k, 0:rows], natural[n % SLOTS][0:rows, m, k * P:(k + 1) * P],
                                             ident[0:rows, 0:rows])
                    i.then_inc(w_turned, 1)
                    if not first or n >= B:
                        pe.wait_ge(d_copied, at - last_user(n, B) + 1)
                    for k in range(DK):
                        i = pe.transpose(ps_d[n % B][0:rows, k * P:(k + 1) * P], down[n % SLOTS][:, k, 0:rows], ident[:, :])
                    i.then_inc(d_turned, 1)

                def group(g, first):
                    turn(g, 0, first)
                    for n in range(N):
                        at = g * N + n
                        if n + 1 < N:
                            turn(g, n + 1, first)
                        pe.wait_ge(w_copied, at + 1)
                        for half in range(2):
                            cols = slice(half * HALF, (half + 1) * HALF)
                            for m, (ps, taken, done) in enumerate(((ps_g, gate_taken, gate_done), (ps_u, up_taken, up_done))):
                                if not first or n:
                                    pe.wait_ge(taken, 2 * at + half - 1)
                                for k in range(DK):
                                    i = matmul3(pe, ps[half][0:tiles[n], :], [w[:, m, k, 0:tiles[n]] for w in w_T[n % 2]],
                                                [q[:, k, cols] for q in x_parts], k == 0, k == DK - 1)
                                i.then_inc(done, 1)

                if router:
                    router.pe_start(pe)
                over_groups(pe, group)
                if router:
                    pe.wait_ge(gate_taken, 2 * N * groups)
                    router.pe_end(pe)

            @block.scalar
            def _(act):
                def copy(g, n, first):
                    at, rows = g * N + n, tiles[n]
                    act.wait_ge(w_turned, at + 1)
                    if not first or n >= 2:
                        act.wait_ge(up_done, 2 * (at - last_user(n, 2) + 1))
                    if router:
                        if n:
                            act.wait_ge(w_copied, at)
                        act.activation(raw_w[:, :, :, 0:rows], ps_w[0][:, :, :, 0:rows], ACT.Copy).then_inc(w_high, 1)
                        act.wait_ge(d_turned, at + 1)
                        if n:
                            act.wait_ge(d_copied, at)
                        act.activation(raw_d[0:rows, :], ps_d[0][0:rows, 0:D], ACT.Copy).then_inc(d_high, 1)
                        return
                    act.activation(w_T[n % 2][0][:, :, :, 0:rows], ps_w[n % B][:, :, :, 0:rows], ACT.Copy).then_inc(w_high, 1)
                    act.wait_ge(d_turned, at + 1)
                    act.activation(down_T[0][0:rows, bass.ds(base + at, 1), :].rearrange("p o d -> p (o d)"),
                                   ps_d[n % B][0:rows, 0:D], ACT.Copy).then_inc(d_high, 1)

                def group(g, first):
                    copy(g, 0, first)
                    for n in range(N):
                        at, rows = g * N + n, tiles[n]
                        if n + 1 < N:
                            copy(g, n + 1, first)
                        for half in range(2):
                            if not first or n:
                                act.wait_ge(up_taken, 2 * at + half - 1)
                            act.wait_ge(gate_done, 2 * at + half + 1)
                            act.activation(gated[half][0:rows, :], ps_g[half][0:rows, :], ACT.Silu).then_inc(gate_taken, 1)
                            if router:
                                act.wait_ge(up_done, 2 * at + half + 1)
                                act.activation(ups[half][0:rows, :], ps_u[half][0:rows, :], ACT.Copy).then_inc(up_copied, 1)

                if router:
                    router.act_start(act)
                over_groups(act, group)
                if router:
                    router.act_end(act)

            @block.vector
            def _(dve):
                if router:
                    router.dve(dve)
                    return

                def low(g, n):
                    at, rows = g * N + n, tiles[n]
                    w = w_T[n % 2]
                    dve.wait_ge(w_high, at + 1)
                    dve.tensor_tensor(w[1][:, :, :, 0:rows], ps_w[n % B][:, :, :, 0:rows], w[0][:, :, :, 0:rows].bitcast(F32),
                                      ALU.subtract).then_inc(w_copied, 1)
                    dve.wait_ge(d_high, at + 1)
                    high, out = (q[0:rows, bass.ds(base + at, 1), :].rearrange("p o d -> p (o d)") for q in down_T)
                    dve.tensor_tensor(out, ps_d[n % B][0:rows, 0:D], high.bitcast(F32), ALU.subtract).then_inc(d_copied, 1)

                def group(g, first):
                    low(g, 0)
                    for n in range(N):
                        at, rows = g * N + n, tiles[n]
                        if n + 1 < N:
                            low(g, n + 1)
                        for half in range(2):
                            cols = slice(half * HALF, (half + 1) * HALF)
                            out = mids[0:rows, bass.ds(base + at, 1), cols].rearrange("p o t -> p (o t)")
                            dve.wait_ge(gate_taken, 2 * at + half + 1)
                            dve.wait_ge(up_done, 2 * at + half + 1)
                            dve.tensor_tensor(out, gated[half][0:rows, :], ps_u[half][0:rows, :], ALU.mult)\
                                .then_inc(up_taken, 1)

                over_groups(dve, group)

            @block.gpsimd
            def _(pool):
                def split(n):
                    rows = tiles[n]
                    for raw, high, low, ready, done in (
                            (raw_w[:, :, :, 0:rows], w_T[n % 2][0][:, :, :, 0:rows], w_T[n % 2][1][:, :, :, 0:rows],
                             w_high, w_copied),
                            (raw_d[0:rows, :], down_T[0][0:rows, base + n, :], down_T[1][0:rows, base + n, :],
                             d_high, d_copied)):
                        pool.wait_ge(ready, n + 1)
                        pool.tensor_scalar(high, raw, 1.0, 0.0, ALU.mult, ALU.add)
                        pool.drain()
                        pool.tensor_tensor(low, raw, high.bitcast(F32), ALU.subtract).then_inc(done, 1)

                if router:
                    split(0)
                    for n in range(N):
                        if n + 1 < N:
                            split(n + 1)
                        for half in range(2):
                            cols = slice(half * HALF, (half + 1) * HALF)
                            pool.wait_ge(up_copied, 2 * n + half + 1)
                            pool.tensor_tensor(mids[0:tiles[n], base + n, cols], gated[half][0:tiles[n], :],
                                               ups[half][0:tiles[n], :], ALU.mult).then_inc(up_taken, 1)
                if not routing:
                    return

                def group(g, first):
                    for n in range(N):
                        at, rows = g * N + n, tiles[n]
                        pool.wait_ge(r_loaded[n % RSLOTS], r_group[n % RSLOTS] * g + r_upto[n])
                        for half in range(2):
                            cols = slice(half * HALF, (half + 1) * HALF)
                            pool.wait_ge(up_taken, 2 * at + half + 1)
                            out = mids[0:rows, bass.ds(base + at, 1), cols].rearrange("p o t -> p (o t)")
                            pool.tensor_tensor(out, out, weight[n % RSLOTS][0:rows, cols], ALU.mult)\
                                .then_inc(weighted, 1)

                over_groups(pool, group)


def routed_tiles(gate_up, down_w, w_dram):
    gu = gate_up.rearrange("(g e) (m f) d -> g e m f d", e=GX, m=2)
    dw = down_w.rearrange("(g e) (k p) f -> g e p k f", e=GX, p=P)
    rw = w_dram.rearrange("(g e) t -> g e t", e=GX)

    def pieces(n):
        at = n * P
        while at < (n + 1) * P:
            e, r = divmod(at, FX)
            k = min(FX - r, (n + 1) * P - at)
            yield e, r, k, slice(at - n * P, at - n * P + k)
            at += k

    def loads(g, n):
        for e, r, k, rows in pieces(n):
            for m, what in enumerate(("gate", "up")):
                yield what, rows, gu[bass.ds(g, 1), e, m, r:r + k, :].rearrange("o f d -> (o f) d")
            yield "down", rows, dw[bass.ds(g, 1), e, :, :, r:r + k].rearrange("o p k f -> (o p) k f")

    def routing(g, n):
        for e, r, k, rows in pieces(n):
            yield "weight", rows, rw[bass.ds(g, 1), e, :].to_broadcast((k, T))

    return loads, routing


def shared_tiles(gate_up, down_w):
    gu = gate_up.rearrange("(m f) d -> m f d", m=2)
    dw = down_w.rearrange("(k p) f -> p k f", p=P)

    def loads(g, n):
        k = min(P, FS - n * P)
        for m, what in enumerate(("gate", "up")):
            yield what, slice(0, k), gu[m, n * P:n * P + k, :]
        yield "down", slice(0, k), dw[:, :, n * P:n * P + k]

    return loads


def network(nc, a, rope_table, earlier_table, out):
    Scope.used.clear()
    gold_w = nc.dram_tensor("gold_weights", [NE, T], F32, kind="Internal").ap()
    decay_sums = nc.dram_tensor("decay_sums", [LH, T], F32, kind="Internal").ap()
    top_w = nc.dram_tensor("top_weights", [NX, T], F32, kind="Internal").ap()

    def row(ap):
        return ap.rearrange("(o n) -> o n", o=1).to_broadcast((P, ap.shape[0]))

    def column(ap):
        return ap.rearrange("(n o) -> n o", o=1)

    def by_tiles(ap):
        return ap.rearrange("(k p) n -> p k n", p=P)

    with Scope(nc, "net") as net:
        ident = net.sb("ident", [P, P])
        neg_half = net.sb("neg_half", [P, 2 * NT])
        x = net.sb("x", [P, NT, D])
        x_parts = [net.sb(f"x_part{m}", [P, DK, T], F32R) for m in range(2)]
        with Scope(nc, "early") as early:
            xT = early.sb("xT", [P, DK, T])
            identb = early.sb("identb", [P, P], BF16)
            norm_row = early.sb("norm_row", [P, 2, HD])
            norm_col = early.sb("norm_col", [P, 4])
            inner_wb = early.sb("inner_wb", [P, 2, DK])
            rope = early.sb("rope", [P, NT, 2, ROT // 2])
            load_constants(nc, [
                (x[:, :, :], by_tiles(a["L0_attn_X"][0])),
                (inner_wb[:, 0, :], a["L0_attn_ln_w"].rearrange("(k p) -> p k", p=P)),
                (inner_wb[:, 1, :], a["L0_attn_ln_b"].rearrange("(k p) -> p k", p=P)),
                (rope[:, :, :, :], rope_table),
                (norm_row[:, 0, :], row(a["L1_attn_kn_w"])), (norm_row[:, 1, :], row(a["L1_attn_kn_b"])),
                (norm_col[:, 0:1], column(a["L1_attn_qn_w"])), (norm_col[:, 1:2], column(a["L1_attn_qn_b"])),
                (norm_col[:, 2:3], column(a["L1_attn_kn_w"])), (norm_col[:, 3:4], column(a["L1_attn_kn_b"])),
            ], ident, identb, neg_half)

            with Scope(nc, "s0") as s:
                xn = s.sb("xn", [P, NT, D])
                w_out, w_out_loaded = s.sb("w_out", [P, DK, D]), s.sem("w_out_loaded")
                context = s.sb("context", [P, NT, D])
                with Scope(nc, "s0a") as t:
                    w_in, w_in_loaded = t.sb("w_in", [P, DK, 3 * D]), t.sem("w_in_loaded")
                    norm_block(nc, "norm0", ident, neg_half, x, normed=xn, normed_T=xT, inner=context, inner_wb=inner_wb,
                               prefetch=lambda sp: sp.dma_start(w_in[:, :, :], by_tiles(a["L0_attn_W_in"]))
                               .then_inc(w_in_loaded, 16))
                    qk = t.sb("qk", [P, NT, 2 * D])
                    v = t.sb("v", [P, NT, NH, VW])
                    k_stack = t.sb("k_stack", [P, NH, T], BF16)
                    qkv_block(nc, w_in_loaded, xT, w_in, rope, qk, v, k_stack,
                              lambda sp: sp.dma_start(w_out[:, :, :], by_tiles(a["L0_attn_W_out"])).then_inc(w_out_loaded, 16))
                    attention_block(nc, ident, identb, qk, v, k_stack, context)
                turn_block(nc, "turn0", ident, context, xT)
                w_down = s.sb("w_down", [P, NE * FK, D])
                rings = [[s.sb(f"ring{m}{b}", [P, DK, FE]) for b in range(2)] for m in range(2)]
                Wg, Wu, Wd = (a[f"L0_ffn_W{m}"] for m in "gud")
                low_rank = LowRank(s, ident, [(a[f"L0_ffn_{m}a"], a[f"L0_ffn_{m}b"]) for m in "GUD"], rings, w_down,
                                   Wg, Wu, Wd)
                down_norm_block(nc, "out0", ident, neg_half, x, [xT[:, k, :] for k in range(DK)], w_down=w_out, add=xn,
                                loaded=w_out_loaded, prefetch=low_rank.sp, parts=x_parts)

                golden_router_block(nc, ident, a["L0_ffn_Wr"], a["L0_ffn_temperature"], earlier_table, x_parts, gold_w,
                                    low_rank)
                mids = s.sb("mids", [P, NE * FK, T])
                experts_block(nc, rings, x_parts, gold_w, Wg, Wu, mids)
                down_norm_block(nc, "out1", ident, neg_half, x, [mids[:, k, :] for k in range(NE * FK)], w_down=w_down,
                                parts=x_parts, xT=xT, y=context, xn=xn)

            clear_semaphores(nc)

            with Scope(nc, "s2") as s:
                gated = s.sb("gated", [P, LH, T])
                w_o, w_o_loaded = s.sb("w_o", [P, LH, D]), s.sem("w_o_loaded")
                with Scope(nc, "s2a") as t:
                    cols = t.sb("cols", [P, 2, NT, LH])
                    decay_block(nc, ident, a["L1_attn_Wb"], a["L1_attn_bb"], x_parts, decay_sums, cols,
                                lambda sp: sp.dma_start(w_o[:, :, :], by_tiles(a["L1_attn_Wo"])).then_inc(w_o_loaded, 16))
                    w = {m: a[f"L1_attn_W{n}"] for m, n in (("q", "q"), ("k", "k"), ("v", "v"), ("gate", "g"))}
                    w.update({f"{m}_taps": (a[f"L1_attn_{m}conv_w"], a[f"L1_attn_{m}conv_b"]) for m in "qk"})
                    linear_attention_block(nc, ident, neg_half, w, xT, x_parts, decay_sums, cols, norm_row, norm_col, gated)
                down_norm_block(nc, "out2", ident, neg_half, x, [gated[:, k, :] for k in range(LH)], w_down=w_o,
                                loaded=w_o_loaded, parts=x_parts)

        with Scope(nc, "s3") as s:
            n = NG * GT + ST
            mids = s.sb("mids", [P, n, T])
            down_T = [s.sb(f"down_T{m}", [P, n, D], F32R) for m in range(2)]
            rows = [P] * (n - 1) + [FS - (ST - 1) * P]
            scratch = [mids[:, b:b + 2, :].rearrange("p a (c i j) -> p (a c) i j", i=NX, j=NX) for b in (0, 2)]
            scratch.append(mids[0:NX, 4, :])
            loads = shared_tiles(a["L1_ffn_shared_gate_up"], a["L1_ffn_shared_down"])
            glu_block(nc, "shared", ident, x_parts, mids, down_T, NG * GT, 1, rows[NG * GT:], loads, None,
                      (a["L1_ffn_gate_weight"], earlier_table, x_parts, top_w, scratch))
            loads, routing = routed_tiles(a["L1_ffn_gate_up_weights"], a["L1_ffn_down_weights"], top_w)
            glu_block(nc, "routed", ident, x_parts, mids, down_T, 0, NG, rows[0:GT], loads, routing)
            down_norm_block(nc, "out3", ident, neg_half, x, [mids[0:rows[k], k, :] for k in range(n)], w_parts=down_T,
                            store=out[0])


_INS = [
    "L0_attn_X", "L0_attn_ln_w", "L0_attn_ln_b", "L0_attn_W_in", "L0_attn_W_out",
    "L0_ffn_Wg", "L0_ffn_Wu", "L0_ffn_Wd", "L0_ffn_Ga", "L0_ffn_Gb", "L0_ffn_Ua", "L0_ffn_Ub", "L0_ffn_Da",
    "L0_ffn_Db", "L0_ffn_Wr", "L0_ffn_temperature",
    "L1_attn_Wq", "L1_attn_Wk", "L1_attn_Wv", "L1_attn_Wb", "L1_attn_bb", "L1_attn_Wg", "L1_attn_Wo",
    "L1_attn_qconv_w", "L1_attn_qconv_b", "L1_attn_kconv_w", "L1_attn_kconv_b",
    "L1_attn_qn_w", "L1_attn_qn_b", "L1_attn_kn_w", "L1_attn_kn_b",
    "L1_ffn_gate_weight", "L1_ffn_gate_up_weights", "L1_ffn_down_weights", "L1_ffn_shared_gate_up",
    "L1_ffn_shared_down",
]


def rope_constants():
    inverse = (1.0 / np.float32(10000.0) ** (np.arange(0, ROT, 2, dtype=np.float32) / ROT)).astype(np.float32)
    angle = np.arange(T, dtype=np.float32)[:, None] * inverse[None, :]
    table = np.stack([np.cos(angle), np.sin(angle)], axis=1).astype(np.float32)
    return np.ascontiguousarray(table.reshape(NT, P, 2, ROT // 2).transpose(1, 0, 2, 3))


def kernel(**inputs):
    import concourse.bacc as bacc
    from concourse.bass_utils import run_bass_kernel_spmd

    nc = bacc.Bacc("TRN2", target_bir_lowering=False, num_devices=1)
    arrays = {f"in_{name}": np.ascontiguousarray(inputs[name]) for name in _INS}
    arrays["rope_table"] = rope_constants()
    arrays["earlier_table"] = np.tril(np.ones((NX, NX), np.float32), -1)
    aps = {name: nc.dram_tensor(name, v.shape, mybir.dt.from_np(v.dtype), kind="ExternalInput").ap()
           for name, v in arrays.items()}
    out = nc.dram_tensor("out_0", (1, T, D), F32, kind="ExternalOutput").ap()
    network(nc, {name: aps[f"in_{name}"] for name in _INS}, aps["rope_table"], aps["earlier_table"], out)
    r = run_bass_kernel_spmd(nc, [arrays], core_ids=[0])
    return r.results[0]["out_0"]
```
